# Optimizing a Trainium2 kernel written in Bass

```python
import numpy as np
import jax
import jax.numpy as jnp

def _softmax(x, axis=-1):
    return jax.nn.softmax(x, axis=axis)

def _gelu(x):
    return jax.nn.gelu(x, approximate=True)

def _silu(x):
    return jax.nn.silu(x)

def _sigmoid(x):
    return jax.nn.sigmoid(x)

def _layernorm(x, axis=-1, eps=1e-05):
    m = jnp.mean(x, axis=axis, keepdims=True)
    v = jnp.var(x, axis=axis, keepdims=True)
    return (x - m) / jnp.sqrt(v + eps)

def _scatter_add(tgt, idx, src, axis=0):
    return tgt.at[idx].add(src)

def _segment_sum(src, seg, n):
    return jax.ops.segment_sum(src, seg, n)
kernel_name = 'mk_perceiver_d2_seqx_r4_ad384a'

def setup_inputs(seed: int=0):
    np.random.seed(seed)
    _w = jnp.asarray

    def _rec_inputs():
        import jax
        import jax.numpy as jnp
        _rk = jax.random.key(seed)
        x = 7.22e-05 + 1 * jax.random.normal(jax.random.fold_in(_rk, 1), (128, 32, 256), jnp.float32)
        _lenS = 32 - jax.random.randint(jax.random.fold_in(_rk, 7), (128,), 0, max(1, 32 // 4) + 1, jnp.int32)
        _lenS2 = 257 - jax.random.randint(jax.random.fold_in(_rk, 8), (128,), 0, max(1, 257 // 4) + 1, jnp.int32)
        _ctx_1024P = jax.random.normal(jax.random.fold_in(_rk, 11), (128, 16, 256), jnp.float32)
        _ctx_1024c = jax.random.dirichlet(jax.random.fold_in(_rk, 511), 0.3 * jnp.ones((16,), jnp.float32), (128, 257))
        _ctx_1024t = jnp.einsum('bsk,bkd->bsd', _ctx_1024c, _ctx_1024P)
        _ctx_1024t = _ctx_1024t * jax.lax.rsqrt(jnp.mean(jnp.square(_ctx_1024t)) + 1e-12) * 0.953939
        ctx_1024 = -1.52775e-05 + 0.999936 * (_ctx_1024t + 0.3 * jax.random.normal(jax.random.fold_in(_rk, 611), (128, 257, 256), jnp.float32))
        return (x, ctx_1024)
    x, ctx_1024 = _rec_inputs()

    def _L0_xattn_setup():
        import jax, jax.numpy as jnp
        import numpy as np
        HIDDEN = 256
        key = jax.random.key(seed)
        ks = jax.random.split(key, 8)
        s = 1.0 / np.sqrt(HIDDEN)
        return {'query': jax.random.normal(ks[0], (8, 256, HIDDEN), dtype=jnp.float32), 'ref': jax.random.normal(ks[1], (8, 1024, HIDDEN), dtype=jnp.float32), 'Wq': jax.random.normal(ks[2], (HIDDEN, HIDDEN), dtype=jnp.float32) * s, 'bq': jax.random.normal(ks[3], (HIDDEN,), dtype=jnp.float32) * s, 'Wk': jax.random.normal(ks[4], (HIDDEN, HIDDEN), dtype=jnp.float32) * s, 'bk': jax.random.normal(ks[5], (HIDDEN,), dtype=jnp.float32) * s, 'Wv': jax.random.normal(ks[6], (HIDDEN, HIDDEN), dtype=jnp.float32) * s, 'bv': jax.random.normal(ks[7], (HIDDEN,), dtype=jnp.float32) * s}
    _L0_xattn_all = _L0_xattn_setup()
    _L0_xattn_in = {k: v for k, v in _L0_xattn_all.items() if k in ('Wq', 'bq', 'Wk', 'bk', 'Wv', 'bv')}
    del _L0_xattn_all

    def _L0_attn_setup():
        import jax, jax.numpy as jnp
        import numpy as np
        D_IN, HEAD_DIM = (256, 128)
        key = jax.random.key(seed)
        ks = jax.random.split(key, 9)
        s = 0.02
        return {'x': jax.random.normal(ks[0], (4, 1024, D_IN), dtype=jnp.float32), 'Wq': jax.random.normal(ks[1], (HEAD_DIM, D_IN), dtype=jnp.float32) * s, 'bq': jnp.zeros((HEAD_DIM,), dtype=jnp.float32), 'Wk': jax.random.normal(ks[2], (HEAD_DIM, D_IN), dtype=jnp.float32) * s, 'bk': jnp.zeros((HEAD_DIM,), dtype=jnp.float32), 'Wv': jax.random.normal(ks[3], (HEAD_DIM, D_IN), dtype=jnp.float32) * s, 'bv': jnp.zeros((HEAD_DIM,), dtype=jnp.float32), 'Wo': jax.random.normal(ks[4], (D_IN, HEAD_DIM), dtype=jnp.float32) * s, 'bo': jnp.zeros((D_IN,), dtype=jnp.float32)}
    _L0_attn_all = _L0_attn_setup()
    _L0_attn_in = {k: v for k, v in _L0_attn_all.items() if k in ('Wq', 'bq', 'Wk', 'bk', 'Wv', 'bv', 'Wo', 'bo')}
    del _L0_attn_all

    def _L0_ffn_setup():
        import jax, jax.numpy as jnp
        import numpy as np
        EMBED_DIM = 256
        HIDDEN = 4 * EMBED_DIM
        BATCH, SEQ = (4, 1024)
        EPS = 1e-05

        def _quant_weight(w):
            s = jnp.clip(jnp.mean(jnp.abs(w)), EPS, None)
            wq = jnp.clip(jnp.round(w / s), -1.0, 1.0) * s
            return w + jax.lax.stop_gradient(wq - w)

        def _quant_act(x):
            scale = 127.0 / jnp.clip(jnp.max(jnp.abs(x), axis=-1, keepdims=True), EPS, None)
            xq = jnp.clip(jnp.round(x * scale), -128.0, 127.0) / scale
            return x + jax.lax.stop_gradient(xq - x)

        def _bitlinear(x, w):
            return jnp.einsum('bsi,oi->bso', _quant_act(x), _quant_weight(w))
        key = jax.random.key(seed)
        k1, k2, k3 = jax.random.split(key, 3)
        x = jax.random.normal(k1, (BATCH, SEQ, EMBED_DIM), dtype=jnp.float32)
        w1 = jax.random.normal(k2, (HIDDEN, EMBED_DIM), dtype=jnp.float32) * (1.0 / np.sqrt(EMBED_DIM))
        w2 = jax.random.normal(k3, (EMBED_DIM, HIDDEN), dtype=jnp.float32) * (1.0 / np.sqrt(HIDDEN))
        return {'x': x, 'w1': w1, 'w2': w2}
    _L0_ffn_all = _L0_ffn_setup()
    _L0_ffn_in = {k: v for k, v in _L0_ffn_all.items() if k in ('w1', 'w2')}
    del _L0_ffn_all

    def _L1_xattn_setup():
        import jax, jax.numpy as jnp
        import numpy as np
        B, SQ, SKV, E, H = (4, 512, 512, 256, 16)
        D = E // H
        key = jax.random.key(seed)
        ks = jax.random.split(key, 8)
        s = 1.0 / np.sqrt(D)
        return {'query': jax.random.normal(ks[0], (B, SQ, E), jnp.float32), 'key_value': jax.random.normal(ks[1], (B, SKV, E), jnp.float32), 'wq': jax.random.normal(ks[2], (H, D, D), jnp.float32) * s, 'bq': jnp.zeros((H, D), jnp.float32), 'wk': jax.random.normal(ks[3], (H, D, D), jnp.float32) * s, 'bk': jnp.zeros((H, D), jnp.float32), 'wv': jax.random.normal(ks[4], (H, D, D), jnp.float32) * s, 'bv': jnp.zeros((H, D), jnp.float32), 'wo': jax.random.normal(ks[5], (E, E), jnp.float32) * (1.0 / np.sqrt(E)), 'bo': jnp.zeros((E,), jnp.float32)}
    _L1_xattn_all = _L1_xattn_setup()
    _L1_xattn_in = {k: v for k, v in _L1_xattn_all.items() if k in ('wq', 'bq', 'wk', 'bk', 'wv', 'bv', 'wo', 'bo')}
    del _L1_xattn_all

    def _L1_attn_setup():
        import jax, jax.numpy as jnp
        import numpy as np
        H = 256
        W_CTX = 2

        def _local_attention(x, Wq, bq, Wk, bk, Wv, bv):
            B, S, Hd = x.shape
            Q = x @ Wq + bq
            K = x @ Wk + bk
            V = x @ Wv + bv
            w = W_CTX
            win = 2 * w + 1
            idx = jnp.arange(S)[:, None] + jnp.arange(-w, w + 1)[None, :]
            valid = (idx >= 0) & (idx < S)
            idx_c = jnp.clip(idx, 0, S - 1)
            Kw = K[:, idx_c]
            Vw = V[:, idx_c]
            scores = jnp.einsum('bsh,bswh->bsw', Q, Kw) / jnp.sqrt(jnp.float32(Hd))
            scores = jnp.where(valid[None], scores, -jnp.inf)
            probs = jax.nn.softmax(scores, axis=-1)
            return jnp.einsum('bsw,bswh->bsh', probs, Vw)
        key = jax.random.key(seed)
        ks = jax.random.split(key, 7)
        B, S = (4, 512)
        sd = 1.0 / np.sqrt(H)
        inp = {'sequence_output': jax.random.normal(ks[0], (B, S, H), dtype=jnp.float32), 'Wq': jax.random.uniform(ks[1], (H, H), jnp.float32, -sd, sd), 'bq': jax.random.uniform(ks[2], (H,), jnp.float32, -sd, sd), 'Wk': jax.random.uniform(ks[3], (H, H), jnp.float32, -sd, sd), 'bk': jax.random.uniform(ks[4], (H,), jnp.float32, -sd, sd), 'Wv': jax.random.uniform(ks[5], (H, H), jnp.float32, -sd, sd), 'bv': jax.random.uniform(ks[6], (H,), jnp.float32, -sd, sd)}
        return inp
    _L1_attn_all = _L1_attn_setup()
    _L1_attn_in = {k: v for k, v in _L1_attn_all.items() if k in ('Wq', 'bq', 'Wk', 'bk', 'Wv', 'bv')}
    del _L1_attn_all

    def _L1_ffn_setup():
        import jax, jax.numpy as jnp
        import numpy as np
        HID, FFN, E, K = (256, 1024, 8, 2)
        CAP_FACTOR = 1.25
        key = jax.random.key(seed)
        k1, k2, k3, k4 = jax.random.split(key, 4)
        B, T = (4, 512)
        x = jax.random.normal(k1, (B, T, HID), dtype=jnp.float32)
        router_w = jax.random.normal(k2, (E, HID), dtype=jnp.float32) * 0.02
        w1 = jax.random.normal(k3, (E, HID, FFN), dtype=jnp.float32) * 0.02
        w2 = jax.random.normal(k4, (E, FFN, HID), dtype=jnp.float32) * 0.02
        return {'x': x, 'router_w': router_w, 'w1': w1, 'w2': w2}
    _L1_ffn_all = _L1_ffn_setup()
    _L1_ffn_in = {k: v for k, v in _L1_ffn_all.items() if k in ('router_w', 'w1', 'w2')}
    del _L1_ffn_all
    return {'x': x, 'ctx_1024': ctx_1024, 'L0_xattn_Wq': _L0_xattn_in['Wq'], 'L0_xattn_bq': _L0_xattn_in['bq'], 'L0_xattn_Wk': _L0_xattn_in['Wk'], 'L0_xattn_bk': _L0_xattn_in['bk'], 'L0_xattn_Wv': _L0_xattn_in['Wv'], 'L0_xattn_bv': _L0_xattn_in['bv'], 'L0_attn_Wq': _L0_attn_in['Wq'], 'L0_attn_bq': _L0_attn_in['bq'], 'L0_attn_Wk': _L0_attn_in['Wk'], 'L0_attn_bk': _L0_attn_in['bk'], 'L0_attn_Wv': _L0_attn_in['Wv'], 'L0_attn_bv': _L0_attn_in['bv'], 'L0_attn_Wo': _L0_attn_in['Wo'], 'L0_attn_bo': _L0_attn_in['bo'], 'L0_ffn_w1': _L0_ffn_in['w1'], 'L0_ffn_w2': _L0_ffn_in['w2'], 'L1_xattn_wq': _L1_xattn_in['wq'], 'L1_xattn_bq': _L1_xattn_in['bq'], 'L1_xattn_wk': _L1_xattn_in['wk'], 'L1_xattn_bk': _L1_xattn_in['bk'], 'L1_xattn_wv': _L1_xattn_in['wv'], 'L1_xattn_bv': _L1_xattn_in['bv'], 'L1_xattn_wo': _L1_xattn_in['wo'], 'L1_xattn_bo': _L1_xattn_in['bo'], 'L1_attn_Wq': _L1_attn_in['Wq'], 'L1_attn_bq': _L1_attn_in['bq'], 'L1_attn_Wk': _L1_attn_in['Wk'], 'L1_attn_bk': _L1_attn_in['bk'], 'L1_attn_Wv': _L1_attn_in['Wv'], 'L1_attn_bv': _L1_attn_in['bv'], 'L1_ffn_router_w': _L1_ffn_in['router_w'], 'L1_ffn_w1': _L1_ffn_in['w1'], 'L1_ffn_w2': _L1_ffn_in['w2']}

def reference(x, ctx_1024, L0_xattn_Wq, L0_xattn_bq, L0_xattn_Wk, L0_xattn_bk, L0_xattn_Wv, L0_xattn_bv, L0_attn_Wq, L0_attn_bq, L0_attn_Wk, L0_attn_bk, L0_attn_Wv, L0_attn_bv, L0_attn_Wo, L0_attn_bo, L0_ffn_w1, L0_ffn_w2, L1_xattn_wq, L1_xattn_bq, L1_xattn_wk, L1_xattn_bk, L1_xattn_wv, L1_xattn_bv, L1_xattn_wo, L1_xattn_bo, L1_attn_Wq, L1_attn_bq, L1_attn_Wk, L1_attn_bk, L1_attn_Wv, L1_attn_bv, L1_ffn_router_w, L1_ffn_w1, L1_ffn_w2):
    import jax
    import jax.numpy as jnp

    def _L0_xattn_ref(query, ref, Wq, bq, Wk, bk, Wv, bv):
        import jax, jax.numpy as jnp
        import numpy as np
        HIDDEN = 256
        norm_fact = 1.0 / np.sqrt(HIDDEN).astype(np.float32)
        Q = query @ Wq + bq
        K = ref @ Wk + bk
        V = ref @ Wv + bv
        scores = jnp.einsum('bqh,bkh->bqk', Q, K)
        attn = jax.nn.softmax(scores, axis=-1) * norm_fact
        return jnp.einsum('bqk,bkh->bqh', attn, V)

    def _L0_attn_ref(x, Wq, bq, Wk, bk, Wv, bv, Wo, bo):
        import jax, jax.numpy as jnp
        import numpy as np
        D_IN, HEAD_DIM = (256, 128)
        B, S, D = x.shape
        Q = jnp.einsum('bsd,hd->bsh', x, Wq) + bq
        K = jnp.einsum('bsd,hd->bsh', x, Wk) + bk
        V = jnp.einsum('bsd,hd->bsh', x, Wv) + bv
        scores = jnp.einsum('bqh,bkh->bqk', Q, K)
        causal = jnp.tril(jnp.ones((S, S), dtype=bool))
        scores = jnp.where(causal, scores, -jnp.inf)
        scale = jnp.float32(HEAD_DIM) ** (-0.5)
        attn = jax.nn.softmax(scores * scale, axis=-1)
        out = jnp.einsum('bqk,bkh->bqh', attn, V)
        return jnp.einsum('bsh,dh->bsd', out, Wo) + bo

    def _L0_ffn_ref(x, w1, w2):
        import jax, jax.numpy as jnp
        import numpy as np
        EMBED_DIM = 256
        HIDDEN = 4 * EMBED_DIM
        BATCH, SEQ = (4, 1024)
        EPS = 1e-05

        def _quant_weight(w):
            s = jnp.clip(jnp.mean(jnp.abs(w)), EPS, None)
            wq = jnp.clip(jnp.round(w / s), -1.0, 1.0) * s
            return w + jax.lax.stop_gradient(wq - w)

        def _quant_act(x):
            scale = 127.0 / jnp.clip(jnp.max(jnp.abs(x), axis=-1, keepdims=True), EPS, None)
            xq = jnp.clip(jnp.round(x * scale), -128.0, 127.0) / scale
            return x + jax.lax.stop_gradient(xq - x)

        def _bitlinear(x, w):
            return jnp.einsum('bsi,oi->bso', _quant_act(x), _quant_weight(w))
        h = jax.nn.gelu(_bitlinear(x, w1), approximate=False)
        return _bitlinear(h, w2)

    def _L1_xattn_ref(query, key_value, wq, bq, wk, bk, wv, bv, wo, bo):
        import jax, jax.numpy as jnp
        import numpy as np
        B, SQ, SKV, E, H = (4, 512, 512, 256, 16)
        D = E // H
        b, sq, e = query.shape
        skv = key_value.shape[1]
        h, d = (wq.shape[0], wq.shape[1])
        q = query.reshape(b, sq, h, d)
        kv = key_value.reshape(b, skv, h, d)
        qh = jnp.einsum('bshd,hed->bshe', q, wq) + bq
        kh = jnp.einsum('bthd,hed->bthe', kv, wk) + bk
        vh = jnp.einsum('bthd,hed->bthe', kv, wv) + bv
        scores = jnp.einsum('bshd,bthd->bhst', qh, kh) / jnp.sqrt(jnp.asarray(d, qh.dtype))
        attn = jax.nn.softmax(scores, axis=-1)
        ctx = jnp.einsum('bhst,bthd->bshd', attn, vh)
        out = ctx.reshape(b, sq, e)
        return out @ wo.T + bo

    def _L1_attn_ref(sequence_output, Wq, bq, Wk, bk, Wv, bv):
        import jax, jax.numpy as jnp
        import numpy as np
        H = 256
        W_CTX = 2

        def _local_attention(x, Wq, bq, Wk, bk, Wv, bv):
            B, S, Hd = x.shape
            Q = x @ Wq + bq
            K = x @ Wk + bk
            V = x @ Wv + bv
            w = W_CTX
            win = 2 * w + 1
            idx = jnp.arange(S)[:, None] + jnp.arange(-w, w + 1)[None, :]
            valid = (idx >= 0) & (idx < S)
            idx_c = jnp.clip(idx, 0, S - 1)
            Kw = K[:, idx_c]
            Vw = V[:, idx_c]
            scores = jnp.einsum('bsh,bswh->bsw', Q, Kw) / jnp.sqrt(jnp.float32(Hd))
            scores = jnp.where(valid[None], scores, -jnp.inf)
            probs = jax.nn.softmax(scores, axis=-1)
            return jnp.einsum('bsw,bswh->bsh', probs, Vw)
        return _local_attention(sequence_output, Wq, bq, Wk, bk, Wv, bv)

    def _L1_ffn_ref(x, router_w, w1, w2):
        import jax, jax.numpy as jnp
        import numpy as np
        HID, FFN, E, K = (256, 1024, 8, 2)
        CAP_FACTOR = 1.25
        B, T, H = x.shape
        N = B * T
        x_flat = x.reshape(N, H)
        C = max(1, int(CAP_FACTOR * N / E * K))
        logits = x_flat @ router_w.T
        probs = jax.nn.softmax(logits, axis=-1)
        top_v, top_i = jax.lax.top_k(probs, K)
        top_v = top_v / jnp.sum(top_v, axis=-1, keepdims=True)
        out = jnp.zeros_like(x_flat)
        for k in range(K):
            eid = top_i[:, k]
            gate = top_v[:, k]
            onehot = jax.nn.one_hot(eid, E, dtype=jnp.int32)
            pos = jnp.take_along_axis(jnp.cumsum(onehot, axis=0), eid[:, None], axis=1)[:, 0] - 1
            keep = pos < C
            slot = jnp.where(keep, eid * C + pos, E * C)
            buf = jnp.zeros((E * C + 1, H), dtype=x.dtype).at[slot].add(x_flat * keep[:, None].astype(x.dtype))
            expert_in = buf[:E * C].reshape(E, C, H)
            h = jax.nn.gelu(jnp.einsum('ech,ehf->ecf', expert_in, w1), approximate=False)
            y = jnp.einsum('ecf,efh->ech', h, w2)
            tok = y.reshape(E * C, H)[jnp.minimum(slot, E * C - 1)]
            out = out + tok * (gate * keep.astype(x.dtype))[:, None]
        return out.reshape(B, T, H)
    x = x + _L0_xattn_ref(_layernorm(x, axis=-1), ctx_1024, L0_xattn_Wq, L0_xattn_bq, L0_xattn_Wk, L0_xattn_bk, L0_xattn_Wv, L0_xattn_bv)
    x = x + _L0_attn_ref(_layernorm(x, axis=-1), L0_attn_Wq, L0_attn_bq, L0_attn_Wk, L0_attn_bk, L0_attn_Wv, L0_attn_bv, L0_attn_Wo, L0_attn_bo)
    x = x + _L0_ffn_ref(_layernorm(x, axis=-1), L0_ffn_w1, L0_ffn_w2)
    x = x + _L1_xattn_ref(_layernorm(x, axis=-1), ctx_1024, L1_xattn_wq, L1_xattn_bq, L1_xattn_wk, L1_xattn_bk, L1_xattn_wv, L1_xattn_bv, L1_xattn_wo, L1_xattn_bo)
    x = x + _L1_attn_ref(_layernorm(x, axis=-1), L1_attn_Wq, L1_attn_bq, L1_attn_Wk, L1_attn_bk, L1_attn_Wv, L1_attn_bv)
    x = x + _L1_ffn_ref(_layernorm(x, axis=-1), L1_ffn_router_w, L1_ffn_w1, L1_ffn_w2)
    return x

_drawn_inputs = setup_inputs


def setup_inputs(seed=0):
    import zlib

    import numpy as np

    out = dict(_drawn_inputs(seed))
    spreads = {'L0_attn_bq': (0.0, 2.0),
     'L0_attn_bk': (0.0, 2.0),
     'L0_attn_bv': (0.0, 0.357),
     'L0_attn_bo': (0.0, 0.1),
     'L1_xattn_bq': (0.0, 0.1),
     'L1_xattn_bk': (0.0, 2.0),
     'L1_xattn_bv': (0.0, 0.1),
     'L1_xattn_bo': (0.0, 0.1)}
    factors = {'L0_xattn_bq': 5.063,
     'L0_xattn_bk': 64.0,
     'L0_xattn_bv': 8.0,
     'L0_attn_Wq': 8.0,
     'L0_attn_Wk': 8.0,
     'L1_attn_bq': 8.0,
     'L1_attn_bk': 64.0}
    for name, (base, spread) in spreads.items():
        noise = np.random.default_rng([zlib.crc32(name.encode()), seed]).standard_normal(out[name].shape)
        drawn = base * np.exp(spread * noise) if base else spread * noise
        out[name] = jnp.asarray(drawn.astype(out[name].dtype))
    for name, factor in factors.items():
        out[name] = (out[name] * factor).astype(out[name].dtype)
    return out
```

```python
from contextlib import ExitStack

import numpy as np

import concourse.bass as bass
from concourse import mybir

F32 = mybir.dt.float32
BF16 = mybir.dt.bfloat16
U32 = mybir.dt.uint32
I32 = mybir.dt.int32
ALU = mybir.AluOpType
ACT = mybir.ActivationFunctionType
AX = mybir.AxisListType.X

P = 128
S = 32
NB = P // S
D = 256
H = D // P
KEYS = 257
KT = (KEYS - 1) // P
HD = 128
HEADS = 16
DH = D // HEADS
G = 4
HG = HEADS // G
GD = HG * DH
FF = 1024
FK = FF // P
EXP = 8
TOPK = 2
EPS = 1e-5
MAGIC = 1.5 * 2.0 ** 23
MASKED = -1e30
LNS = 6

CONSTS = ["ident", "causal", "band", "head_of_col", "head_of_dim", "fold", "before", "ones", "rev8", "trash", "row", "eids"]
WIDTH = {"ident": P, "causal": P, "band": P, "head_of_col": D, "head_of_dim": HG, "fold": S, "before": P,
         "ones": P, "rev8": EXP, "trash": TOPK, "row": 1, "eids": EXP}
FULL = ["x0_Wq_T", "x0_Wk_T", "x0_Wv", "x1_woT", "a1_Wq", "a1_Wk", "a1_Wv"]
ROWS = ["x0_bv", "a0_bo", "x1_bo", "a1_bv"]
COLS = ["x0_bq", "x1_bq", "x1_bv", "a1_bq", "a1_bk"]


class Signal:

    def __init__(self, handle, per):
        self.handle, self.per = handle, per

    def at(self, r, k):
        return r * self.per + k


def build(nc, t_in, out):
    tiles = t_in["x"].shape[0] * 2
    rounds = tiles // 2
    tokens = tiles * P
    cap = max(1, int(1.25 * tokens / EXP * TOPK))
    blocks = tokens * TOPK // P + EXP
    assert blocks % 2 == 0 and rounds % 2 == 0 and blocks <= P

    xres = nc.dram_tensor("xres", [rounds, 2, P, D], F32).ap()
    xnorm = nc.dram_tensor("xnorm", [rounds, 2, P, D], F32).ap()
    xrows = nc.dram_tensor("xrows", [blocks + TOPK, P, D], F32).ap()
    yrows = nc.dram_tensor("yrows", [blocks + TOPK, P, D], F32).ap()

    top = ExitStack()
    with top:
        def sem(name, stack=top):
            return stack.enter_context(nc.semaphore(name))

        def sig(name, per):
            return Signal(sem(name), per)

        def sb_in(stack):
            return lambda name, shape, dt=F32: stack.enter_context(nc.sbuf_tensor(name, shape, dt))

        keep = sb_in(top)
        const = {n: keep("c_" + n, [P, WIDTH[n]]) for n in CONSTS}
        ident = const["ident"]
        logits = keep("logits", [P, tiles, EXP])
        ps = top.enter_context(nc.psum_tensor("ps", [P, 8, 512], F32))
        zero = keep("zero", [P, 1, D])
        consts_loaded = sem("consts_loaded")

        main = ExitStack()
        with main:
            stack_phase(nc, main, t_in, const, logits, ps, consts_loaded, zero, xrows, yrows, xres, xnorm, rounds, sem, sig, sb_in(main))
        moe = ExitStack()
        with moe:
            expert_phase(nc, t_in, const, logits, ps, xres, xnorm, xrows, yrows, out, rounds, cap, blocks, zero,
                         sem, sig, sb_in(moe))


def stack_phase(nc, ctx, t_in, const, logits, ps, consts_loaded, zero, xrows, yrows, xres, xnorm, rounds, sem, sig, sb):
    ident = const["ident"]
    full = {n: sb("w_" + n, [P, H, D]) for n in FULL}
    rows = {n: sb("r_" + n, [P, D]) for n in ROWS}
    cols = {n: sb("b_" + n, [P, H]) for n in COLS}
    a0_qkv = {n: sb("w_" + n, [P, H, HD]) for n in ("a0_Wq_T", "a0_Wk_T", "a0_Wv_T")}
    a0_woT = sb("a0_woT", [P, D])
    a0_col = {n: sb("b_" + n, [P, 1]) for n in ("a0_bq", "a0_bk", "a0_bv")}
    bd = {n: sb("w_" + n, [P, H, P]) for n in ("x1_wq", "x1_wk", "x1_wv")}
    router = sb("router", [P, H, EXP])
    fw = [sb("f1", [P, H, FF], BF16), sb("f2", [P, FK, D], BF16)]
    fw_abs = sb("fw_abs", [P, 2])
    fw_scale = sb("fw_scale", [P, 2])
    fw_inv = sb("fw_inv", [P, 2])
    identb = sb("identb", [P, P], BF16)
    x0_A = sb("x0_A", [P, H, D])
    x0_c = sb("x0_c", [P, H])
    x1_B = sb("x1_B", [P, H, P])
    x1_c = sb("x1_c", [P, H])
    x1_W = sb("x1_W", [P, H, D])
    bv_rep = sb("bv_rep", [P, H, P])
    minus_half = sb("minus_half", [P, 1])

    xin = [[sb(f"xin{s}{j}", [P, D]) for j in (0, 1)] for s in (0, 1)]
    cn = [[sb(f"cn{s}{j}", [P, NB, KT, D]) for j in (0, 1)] for s in (0, 1)]
    cT = [[sb(f"cT{s}{j}", [P, H, NB, KEYS]) for j in (0, 1)] for s in (0, 1)]
    lastq = [[sb(f"lastq{s}{j}", [P, D]) for j in (0, 1)] for s in (0, 1)]
    lastk = [[sb(f"lastk{s}{j}", [P, NB, D]) for j in (0, 1)] for s in (0, 1)]

    def pair(name, shape, dt=F32):
        return [sb(f"{name}{j}", shape, dt) for j in (0, 1)]

    x = pair("x", [P, D])
    xb = pair("xb", [P, D])
    st6 = pair("st6", [P, 6])
    mv = pair("mv", [P, 2])
    ve = pair("ve", [P, 1])
    rstd = pair("rstd", [P, 1])
    xn = pair("xn", [P, D])
    xnT = pair("xnT", [P, H, P])
    qT = pair("qT", [P, H, P])
    kT = pair("kT", [P, H, P])
    val = pair("val", [P, D])
    nmax = pair("nmax", [P, 1])
    rsum = pair("rsum", [P, 1])
    rinv = pair("rinv", [P, 1])
    prob = pair("prob", [P, KEYS])
    probT = pair("probT", [P, KT, P])
    att = pair("att", [P, D])
    attT = pair("attT", [P, H, P])
    am = pair("am", [P, 1])
    qs = pair("qs", [P, 1])
    dq = pair("dq", [P, 2])
    xq = pair("xq", [P, D], BF16)
    xqT = pair("xqT", [P, H, P], BF16)
    hid_both = sb("hid", [P, 2, FF])
    hid = [hid_both[:, j, :] for j in (0, 1)]
    hq = pair("hq", [P, FF], BF16)
    hqT = pair("hqT", [P, FK, P], BF16)
    qblk = pair("qblk", [P, H, NB, HG, S])
    p1 = pair("p1_", [P, G, KEYS])
    p1T_both = sb("p1T", [P, 2, G, KT, P])
    p1T = [p1T_both[:, j] for j in (0, 1)]
    fw_raw = [p1T_both[:].rearrange("p j g k t -> p (j g k t)"), hid_both[:].rearrange("p j f -> p (j f)")]
    nmax1 = pair("nmax1", [P, G])
    rsum1 = pair("rsum1", [P, G])
    rinv1 = pair("rinv1", [P, G])
    o1 = pair("o1_", [P, G, GD])
    om = pair("om", [P, G, GD])
    hold = sb("hold", [P, 2])

    wload = sem("weights_loaded")
    NW = len(FULL) + len(ROWS) + len(COLS) + 3 + 1 + 3 + 3 + 1 + 2
    su_mm, su_cp = sem("setup_product"), sem("setup_copied")
    su_q = sem("weights_quantised_step")
    half_set = sem("minus_half_set")
    zero_ok, zeroed = sem("zero_rows"), sem("rows_zeroed")
    x_in = [[sem(f"x_in{s}{j}") for j in (0, 1)] for s in (0, 1)]
    c_in = [[sem(f"context_in{s}{j}") for j in (0, 1)] for s in (0, 1)]
    x_saved, n_saved = [sem(f"x_saved{j}") for j in (0, 1)], [sem(f"norm_saved{j}") for j in (0, 1)]
    LN = 2 * LNS
    ln_st, ln_mv, ln_ve, ln_rs = sig("ln_stats", LN), sig("ln_moments", LN), sig("ln_var_eps", LN), sig("ln_rstd", LN)
    xn_ok, xnT_ps, xnT_ok = sig("xn_ready", LN), sig("xnT_in_psum", LN - 2), sig("xnT_ready", LN - 2)
    x_new = sig("residual_updated", 2 * (LNS - 1))
    xb_ok = sig("residual_plus_bias", 2 * 4)
    SM = 2 * 3
    q_ps, q_ok = sig("queries_in_psum", 2 * 4), sig("queries_ready", 2 * 3)
    k_ok, v_ok = sig("keys_ready", 2 * 2), sig("values_ready", 2 * 2)
    sc_ps, sc_m, nm_ok = sig("scores_in_psum", SM), sig("scores_masked", 4), sig("row_max_ready", SM)
    pr_ok, ri_ok, pn_ok = sig("probs_ready", SM), sig("row_sum_inverted", SM), sig("probs_scaled", 2)
    pT_ps, pT_ok = sig("probsT_in_psum", SM), sig("probsT_ready", SM)
    pv_ps = sig("attended_in_psum", SM)
    last_ok, att_ok, attT_ps, attT_ok = sig("last_key_added", 2), sig("attended_ready", 2), sig("attendedT_in_psum", 2), sig("attendedT_ready", 4)
    y_ps = sig("block_out_in_psum", 6)
    am_raw, am_ok, qs_inv, qs_ok, dq_ok = sig("absmax_raw", 4), sig("absmax_ready", 4), sig("absmax_inverted", 4), sig("quant_scale_ready", 4), sig("dequant_ready", 4)
    qr_ok, qz_ok, qT_ps, qT_ok = sig("scaled_rounded", 4), sig("quantised", 4), sig("quantisedT_in_psum", 4), sig("quantisedT_ready", 4)
    up_ps, hid_ok, dn_ps = sig("up_in_psum", 2), sig("hidden_ready", 2), sig("down_in_psum", 2)
    qb_ok = sig("query_blocks_ready", 2)
    U = 2 * NB
    s1_ps, m1_ok, e1_ok = sig("x1_scores_in_psum", U * G), sig("x1_row_max", U * G), sig("x1_probs", U * G)
    t1_ps, t1_act, t1_dve = sig("x1_probsT_in_psum", U * G), sig("x1_probsT_lo", U), sig("x1_probsT_hi", U)
    v1_ps, r1_ok, o1_ok, om_ok = sig("x1_attended_in_psum", U), sig("x1_row_sum_inverted", U), sig("x1_last_key_added", U), sig("x1_heads_selected", U)
    f1_ps, f1_ok = sig("x1_folded_in_psum", U), sig("x1_folded_ready", U)
    lg_ps, lg_ok = sig("logits_in_psum", 2), sig("logits_saved", 2)

    def W(eng, s, r, k):
        eng.wait_ge(s.handle, s.at(r, k))

    def ap(t):
        return t if isinstance(t, bass.AP) else t[:]

    def bank(j, b):
        return ps[:, 4 * j + b, :]

    def halves(ap):
        return ap[:, 0:H * P].rearrange("p (h t) -> p h t", h=H)

    with nc.Block() as block:
        @block.sync
        def _(sp):
            for n in CONSTS:
                sp.dma_start(const[n][:], t_in["c_" + n]).then_inc(consts_loaded, 16)
            for n in FULL:
                sp.dma_start(full[n][:], t_in[n].rearrange("(h p) d -> p h d", p=P)).then_inc(wload, 16)
            for n in ROWS:
                sp.dma_start(rows[n][:], t_in[n].partition_broadcast(P)).then_inc(wload, 16)
            for n in COLS:
                sp.dma_start(cols[n][:], t_in[n]).then_inc(wload, 16)
            for n, buf in a0_qkv.items():
                sp.dma_start(buf[:], t_in[n].rearrange("(h p) d -> p h d", p=P)).then_inc(wload, 16)
            sp.dma_start(a0_woT[:], t_in["a0_woT"]).then_inc(wload, 16)
            for n, buf in a0_col.items():
                sp.dma_start(buf[:], t_in[n]).then_inc(wload, 16)
            for n, buf in bd.items():
                sp.dma_start(buf[:], t_in[n]).then_inc(wload, 16)
            sp.dma_start(router[:], t_in["router"].rearrange("(h p) e -> p h e", p=P)).then_inc(wload, 16)
            sp.dma_start(fw_raw[0].rearrange("p (h f) -> p h f", h=H), t_in["f1"].rearrange("(h p) f -> p h f", p=P)).then_inc(wload, 16)
            sp.dma_start(fw_raw[1].rearrange("p (k d) -> p k d", k=FK), t_in["f2"].rearrange("(k p) d -> p k d", p=P)).then_inc(wload, 16)

            def load(r, s):
                for j in (0, 1):
                    sp.dma_start(xin[s][j][:], t_in["x"][r, j]).then_inc(x_in[s][j], 16)
                for j in (0, 1):
                    sp.dma_start(cT[s][j][:], t_in["cT"][r, j]).then_inc(c_in[s][j], 16)
                    sp.dma_start(cn[s][j][:], t_in["cn"][r, j]).then_inc(c_in[s][j], 16)
                    sp.dma_start(lastq[s][j][:], t_in["lastq"][r, j]).then_inc(c_in[s][j], 16)
                    sp.dma_start(lastk[s][j][:], t_in["lastk"][r, j].partition_broadcast(P)).then_inc(c_in[s][j], 16)

            def store(r):
                for j in (0, 1):
                    W(sp, x_new, r, 2 * (LNS - 2) + j + 1)
                    sp.dma_start(xres[r, j], x[j][:]).then_inc(x_saved[j], 16)
                for j in (0, 1):
                    W(sp, xn_ok, r, 2 * (LNS - 1) + j + 1)
                    sp.dma_start(xnorm[r, j], xn[j][:]).then_inc(n_saved[j], 16)

            load(0, 0)
            load(1, 1)
            sp.wait_ge(zero_ok, 1)
            n_rows = xrows.shape[0]
            sp.dma_start(xrows.rearrange("b p d -> p b d"), zero[:].broadcast_to([P, n_rows, D])).then_inc(zeroed, 16)
            sp.dma_start(yrows[n_rows - TOPK:n_rows].rearrange("b p d -> p b d"), zero[:].broadcast_to([P, TOPK, D])).then_inc(zeroed, 16)
            with sp.Fori(0, rounds // 2 - 1) as i:
                for s in (0, 1):
                    r = i * 2 + s
                    W(sp, x_new, r, 8)
                    load(r + 2, s)
                    store(r)
            for s in (0, 1):
                store(rounds - 2 + s)
            sp.wait_ge(zeroed, 32)
            for j in (0, 1):
                sp.wait_ge(x_saved[j], 16 * rounds + 16)
                sp.wait_ge(n_saved[j], 16 * rounds + 16)

        @block.tensor
        def _(pe):
            pe.wait_ge(consts_loaded, 16 * len(CONSTS))
            pe.wait_ge(wload, 16 * NW)
            mm = nc.tensor.matmul
            for h in range(H):
                for k in range(H):
                    mm(ps[:, h, 0:D], full["x0_Wq_T"][:, k, h * P:(h + 1) * P], full["x0_Wk_T"][:, k, :], start=k == 0, stop=k == H - 1)
            for h in range(H):
                mm(ps[:, 2, h * P:(h + 1) * P], bd["x1_wq"][:, h, :], bd["x1_wk"][:, h, :], start=True, stop=True)
            for h in range(H):
                mm(ps[:, 3 + h, 0:D], bd["x1_wv"][:, h, :], full["x1_woT"][:, h, :], start=True, stop=True)
            for h in range(H):
                for k in range(H):
                    mm(ps[:, 5, h:h + 1], full["x0_Wk_T"][:, k, h * P:(h + 1) * P], cols["x0_bq"][:, k:k + 1], start=k == 0, stop=k == H - 1)
            for h in range(H):
                mm(ps[:, 5, 8 + h:9 + h], bd["x1_wk"][:, h, :], cols["x1_bq"][:, h:h + 1], start=True, stop=True)
            pe.wait_ge(su_cp, 1)
            for k in range(H):
                t = mm(ps[:, 6, 0:D], bv_rep[:, k, :], full["x1_woT"][:, k, :], start=k == 0, stop=k == H - 1)
            t.then_inc(su_mm, 1)
            pe.wait_ge(su_q, 3)
            mm(ps[:, 7, 0:2], const["ones"][:], fw_abs[:], start=True, stop=True).then_inc(su_mm, 1)
            pe.wait_ge(su_q, 20)
            pe.wait_ge(su_cp, 7)

            def norm_T(r, u):
                for j in (0, 1):
                    W(pe, xn_ok, r, 2 * (u if u < 2 else u + 1) + j + 1)
                    for h in range(H):
                        t = nc.tensor.transpose(halves(bank(j, 0))[:, h, :], xn[j][:, h * P:(h + 1) * P], ident[:])
                    t.then_inc(xnT_ps.handle, 1)

            def probs_T(r, n, parts, ready):
                for j in (0, 1):
                    W(pe, ready, r, (2 * n if ready is pr_ok else 0) + j + 1)
                    for k in range(parts):
                        t = nc.tensor.transpose(halves(bank(j, 0))[:, k, :], prob[j][:, k * P:(k + 1) * P], ident[:])
                    t.then_inc(pT_ps.handle, 1)

            def one_round(r, s):
                norm_T(r, 0)
                for j in (0, 1):
                    W(pe, xnT_ok, r, j + 1)
                    for h in range(H):
                        for k in range(H):
                            t = mm(halves(bank(j, 1))[:, h, :], x0_A[:, k, h * P:(h + 1) * P], xnT[j][:, k, :], start=k == 0, stop=k == H - 1)
                    t.then_inc(q_ps.handle, 1)
                for j in (0, 1):
                    W(pe, q_ok, r, j + 1)
                    pe.wait_ge(c_in[s][j], (r - s) * 32 + 64)
                    for b in range(NB):
                        for k in range(H):
                            t = mm(bank(j, 2)[b * S:(b + 1) * S, 0:KEYS], qT[j][:, k, b * S:(b + 1) * S], cT[s][j][:, k, b, :], start=k == 0, stop=k == H - 1)
                    t.then_inc(sc_ps.handle, 1)
                probs_T(r, 0, KT, pr_ok)
                for j in (0, 1):
                    W(pe, pT_ok, r, j + 1)
                    for b in range(NB):
                        for k in range(KT):
                            t = mm(bank(j, 3)[b * S:(b + 1) * S, 0:D], probT[j][:, k, b * S:(b + 1) * S], cn[s][j][:, b, k, :], start=k == 0, stop=k == KT - 1)
                    t.then_inc(pv_ps.handle, 1)
                for j in (0, 1):
                    W(pe, att_ok, r, j + 1)
                    for h in range(H):
                        t = nc.tensor.transpose(halves(bank(j, 0))[:, h, :], att[j][:, h * P:(h + 1) * P], ident[:])
                    t.then_inc(attT_ps.handle, 1)
                for j in (0, 1):
                    W(pe, attT_ok, r, j + 1)
                    for k in range(H):
                        t = mm(bank(j, 1)[:, 0:D], attT[j][:, k, :], full["x0_Wv"][:, k, :], start=k == 0, stop=k == H - 1)
                    t.then_inc(y_ps.handle, 1)
                norm_T(r, 1)
                for j in (0, 1):
                    W(pe, xnT_ok, r, 2 + j + 1)
                    for n, wname in enumerate(("a0_Wq_T", "a0_Wk_T")):
                        for k in range(H):
                            t = mm(halves(bank(j, 1))[:, n, :], a0_qkv[wname][:, k, :], xnT[j][:, k, :], start=k == 0, stop=k == H - 1)
                    for k in range(H):
                        t = mm(bank(j, 2)[:, 0:HD], xnT[j][:, k, :], a0_qkv["a0_Wv_T"][:, k, :], start=k == 0, stop=k == H - 1)
                    t.then_inc(q_ps.handle, 1)
                for j in (0, 1):
                    W(pe, q_ok, r, 2 + j + 1)
                    W(pe, k_ok, r, j + 1)
                    mm(bank(j, 3)[:, 0:P], qT[j][:, 0, :], kT[j][:, 0, :], start=True, stop=True).then_inc(sc_ps.handle, 1)
                probs_T(r, 1, 1, pn_ok)
                for j in (0, 1):
                    W(pe, pT_ok, r, 2 + j + 1)
                    W(pe, v_ok, r, j + 1)
                    mm(bank(j, 2)[:, 0:P], val[j][:, 0:HD], probT[j][:, 0, :], start=True, stop=True).then_inc(pv_ps.handle, 1)
                for j in (0, 1):
                    W(pe, attT_ok, r, 2 + j + 1)
                    mm(bank(j, 1)[:, 0:D], attT[j][:, 0, :], a0_woT[:], start=True, stop=True).then_inc(y_ps.handle, 1)
                for j in (0, 1):
                    W(pe, qz_ok, r, j + 1)
                    dst = bank(j, 0).bitcast(BF16)
                    for h in range(H):
                        t = nc.tensor.transpose(dst[:, h * P:(h + 1) * P], xq[j][:, h * P:(h + 1) * P], identb[:])
                    t.then_inc(qT_ps.handle, 1)
                for j in (0, 1):
                    W(pe, qT_ok, r, j + 1)
                    for n in range(FF // 512):
                        for k in range(H):
                            t = mm(bank(j, 1 + n), xqT[j][:, k, :], fw[0][:, k, n * 512:(n + 1) * 512], start=k == 0, stop=k == H - 1)
                    t.then_inc(up_ps.handle, 1)
                for j in (0, 1):
                    W(pe, qz_ok, r, 2 + j + 1)
                    dst = bank(j, 3).bitcast(BF16)
                    for k in range(FK):
                        t = nc.tensor.transpose(dst[:, k * P:(k + 1) * P], hq[j][:, k * P:(k + 1) * P], identb[:])
                    t.then_inc(qT_ps.handle, 1)
                for j in (0, 1):
                    W(pe, qT_ok, r, 2 + j + 1)
                    for k in range(FK):
                        t = mm(bank(j, 0)[:, 0:D], hqT[j][:, k, :], fw[1][:, k, :], start=k == 0, stop=k == FK - 1)
                    t.then_inc(dn_ps.handle, 1)
                norm_T(r, 2)
                for j in (0, 1):
                    W(pe, xnT_ok, r, 4 + j + 1)
                    for h in range(H):
                        t = mm(halves(bank(j, 1))[:, h, :], x1_B[:, h, :], xnT[j][:, h, :], start=True, stop=True)
                    t.then_inc(q_ps.handle, 1)
                for v in range(U + 2):
                    if v < U:
                        b, j = v // 2, v % 2
                        if b == 0:
                            W(pe, qb_ok, r, j + 1)
                        for g in range(G):
                            if v >= 1:
                                W(pe, e1_ok, r, G * (v - 1) + g + 1)
                            lo = GD * (g % 2)
                            mm(ps[:, g, 0:KEYS], qblk[j][lo:lo + GD, g // 2, b, :, :].rearrange("p h q -> p (h q)"),
                               cT[s][j][lo:lo + GD, g // 2, b, :], start=True, stop=True).then_inc(s1_ps.handle, 1)
                    if v >= 2:
                        u = v - 2
                        j = u % 2
                        W(pe, om_ok, r, u + 1)
                        if u >= 1:
                            W(pe, f1_ok, r, u)
                        for h in range(H):
                            t = mm(ps[:, 7, h * S:(h + 1) * S], om[j][:, 2 * h:2 * h + 2, :].rearrange("p g d -> p (g d)"), const["fold"][:], start=True, stop=True)
                        t.then_inc(f1_ps.handle, 1)
                    if 1 <= v <= U:
                        u = v - 1
                        b, j = u // 2, u % 2
                        for g in range(G):
                            W(pe, e1_ok, r, G * u + g + 1)
                            if u >= 1 and g % 2 == 0:
                                W(pe, t1_act if g == 0 else t1_dve, r, u)
                            for k in range(KT):
                                t = nc.tensor.transpose(ps[:, 4 + g // 2, ((g % 2) * KT + k) * P:((g % 2) * KT + k + 1) * P], p1[j][:, g, k * P:(k + 1) * P], ident[:])
                            t.then_inc(t1_ps.handle, 1)
                        if u >= 1:
                            W(pe, o1_ok, r, u)
                        for g in range(G):
                            if g % 2 == 0:
                                W(pe, t1_act if g == 0 else t1_dve, r, u + 1)
                            for k in range(KT):
                                t = mm(ps[:, 6, g * P:(g + 1) * P], p1T[j][:, g, k, :], cn[s][j][:, b, k, g // 2 * P:(g // 2 + 1) * P], start=k == 0, stop=k == KT - 1)
                        t.then_inc(v1_ps.handle, 1)
                for j in (0, 1):
                    W(pe, f1_ok, r, U)
                    for k in range(H):
                        t = mm(bank(j, 1)[:, 0:D], attT[j][:, k, :], x1_W[:, k, :], start=k == 0, stop=k == H - 1)
                    t.then_inc(y_ps.handle, 1)
                norm_T(r, 3)
                for j in (0, 1):
                    W(pe, xnT_ok, r, 6 + j + 1)
                    for bk, wname in ((1, "a1_Wq"), (2, "a1_Wk")):
                        for h in range(H):
                            for k in range(H):
                                t = mm(halves(bank(j, bk))[:, h, :], full[wname][:, k, h * P:(h + 1) * P], xnT[j][:, k, :], start=k == 0, stop=k == H - 1)
                    for k in range(H):
                        t = mm(bank(j, 3)[:, 0:D], xnT[j][:, k, :], full["a1_Wv"][:, k, :], start=k == 0, stop=k == H - 1)
                    t.then_inc(q_ps.handle, 1)
                for j in (0, 1):
                    W(pe, q_ok, r, 4 + j + 1)
                    W(pe, k_ok, r, 2 + j + 1)
                    for k in range(H):
                        t = mm(bank(j, 0)[:, 0:P], qT[j][:, k, :], kT[j][:, k, :], start=k == 0, stop=k == H - 1)
                    t.then_inc(sc_ps.handle, 1)
                probs_T(r, 2, 1, pr_ok)
                for j in (0, 1):
                    W(pe, pT_ok, r, 4 + j + 1)
                    W(pe, v_ok, r, 2 + j + 1)
                    mm(bank(j, 1)[:, 0:D], probT[j][:, 0, :], val[j][:], start=True, stop=True).then_inc(pv_ps.handle, 1)
                norm_T(r, 4)
                for j in (0, 1):
                    W(pe, xnT_ok, r, 8 + j + 1)
                    for k in range(H):
                        t = mm(bank(j, 2)[:, 0:EXP], xnT[j][:, k, :], router[:, k, :], start=k == 0, stop=k == H - 1)
                    t.then_inc(lg_ps.handle, 1)

            with pe.Fori(0, rounds // 2) as i:
                for s in (0, 1):
                    one_round(i * 2 + s, s)

        @block.scalar
        def _(act):
            A = nc.scalar.activation
            act.wait_ge(consts_loaded, 16 * len(CONSTS))
            act.wait_ge(wload, 16 * NW)

            def norm_T(r, u):
                for j in (0, 1):
                    W(act, xnT_ps, r, 2 * u + j + 1)
                    A(xnT[j][:], halves(bank(j, 0)), ACT.Copy).then_inc(xnT_ok.handle, 1)

            def softmax(r, n, width):
                for j in (0, 1):
                    W(act, nm_ok, r, 2 * n + j + 1)
                    src = bank(j, 2)[:, 0:width] if n == 0 else att[j][:, 0:width]
                    A(prob[j][:, 0:width], src, ACT.Exp, bias=nmax[j][:], accum_out=rsum[j][:]).then_inc(pr_ok.handle, 1)

            def probs_T(r, n, parts):
                for j in (0, 1):
                    W(act, pT_ps, r, 2 * n + j + 1)
                    A(probT[j][:, 0:parts, :], halves(bank(j, 0))[:, 0:parts, :], ACT.Copy).then_inc(pT_ok.handle, 1)

            def one_round(r, s):
                norm_T(r, 0)
                for j in (0, 1):
                    W(act, q_ps, r, j + 1)
                    for h in range(H):
                        t = A(qT[j][:, h, :], halves(bank(j, 1))[:, h, :], ACT.Identity, bias=x0_c[:, h:h + 1])
                    t.then_inc(q_ok.handle, 1)
                softmax(r, 0, KEYS)
                probs_T(r, 0, KT)
                for j in (0, 1):
                    W(act, attT_ps, r, j + 1)
                    A(attT[j][:], halves(bank(j, 0)), ACT.Copy).then_inc(attT_ok.handle, 1)
                norm_T(r, 1)
                for j in (0, 1):
                    W(act, q_ps, r, 2 + j + 1)
                    A(qT[j][:, 0, :], halves(bank(j, 1))[:, 0, :], ACT.Identity, bias=a0_col["a0_bq"][:]).then_inc(q_ok.handle, 1)
                    A(kT[j][:, 0, :], halves(bank(j, 1))[:, 1, :], ACT.Identity, bias=a0_col["a0_bk"][:]).then_inc(k_ok.handle, 1)
                softmax(r, 1, P)
                probs_T(r, 1, 1)
                for j in (0, 1):
                    W(act, pv_ps, r, 2 + j + 1)
                    A(attT[j][:, 0, :], bank(j, 2)[:, 0:P], ACT.Identity, bias=a0_col["a0_bv"][:]).then_inc(attT_ok.handle, 1)
                for j in (0, 1):
                    W(act, qT_ps, r, j + 1)
                    A(xqT[j][:].rearrange("p h t -> p (h t)"), bank(j, 0).bitcast(BF16)[:, 0:H * P], ACT.Copy).then_inc(qT_ok.handle, 1)
                for j in (0, 1):
                    W(act, up_ps, r, j + 1)
                    W(act, dq_ok, r, j + 1)
                    A(hid[j], ps[:, 4 * j + 1:4 * j + 3, :].rearrange("p b f -> p (b f)"), ACT.Gelu, scale=dq[j][:, 0:1]).then_inc(hid_ok.handle, 1)
                for j in (0, 1):
                    W(act, qT_ps, r, 2 + j + 1)
                    A(hqT[j][:].rearrange("p k t -> p (k t)"), bank(j, 3).bitcast(BF16), ACT.Copy).then_inc(qT_ok.handle, 1)
                norm_T(r, 2)
                for v in range(U + 1):
                    if v < U:
                        j = v % 2
                        for g in range(G):
                            W(act, m1_ok, r, G * v + g + 1)
                            A(p1[j][:, g, :], ps[:, g, 0:KEYS], ACT.Exp, bias=nmax1[j][:, g:g + 1], accum_out=rsum1[j][:, g:g + 1]).then_inc(e1_ok.handle, 1)
                    if v >= 1:
                        u = v - 1
                        W(act, t1_ps, r, G * u + 2)
                        A(p1T[u % 2][:, 0:2].rearrange("p g k t -> p (g k t)"), ps[:, 4, :], ACT.Copy).then_inc(t1_act.handle, 1)
                norm_T(r, 3)
                for j in (0, 1):
                    W(act, q_ps, r, 6 + j + 1)
                    for h in range(H):
                        t = A(qT[j][:, h, :], halves(bank(j, 1))[:, h, :], ACT.Identity, bias=cols["a1_bq"][:, h:h + 1])
                    t.then_inc(q_ok.handle, 1)
                    for h in range(H):
                        t = A(kT[j][:, h, :], halves(bank(j, 2))[:, h, :], ACT.Identity, bias=cols["a1_bk"][:, h:h + 1])
                    t.then_inc(k_ok.handle, 1)
                softmax(r, 2, P)
                probs_T(r, 2, 1)
                norm_T(r, 4)

            act.wait_ge(su_cp, 7)
            with act.Fori(0, rounds // 2) as i:
                for s in (0, 1):
                    one_round(i * 2 + s, s)

        @block.gpsimd
        def _(pool):
            nc.gpsimd.memset(zero[:], 0.0).then_inc(zero_ok, 1)
            nc.gpsimd.memset(minus_half[:], -0.5).then_inc(half_set, 1)
            pool.wait_ge(half_set, 1)
            pool.wait_ge(wload, 16 * NW)

            def rstds(r, u):
                for j in (0, 1):
                    W(pool, ln_ve, r, 2 * u + j + 1)
                    nc.gpsimd.tensor_tensor(rstd[j][:], ve[j][:], minus_half[:], ALU.pow).then_inc(ln_rs.handle, 1)

            def plus_bias(r, n, name):
                for j in (0, 1):
                    W(pool, x_new, r, 2 * n + j + 1)
                    nc.gpsimd.tensor_tensor(xb[j][:], x[j][:], rows[name][:], ALU.add).then_inc(xb_ok.handle, 1)

            def one_round(r, s):
                for j in (0, 1):
                    pool.wait_ge(x_in[s][j], (r - s) * 8 + 16)
                    nc.gpsimd.tensor_tensor(xb[j][:], xin[s][j][:], rows["x0_bv"][:], ALU.add).then_inc(xb_ok.handle, 1)
                rstds(r, 0)
                plus_bias(r, 0, "a0_bo")
                rstds(r, 1)
                rstds(r, 2)
                plus_bias(r, 2, "x1_bo")
                rstds(r, 3)
                plus_bias(r, 3, "a1_bv")
                rstds(r, 4)
                rstds(r, 5)

            pool.wait_ge(su_cp, 7)
            with pool.Fori(0, rounds // 2) as i:
                for s in (0, 1):
                    one_round(i * 2 + s, s)

        @block.vector
        def _(dve):
            v_ = nc.vector
            dve.wait_ge(consts_loaded, 16 * len(CONSTS))
            dve.wait_ge(wload, 16 * NW)
            for h in range(H):
                t = v_.tensor_copy(bv_rep[:, h, :], cols["x1_bv"][:, h:h + 1].to_broadcast([P, P]))
            t.then_inc(su_cp, 1)
            v_.tensor_copy(identb[:], ident[:]).then_inc(su_q, 1)
            for n in (0, 1):
                v_.tensor_reduce(fw_abs[:, n:n + 1], fw_raw[n], AX, ALU.add, apply_absolute_value=True).then_inc(su_q, 1)
            dve.wait_ge(su_mm, 2)
            v_.tensor_scalar(fw_scale[:], ps[:, 7, 0:2], 1.0 / (D * FF), EPS, ALU.mult, ALU.max).then_inc(su_q, 1)
            dve.wait_ge(su_q, 4)
            v_.reciprocal(fw_inv[:], fw_scale[:]).then_inc(su_q, 1)
            dve.wait_ge(su_q, 5)
            for n in (0, 1):
                v_.tensor_scalar(fw_raw[n], fw_raw[n], fw_inv[:, n:n + 1], MAGIC, ALU.mult, ALU.add).then_inc(su_q, 1)
            dve.wait_ge(su_q, 7)
            for n in (0, 1):
                v_.tensor_scalar(fw_raw[n], fw_raw[n], MAGIC, 1.0, ALU.subtract, ALU.min).then_inc(su_q, 1)
            dve.wait_ge(su_q, 9)
            v_.tensor_scalar(fw[0][:].rearrange("p h f -> p (h f)"), fw_raw[0][:], -1.0, None, ALU.max).then_inc(su_q, 1)
            v_.tensor_scalar(fw[1][:].rearrange("p k d -> p (k d)"), fw_raw[1][:], -1.0, None, ALU.max).then_inc(su_q, 1)
            v_.tensor_scalar(fw_scale[:], fw_scale[:], 1.0 / 127.0, None, ALU.mult).then_inc(su_q, 9)
            v_.tensor_copy(x0_A[:], ps[:, 0:2, 0:D]).then_inc(su_cp, 1)
            v_.tensor_copy(x1_B[:], halves(ps[:, 2, :])).then_inc(su_cp, 1)
            v_.tensor_copy(x1_W[:], ps[:, 3:5, 0:D]).then_inc(su_cp, 1)
            v_.tensor_copy(x0_c[:], ps[:, 5, 0:H]).then_inc(su_cp, 1)
            v_.tensor_copy(x1_c[:], ps[:, 5, 8:8 + H]).then_inc(su_cp, 1)
            v_.tensor_tensor(rows["x1_bo"][:], ps[:, 6, 0:D], rows["x1_bo"][:], ALU.add)
            v_.tensor_scalar(rows["x0_bv"][:], rows["x0_bv"][:], float(D) ** -0.5, None, ALU.mult).then_inc(su_cp, 1)
            dve.wait_ge(su_cp, 7)
            dve.wait_ge(su_q, 20)
            for j in (0, 1):
                dve.sem_inc(x_saved[j], 16)
                dve.sem_inc(n_saved[j], 16)

            def norm(r, s, u):
                src = xin[s] if u == 0 else x
                for j in (0, 1):
                    if u == 0:
                        dve.wait_ge(x_saved[j], r * 16 + 16)
                        dve.wait_ge(n_saved[j], r * 16 + 16)
                        dve.wait_ge(x_in[s][j], (r - s) * 8 + 16)
                    else:
                        W(dve, x_new, r, 2 * (u - 1) + j + 1)
                    v_.bn_stats(st6[j][:], src[j][:]).then_inc(ln_st.handle, 1)
                for j in (0, 1):
                    W(dve, ln_st, r, 2 * u + j + 1)
                    v_.memset(hold[:, j:j + 1], 0.0)
                    v_.bn_aggr(mv[j][:], st6[j][:]).then_inc(ln_mv.handle, 1)
                for j in (0, 1):
                    W(dve, ln_mv, r, 2 * u + j + 1)
                    v_.tensor_scalar(ve[j][:], mv[j][:, 1:2], EPS, None, ALU.add).then_inc(ln_ve.handle, 1)
                for j in (0, 1):
                    W(dve, ln_rs, r, 2 * u + j + 1)
                    v_.tensor_scalar(xn[j][:], src[j][:], mv[j][:, 0:1], rstd[j][:], ALU.subtract, ALU.mult).then_inc(xn_ok.handle, 1)

            def row_max(r, n, width, scale, mask):
                for j in (0, 1):
                    W(dve, sc_ps, r, 2 * n + j + 1)
                    if mask is None:
                        v_.tensor_reduce(nmax[j][:], bank(j, 2)[:, 0:width], AX, ALU.max, negate=True).then_inc(nm_ok.handle, 1)
                    else:
                        src = bank(j, 3 if n == 1 else 0)[:, 0:width]
                        v_.scalar_tensor_tensor(att[j][:, 0:width], src, scale, mask[:], ALU.mult, ALU.add).then_inc(sc_m.handle, 1)
                if mask is not None:
                    for j in (0, 1):
                        W(dve, sc_m, r, 2 * (n - 1) + j + 1)
                        v_.tensor_reduce(nmax[j][:], att[j][:, 0:width], AX, ALU.max, negate=True).then_inc(nm_ok.handle, 1)

            def inverse_sum(r, n):
                for j in (0, 1):
                    W(dve, pr_ok, r, 2 * n + j + 1)
                    v_.reciprocal(rinv[j][:], rsum[j][:]).then_inc(ri_ok.handle, 1)

            def quantise(r, n, src, rounded, q, width):
                for j in (0, 1):
                    if n == 0:
                        W(dve, xn_ok, r, 4 + j + 1)
                    else:
                        W(dve, hid_ok, r, j + 1)
                    v_.tensor_reduce(am[j][:], ap(src[j]), AX, ALU.max, apply_absolute_value=True).then_inc(am_raw.handle, 1)
                for j in (0, 1):
                    W(dve, am_raw, r, 2 * n + j + 1)
                    v_.tensor_scalar(am[j][:], am[j][:], EPS, None, ALU.max).then_inc(am_ok.handle, 1)
                for j in (0, 1):
                    W(dve, am_ok, r, 2 * n + j + 1)
                    v_.reciprocal(qs[j][:], am[j][:]).then_inc(qs_inv.handle, 1)
                    v_.tensor_scalar(dq[j][:, n:n + 1], am[j][:], fw_scale[:, n:n + 1], None, ALU.mult).then_inc(dq_ok.handle, 1)
                for j in (0, 1):
                    W(dve, qs_inv, r, 2 * n + j + 1)
                    v_.tensor_scalar(qs[j][:], qs[j][:], 127.0, None, ALU.mult).then_inc(qs_ok.handle, 1)
                for j in (0, 1):
                    W(dve, qs_ok, r, 2 * n + j + 1)
                    v_.tensor_scalar(ap(rounded[j]), ap(src[j]), qs[j][:], MAGIC, ALU.mult, ALU.add).then_inc(qr_ok.handle, 1)
                for j in (0, 1):
                    W(dve, qr_ok, r, 2 * n + j + 1)
                    v_.tensor_scalar(q[j][:], ap(rounded[j]), MAGIC, 127.0, ALU.subtract, ALU.min).then_inc(qz_ok.handle, 1)

            def one_round(r, s):
                norm(r, s, 0)
                row_max(r, 0, KEYS, 1.0, None)
                inverse_sum(r, 0)
                for j in (0, 1):
                    W(dve, pv_ps, r, j + 1)
                    v_.scalar_tensor_tensor(att[j][:], lastq[s][j][:], prob[j][:, KEYS - 1:KEYS], bank(j, 3)[:, 0:D], ALU.mult, ALU.add).then_inc(last_ok.handle, 1)
                for j in (0, 1):
                    W(dve, last_ok, r, j + 1)
                    W(dve, ri_ok, r, j + 1)
                    v_.tensor_scalar(att[j][:], att[j][:], rinv[j][:], float(D) ** -0.5, ALU.mult, ALU.mult).then_inc(att_ok.handle, 1)
                for j in (0, 1):
                    W(dve, y_ps, r, j + 1)
                    W(dve, xb_ok, r, j + 1)
                    v_.tensor_tensor(x[j][:], bank(j, 1)[:, 0:D], xb[j][:], ALU.add).then_inc(x_new.handle, 1)
                norm(r, s, 1)
                for j in (0, 1):
                    W(dve, q_ps, r, 2 + j + 1)
                    v_.tensor_copy(val[j][:, 0:HD], bank(j, 2)[:, 0:HD]).then_inc(v_ok.handle, 1)
                row_max(r, 1, P, float(HD) ** -0.5, const["causal"])
                inverse_sum(r, 1)
                for j in (0, 1):
                    W(dve, ri_ok, r, 2 + j + 1)
                    v_.tensor_scalar(prob[j][:, 0:P], prob[j][:, 0:P], rinv[j][:], None, ALU.mult).then_inc(pn_ok.handle, 1)
                for j in (0, 1):
                    W(dve, y_ps, r, 2 + j + 1)
                    W(dve, xb_ok, r, 2 + j + 1)
                    v_.tensor_tensor(x[j][:], bank(j, 1)[:, 0:D], xb[j][:], ALU.add).then_inc(x_new.handle, 1)
                norm(r, s, 2)
                quantise(r, 0, xn, att, xq, D)
                quantise(r, 1, hid, hid, hq, FF)
                for j in (0, 1):
                    W(dve, dn_ps, r, j + 1)
                    W(dve, dq_ok, r, 2 + j + 1)
                    v_.scalar_tensor_tensor(x[j][:], bank(j, 0)[:, 0:D], dq[j][:, 1:2], x[j][:], ALU.mult, ALU.add).then_inc(x_new.handle, 1)
                norm(r, s, 3)
                for j in (0, 1):
                    W(dve, q_ps, r, 4 + j + 1)
                    for h in range(H):
                        for n in range(HG):
                            t = v_.tensor_scalar(qblk[j][:, h, :, n, :], halves(bank(j, 1))[:, h, :].rearrange("p (b q) -> p b q", b=NB),
                                                 x1_c[:, h:h + 1], const["head_of_dim"][:, n:n + 1], ALU.add, ALU.mult)
                    t.then_inc(qb_ok.handle, 1)
                for v in range(U + 2):
                    if v < U:
                        j = v % 2
                        for g in range(G):
                            W(dve, s1_ps, r, G * v + g + 1)
                            v_.tensor_reduce(nmax1[j][:, g:g + 1], ps[:, g, 0:KEYS], AX, ALU.max, negate=True).then_inc(m1_ok.handle, 1)
                    if v >= 2:
                        u = v - 2
                        b, j = u // 2, u % 2
                        W(dve, f1_ps, r, u + 1)
                        v_.tensor_copy(attT[j][:, :, b * S:(b + 1) * S], ps[:, 7, 0:H * S].rearrange("p (h q) -> p h q", h=H)).then_inc(f1_ok.handle, 1)
                    if 1 <= v <= U:
                        u = v - 1
                        b, j = u // 2, u % 2
                        W(dve, e1_ok, r, G * u + G)
                        v_.reciprocal(rinv1[j][:], rsum1[j][:]).then_inc(r1_ok.handle, 1)
                        W(dve, t1_ps, r, G * u + G)
                        v_.tensor_copy(p1T[j][:, 2:4].rearrange("p g k t -> p (g k t)"), ps[:, 5, :]).then_inc(t1_dve.handle, 1)
                        W(dve, v1_ps, r, u + 1)
                        for g in range(G):
                            t = v_.scalar_tensor_tensor(o1[j][:, g, :], lastk[s][j][:, b, g * GD:(g + 1) * GD], p1[j][:, g, KEYS - 1:KEYS],
                                                        ps[:, 6, g * P + g % 2 * GD:g * P + g % 2 * GD + GD], ALU.mult, ALU.add)
                        t.then_inc(o1_ok.handle, 1)
                        W(dve, r1_ok, r, u + 1)
                        W(dve, o1_ok, r, u + 1)
                        for g in range(G):
                            t = v_.scalar_tensor_tensor(om[j][:, g, :], o1[j][:, g, :], rinv1[j][:, g:g + 1], const["head_of_col"][:, g * GD:(g + 1) * GD], ALU.mult, ALU.mult)
                        t.then_inc(om_ok.handle, 1)
                for j in (0, 1):
                    W(dve, y_ps, r, 4 + j + 1)
                    W(dve, xb_ok, r, 4 + j + 1)
                    v_.tensor_tensor(x[j][:], bank(j, 1)[:, 0:D], xb[j][:], ALU.add).then_inc(x_new.handle, 1)
                norm(r, s, 4)
                for j in (0, 1):
                    W(dve, q_ps, r, 6 + j + 1)
                    v_.tensor_copy(val[j][:], bank(j, 3)[:, 0:D]).then_inc(v_ok.handle, 1)
                row_max(r, 2, P, float(D) ** -0.5, const["band"])
                inverse_sum(r, 2)
                for j in (0, 1):
                    W(dve, pv_ps, r, 4 + j + 1)
                    W(dve, ri_ok, r, 4 + j + 1)
                    W(dve, xb_ok, r, 6 + j + 1)
                    v_.scalar_tensor_tensor(x[j][:], bank(j, 1)[:, 0:D], rinv[j][:], xb[j][:], ALU.mult, ALU.add).then_inc(x_new.handle, 1)
                norm(r, s, 5)
                for j in (0, 1):
                    W(dve, lg_ps, r, j + 1)
                    v_.tensor_copy(logits[:, r * 2 + j, :], bank(j, 2)[:, 0:EXP]).then_inc(lg_ok.handle, 1)

            with dve.Fori(0, rounds // 2) as i:
                for s in (0, 1):
                    one_round(i * 2 + s, s)


def expert_phase(nc, t_in, const, logits, ps, xres, xnorm, xrows, yrows, out, rounds, cap, blocks, zero, sem, sig, sb):
    ident = const["ident"]
    T = rounds * 2
    w1 = sb("w1", [P, EXP, H, FF])
    w2 = sb("w2", [P, EXP, FK, D])
    hold = sb("rt_hold", [P, 2])
    prob = sb("rt_prob", [P, T, EXP])
    prob2 = sb("rt_prob2", [P, T, EXP])
    key = sb("rt_key", [P, T, EXP])
    hot = sb("rt_hot", [P, T, TOPK, EXP])
    best = sb("rt_best", [P, TOPK, T])
    tmp = sb("rt_tmp", [P, T])
    scan = [sb(f"rt_scan{n}", [P, T, TOPK * EXP]) for n in (0, 1)]
    pos = sb("rt_pos", [P, T, TOPK, EXP])
    kept = sb("rt_kept", [P, T, TOPK])
    gate = sb("gate", [P, T, TOPK])
    slotf = sb("rt_slotf", [P, T, TOPK])
    slot = sb("slot", [P, T, TOPK], U32)
    count = sb("rt_count", [P, EXP])
    first = sb("rt_first", [P, EXP])
    nb_i = sb("rt_blocks_i", [P, EXP], I32)
    nb = sb("rt_blocks", [P, EXP])
    upto = sb("rt_upto", [P, EXP + 1])
    ge = sb("rt_ge", [P, EXP])
    lt = sb("rt_lt", [P, EXP])
    tab = sb("rt_tab", [P, 1])
    tab_i = sb("block_expert", [1, P], I32)
    xs = [sb(f"xs{b}", [P, D]) for b in (0, 1)]
    ix = [sb(f"ix{b}", [P, TOPK], U32) for b in (0, 1)]
    xe = [sb(f"xe{b}", [P, D]) for b in (0, 1)]
    xeT = [sb(f"xeT{b}", [P, H, P]) for b in (0, 1)]
    he = [sb(f"he{b}", [P, FF]) for b in (0, 1)]
    heT = [sb(f"heT{b}", [P, FK, P]) for b in (0, 1)]
    ye = [sb(f"ye{b}", [P, D]) for b in (0, 1)]
    xo = [sb(f"xo{b}", [P, D]) for b in (0, 1)]
    yg = [[sb(f"yg{b}{k}", [P, D]) for k in range(TOPK)] for b in (0, 1)]

    w_in = sem("expert_weights_in")
    rt = sem("routing_step")
    rt_exp = sem("routing_exp")
    rt_pe = sem("routing_sums_in_psum")
    tab_ok = sem("block_table_ready")
    xs_in = [sem(f"norm_rows_in{b}") for b in (0, 1)]
    ix_ok = sig("slots_staged", 2)
    sent = [sem(f"rows_sent{b}") for b in (0, 1)]
    carried = sem("waits_carried")
    xe_in = [sem(f"block_in{b}") for b in (0, 1)]
    ye_out = [sem(f"block_out{b}") for b in (0, 1)]
    xeT_ps, xeT_ok, up_ps, he_ok = sig("block_xT_in_psum", 1), sig("block_xT_ready", 1), sig("block_up_in_psum", 2), sig("block_hidden", 2)
    heT_ps, heT_lo, heT_hi, y_ps, ye_ok = sig("block_hiddenT_in_psum", 2), sig("block_hiddenT_lo", 1), sig("block_hiddenT_hi", 1), sig("block_y_in_psum", 1), sig("block_y", 1)
    xo_in = [sem(f"residual_in{b}") for b in (0, 1)]
    yg_in = [sem(f"expert_rows_in{b}") for b in (0, 1)]
    ix2_ok, g_ok, xo_ok = sig("slots_staged_again", 2), sig("gated_first", 2), sig("output_ready", 2)
    out_saved = [sem(f"output_saved{b}") for b in (0, 1)]

    def W(eng, s, r, k):
        eng.wait_ge(s.handle, s.at(r, k))

    def skewed(eng, block_work):
        for u in (0, 1):
            block_work(u, u, first=u == 0)
        with eng.Fori(1, blocks // 2 - 1) as i:
            for b in (0, 1):
                block_work(i * 2 + b, b)
        for u in (blocks - 2, blocks - 1):
            block_work(u, u % 2, last=u == blocks - 1)

    R_LOGIT, R_HOT, R_KEPT, R_TAB = {}, {}, {}, {}

    def routing(dve):
        v_ = nc.vector
        n = [0]

        def step(ins):
            n[0] += 1
            ins.then_inc(rt, 1)
            dve.wait_ge(rt, n[0])
            return n[0]

        def bc(ap, axis, size):
            shape = list(ap.shape)
            shape.insert(axis, size)
            return ap.unsqueeze(axis).broadcast_to(shape)

        step(v_.tensor_reduce(tmp[:], logits[:], AX, ALU.max))
        R_LOGIT[0] = step(v_.tensor_tensor(prob[:], logits[:], bc(tmp[:], 2, EXP), ALU.subtract))
        dve.wait_ge(rt_exp, 1)
        step(v_.tensor_reduce(tmp[:], prob[:], AX, ALU.add))
        step(v_.reciprocal(tmp[:], tmp[:]))
        step(v_.tensor_tensor(prob[:], prob[:], bc(tmp[:], 2, EXP), ALU.mult))
        src = prob
        for k in range(TOPK):
            step(v_.tensor_reduce(best[:, k, :], src[:], AX, ALU.max))
            step(v_.tensor_tensor(key[:], src[:], bc(best[:, k, :], 2, EXP), ALU.is_equal))
            step(v_.tensor_tensor(key[:], key[:], bc(const["rev8"][:], 1, T), ALU.mult))
            step(v_.tensor_reduce(tmp[:], key[:], AX, ALU.max))
            R_HOT[0] = step(v_.tensor_tensor(hot[:, :, k, :], key[:], bc(tmp[:], 2, EXP), ALU.is_equal))
            if k == 0:
                step(v_.scalar_tensor_tensor(prob2[:], hot[:, :, 0, :], -2.0, prob[:], ALU.mult, ALU.add))
                src = prob2
        step(v_.tensor_tensor(tmp[:], best[:, 0, :], best[:, 1, :], ALU.add))
        step(v_.reciprocal(tmp[:], tmp[:]))
        for k in range(TOPK):
            step(v_.tensor_tensor(gate[:, :, k], best[:, k, :], tmp[:], ALU.mult))

        def running(width, inside, totals):
            a, b = scan
            step(v_.tensor_copy(a[:, :, 0:width], totals))
            d = 1
            while d < T:
                step(v_.tensor_copy(b[:, 0:d, 0:width], a[:, 0:d, 0:width]))
                step(v_.tensor_tensor(b[:, d:T, 0:width], a[:, d:T, 0:width], a[:, 0:T - d, 0:width], ALU.add))
                a, b = b, a
                d *= 2
            step(v_.tensor_copy(b[:, :, 0:width], a[:, :, 0:width]))
            step(v_.tensor_tensor(b[:, :, 0:width], b[:, :, 0:width], totals, ALU.subtract))
            step(v_.tensor_tensor(b[:, :, 0:width], b[:, :, 0:width], inside, ALU.add))
            return a, b

        TE = TOPK * EXP
        dve.wait_ge(rt_pe, 1)
        _, where = running(TE, ps[:, 0, 0:T * TE].rearrange("p (t e) -> p t e", e=TE), ps[:, 1, 0:T * TE].rearrange("p (t e) -> p t e", e=TE))
        hot_f = hot[:].rearrange("p t k e -> p t (k e)")
        R_KEPT[0] = step(v_.scalar_tensor_tensor(hot_f, where[:, :, 0:TE], float(cap), hot_f, ALU.is_lt, ALU.mult))
        step(v_.tensor_reduce(kept[:], hot[:], AX, ALU.add))
        step(v_.tensor_tensor(gate[:], gate[:], kept[:], ALU.mult))
        R_KEPT[0] = step(v_.tensor_tensor(key[:], hot[:, :, 0, :], hot[:, :, 1, :], ALU.add))
        dve.wait_ge(rt_pe, 2)
        total, where = running(EXP, ps[:, 2, 0:T * EXP].rearrange("p (t e) -> p t e", e=EXP), ps[:, 3, 0:T * EXP].rearrange("p (t e) -> p t e", e=EXP))
        step(v_.tensor_copy(count[:], total[:, T - 1, 0:EXP]))
        step(v_.tensor_scalar(count[:], count[:], float(P - 1), None, ALU.add))
        step(v_.tensor_copy(nb_i[:], count[:]))
        step(v_.tensor_scalar(nb_i[:], nb_i[:], P.bit_length() - 1, None, ALU.arith_shift_right))
        step(v_.tensor_copy(nb[:], nb_i[:]))
        step(v_.memset(upto[:], 0.0))
        for e in range(EXP):
            step(v_.tensor_tensor(upto[:, e + 1:e + 2], upto[:, e:e + 1], nb[:, e:e + 1], ALU.add))
        step(v_.tensor_scalar(first[:], upto[:, 0:EXP], float(P), None, ALU.mult))
        step(v_.tensor_tensor(where[:, :, 0:EXP], where[:, :, 0:EXP], bc(first[:], 1, T), ALU.add))
        for k in range(TOPK):
            step(v_.tensor_tensor(pos[:, :, k, :], hot[:, :, k, :], where[:, :, 0:EXP], ALU.mult))
        step(v_.tensor_reduce(slotf[:], pos[:], AX, ALU.add))
        step(v_.tensor_scalar(kept[:], kept[:], -1.0, 1.0, ALU.mult, ALU.add))
        step(v_.tensor_tensor(kept[:], kept[:], bc(const["trash"][:], 1, T), ALU.mult))
        step(v_.tensor_tensor(slotf[:], slotf[:], kept[:], ALU.add))
        step(v_.tensor_copy(slot[:], slotf[:]))
        for b in (0, 1):
            v_.tensor_copy(ix[b][:], slot[:, b, :]).then_inc(ix_ok.handle, 1)
        step(v_.tensor_scalar(ge[:], upto[:, 0:EXP], const["row"][:], None, ALU.is_le))
        step(v_.tensor_scalar(lt[:], upto[:, 1:EXP + 1], const["row"][:], None, ALU.is_gt))
        step(v_.tensor_tensor(ge[:], ge[:], lt[:], ALU.mult))
        step(v_.tensor_tensor(lt[:], ge[:], const["eids"][:], ALU.mult))
        R_TAB[0] = step(v_.tensor_reduce(tab[:], lt[:], AX, ALU.add))
        dve.wait_ge(rt_pe, 3)
        v_.tensor_copy(tab_i[:], ps[0:1, 4, 0:P]).then_inc(tab_ok, 1)

    with nc.Block() as block:
        @block.vector
        def _(dve):
            v_ = nc.vector
            routing(dve)
            with dve.Fori(1, rounds) as i:
                for b in (0, 1):
                    dve.wait_ge(sent[b], i * 32)
                    v_.tensor_copy(ix[b][:], slot[:, i * 2 + b, :]).then_inc(ix_ok.handle, 1)
            def block_copies(u, b, first=False, last=False):
                if not last:
                    W(dve, xeT_ps, u + 1, 1)
                    v_.tensor_copy(xeT[1 - b][:].rearrange("p h t -> p (h t)"), ps[:, 5 - b, 0:D]).then_inc(xeT_ok.handle, 1)
                if not first:
                    down_copy(u - 1, 1 - b)
                W(dve, heT_ps, u, 2)
                v_.tensor_copy(heT[b][:, FK // 2:FK, :].rearrange("p k t -> p (k t)"), ps[:, 2 * b + 1, :]).then_inc(heT_hi.handle, 1)

            def down_copy(u, b):
                W(dve, y_ps, u, 1)
                dve.wait_ge(ye_out[b], (u - b) * 8 + 16)
                v_.tensor_copy(ye[b][:], ps[:, 6 + b, 0:D]).then_inc(ye_ok.handle, 1)

            W(dve, xeT_ps, 0, 1)
            v_.tensor_copy(xeT[0][:].rearrange("p h t -> p (h t)"), ps[:, 4, 0:D]).then_inc(xeT_ok.handle, 1)
            skewed(dve, block_copies)
            down_copy(blocks - 1, 1)

            def stage_slots(i, b):
                v_.tensor_copy(ix[b][:], slot[:, i * 2 + b, :]).then_inc(ix2_ok.handle, 1)

            def combine(i):
                for b in (0, 1):
                    dve.wait_ge(yg_in[b], i * 32 + 32)
                    dve.wait_ge(xo_in[b], i * 16 + 16)
                    v_.scalar_tensor_tensor(xo[b][:], yg[b][0][:], gate[:, i * 2 + b, 0:1], xo[b][:], ALU.mult, ALU.add).then_inc(g_ok.handle, 1)
                for b in (0, 1):
                    W(dve, g_ok, i, b + 1)
                    v_.scalar_tensor_tensor(xo[b][:], yg[b][1][:], gate[:, i * 2 + b, 1:2], xo[b][:], ALU.mult, ALU.add).then_inc(xo_ok.handle, 1)

            for b in (0, 1):
                stage_slots(0, b)
            with dve.Fori(0, rounds - 1) as i:
                combine(i)
                for b in (0, 1):
                    stage_slots(i + 1, b)
            combine(rounds - 1)

        @block.tensor
        def _(pe):
            mm = nc.tensor.matmul
            TE = TOPK * EXP
            for src, s, width, at in ((hot[:].rearrange("p t k e -> p (t k e)"), R_HOT, T * TE, 0), (key[:].rearrange("p t e -> p (t e)"), R_KEPT, T * EXP, 2)):
                pe.wait_ge(rt, s[0] if s is R_KEPT else R_HOT[0])
                mm(ps[:, at, 0:width], const["before"][:], src, start=True, stop=True)
                mm(ps[:, at + 1, 0:width], const["ones"][:], src, start=True, stop=True).then_inc(rt_pe, 1)
            pe.wait_ge(rt, R_TAB[0])
            mm(ps[0:1, 4, 0:P], tab[:], ident[:], start=True, stop=True).then_inc(rt_pe, 1)
            pe.wait_ge(tab_ok, 1)
            pe.wait_ge(w_in, 2 * EXP * 16)

            def rows_T(u, b):
                pe.wait_ge(xe_in[b], (u - b) * 8 + 16)
                for h in range(H):
                    t = nc.tensor.transpose(ps[:, 4 + b, h * P:(h + 1) * P], xe[b][:, h * P:(h + 1) * P], ident[:])
                t.then_inc(xeT_ps.handle, 1)

            def down(u, b, e):
                W(pe, heT_lo, u, 1)
                W(pe, heT_hi, u, 1)
                for k in range(FK):
                    t = mm(ps[:, 6 + b, 0:D], heT[b][:, k, :], w2[:, e, k, :], start=k == 0, stop=k == FK - 1)
                t.then_inc(y_ps.handle, 1)

            def expert(u):
                return pe.value_load(tab_i[0:1, bass.ds(u, 1)], min_val=0, max_val=EXP - 1)

            def block_products(u, b, first=False, last=False):
                e = expert(u)
                W(pe, xeT_ok, u, 1)
                for n in range(2):
                    for k in range(H):
                        t = mm(ps[:, 2 * b + n, :], xeT[b][:, k, :], w1[:, e, k, n * 512:(n + 1) * 512], start=k == 0, stop=k == H - 1)
                    t.then_inc(up_ps.handle, 1)
                if not last:
                    rows_T(u + 1, 1 - b)
                if not first:
                    down(u - 1, 1 - b, expert(u - 1))
                for n in range(2):
                    W(pe, he_ok, u, n + 1)
                    for k in range(FK // 2):
                        f = n * FK // 2 + k
                        t = nc.tensor.transpose(ps[:, 2 * b + n, k * P:(k + 1) * P], he[b][:, f * P:(f + 1) * P], ident[:])
                    t.then_inc(heT_ps.handle, 1)

            rows_T(0, 0)
            skewed(pe, block_products)
            down(blocks - 1, 1, expert(blocks - 1))

        @block.scalar
        def _(act):
            A = nc.scalar.activation
            act.wait_ge(rt, R_LOGIT[0])
            A(prob[:], prob[:], ACT.Exp).then_inc(rt_exp, 1)

            def block_gelu(u, b, first=False, last=False):
                for n in range(2):
                    W(act, up_ps, u, n + 1)
                    A(he[b][:, n * 512:(n + 1) * 512], ps[:, 2 * b + n, :], ACT.Gelu).then_inc(he_ok.handle, 1)
                W(act, heT_ps, u, 1)
                A(heT[b][:, 0:FK // 2, :].rearrange("p k t -> p (k t)"), ps[:, 2 * b, :], ACT.Copy).then_inc(heT_lo.handle, 1)

            skewed(act, block_gelu)

        @block.gpsimd
        def _(pool):
            g = nc.gpsimd
            pool.sem_inc(carried, 1)
            x_flat, y_flat = xrows.rearrange("b p d -> (b p) d"), yrows.rearrange("b p d -> (b p) d")
            with pool.Fori(0, rounds) as i:
                for b in (0, 1):
                    pool.wait_ge(xs_in[b], i * 16 + 16)
                    W(pool, ix_ok, i, b + 1)
                    pool.wait_ge(carried, i * 2 + b + 1)
                    g.tensor_tensor(hold[:, 0:1], zero[:, 0, 0:1], zero[:, 0, 0:1], ALU.add).then_inc(carried, 1)
                    for k in range(TOPK):
                        g.indirect_dma_start(x_flat, bass.IndirectOffsetOnAxis(ap=ix[b][:, k:k + 1], axis=0), xs[b][:], None).then_inc(sent[b], 16)
            with pool.Fori(0, rounds) as i:
                for b in (0, 1):
                    for q in (0, 1):
                        pool.wait_ge(ye_out[q], 16 * (blocks // 2) + 16)
                    W(pool, ix2_ok, i, b + 1)
                    pool.wait_ge(carried, rounds * 2 + i * 2 + b + 1)
                    g.tensor_tensor(hold[:, 0:1], zero[:, 0, 0:1], zero[:, 0, 0:1], ALU.add).then_inc(carried, 1)
                    for k in range(TOPK):
                        g.indirect_dma_start(yg[b][k][:], None, y_flat, bass.IndirectOffsetOnAxis(ap=ix[b][:, k:k + 1], axis=0)).then_inc(yg_in[b], 16)

        @block.sync
        def _(sp):
            for b in (0, 1):
                sp.sem_inc(ye_out[b], 16)
                sp.sem_inc(out_saved[b], 16)
            for e in range(EXP):
                sp.dma_start(w1[:, e], t_in["m_w1"][e]).then_inc(w_in, 16)
                sp.dma_start(w2[:, e], t_in["m_w2"][e]).then_inc(w_in, 16)
            for b in (0, 1):
                sp.dma_start(xs[b][:], xnorm[0, b]).then_inc(xs_in[b], 16)
            with sp.Fori(1, rounds) as i:
                for b in (0, 1):
                    sp.wait_ge(sent[b], i * 32)
                    sp.dma_start(xs[b][:], xnorm[i, b]).then_inc(xs_in[b], 16)
            for b in (0, 1):
                sp.wait_ge(sent[b], rounds * 32)

            def load_block(u, b):
                sp.dma_start(xe[b][:], xrows[u]).then_inc(xe_in[b], 16)

            def store_block(u, b):
                W(sp, ye_ok, u, 1)
                sp.dma_start(yrows[u], ye[b][:]).then_inc(ye_out[b], 16)

            def block_transfers(u, b, first=False, last=False):
                if not first:
                    store_block(u - 1, 1 - b)
                if not last:
                    W(sp, xeT_ps, u + 1, 1)
                    load_block(u + 3, 1 - b)

            load_block(0, 0)
            load_block(1, 1)
            W(sp, xeT_ps, 0, 1)
            load_block(2, 0)
            block_transfers(0, 0, first=True)
            with sp.Fori(0, (blocks - 4) // 2) as i:
                for b in (0, 1):
                    block_transfers(i * 2 + b + 1, 1 - b)
            for u in range(blocks - 3, blocks):
                block_transfers(u, u % 2, last=True)
            store_block(blocks - 1, 1)
            with sp.Fori(0, rounds) as i:
                for b in (0, 1):
                    sp.wait_ge(out_saved[b], i * 16 + 16)
                    sp.dma_start(xo[b][:], xres[i, b]).then_inc(xo_in[b], 16)
                for b in (0, 1):
                    W(sp, xo_ok, i, b + 1)
                    sp.dma_start(out[i, b], xo[b][:]).then_inc(out_saved[b], 16)
            for b in (0, 1):
                sp.wait_ge(out_saved[b], rounds * 16 + 16)


def shape_constants(np, blocks):
    f = np.float32
    p = np.arange(P)
    same = p[:, None] // S == p[None, :] // S
    c = {}
    c["ident"] = np.eye(P, dtype=f)
    c["causal"] = np.where(same & (p[None, :] <= p[:, None]), 0.0, MASKED).astype(f)
    c["band"] = np.where(same & (abs(p[None, :] - p[:, None]) <= 2), 0.0, MASKED).astype(f)
    col = np.arange(D)
    c["head_of_col"] = (p[:, None] // S == (col[None, :] % GD) // DH).astype(f)
    c["head_of_dim"] = (((p % GD) // DH)[:, None] == np.arange(HG)[None, :]).astype(f) * f(DH ** -0.5)
    c["fold"] = (p[:, None] % S == np.arange(S)[None, :]).astype(f)
    c["before"] = (p[:, None] < p[None, :]).astype(f)
    c["ones"] = np.ones((P, P), f)
    c["rev8"] = np.broadcast_to((EXP - np.arange(EXP)).astype(f), (P, EXP))
    c["trash"] = (blocks * P + np.arange(TOPK)[None, :] * P + p[:, None]).astype(f)
    c["row"] = p[:, None].astype(f)
    c["eids"] = np.broadcast_to(np.arange(EXP).astype(f), (P, EXP))
    return {"c_" + n: np.ascontiguousarray(a) for n, a in c.items()}


def lay_out(np, v):
    a = {n: np.asarray(x) for n, x in v.items()}
    B = a["x"].shape[0]
    rounds = B // NB // 2
    tokens = B * S
    d = shape_constants(np, tokens * TOPK // P + EXP)
    d["x"] = a["x"].reshape(rounds, 2, P, D)
    ctx = a["ctx_1024"].reshape(rounds, 2, NB, KEYS, D)
    d["cn"] = ctx[:, :, :, :KEYS - 1].reshape(rounds, 2, NB, KT, P, D).transpose(0, 1, 4, 2, 3, 5)
    d["cT"] = ctx.reshape(rounds, 2, NB, KEYS, H, P).transpose(0, 1, 5, 4, 2, 3)
    d["lastk"] = ctx[:, :, :, KEYS - 1]
    d["lastq"] = np.repeat(d["lastk"], S, axis=2)
    d["x0_Wq_T"], d["x0_Wk_T"], d["x0_Wv"] = a["L0_xattn_Wq"].T, a["L0_xattn_Wk"].T, a["L0_xattn_Wv"]
    d["x1_woT"] = a["L1_xattn_wo"].T
    for n in ("Wq", "Wk", "Wv"):
        d["a1_" + n] = a["L1_attn_" + n]
        d[f"a0_{n}_T"] = a["L0_attn_" + n].T
    d["x0_bv"], d["a0_bo"], d["x1_bo"], d["a1_bv"] = a["L0_xattn_bv"], a["L0_attn_bo"], a["L1_xattn_bo"], a["L1_attn_bv"]

    def column(x):
        return x.reshape(H, P).T

    d["x0_bq"], d["a1_bq"], d["a1_bk"] = column(a["L0_xattn_bq"]), column(a["L1_attn_bq"]), column(a["L1_attn_bk"])
    d["x1_bq"], d["x1_bv"] = column(a["L1_xattn_bq"].reshape(-1)), column(a["L1_xattn_bv"].reshape(-1))
    d["a0_woT"] = a["L0_attn_Wo"].T
    for n in ("bq", "bk", "bv"):
        d["a0_" + n] = a["L0_attn_" + n].reshape(P, 1)
    for n in ("wq", "wk", "wv"):
        w = np.zeros((P, H, P), np.float32)
        for h in range(HEADS):
            lo = h * DH % P
            w[lo:lo + DH, h * DH // P, lo:lo + DH] = a["L1_xattn_" + n][h]
        d["x1_" + n] = w
    d["router"] = a["L1_ffn_router_w"].T
    d["f1"], d["f2"] = a["L0_ffn_w1"].T, a["L0_ffn_w2"].T
    d["m_w1"] = a["L1_ffn_w1"].reshape(EXP, H, P, FF).transpose(0, 2, 1, 3)
    d["m_w2"] = a["L1_ffn_w2"].reshape(EXP, FK, P, D).transpose(0, 2, 1, 3)
    return {n: np.ascontiguousarray(x) for n, x in d.items()}


def kernel(**inputs):
    import numpy as _np
    import concourse.bacc as _bacc
    from concourse import mybir as _mybir
    from concourse.bass_utils import run_bass_kernel_spmd as _run

    arrays = lay_out(_np, inputs)
    nc = _bacc.Bacc("TRN2", target_bir_lowering=False, num_devices=1)
    handles = {n: nc.dram_tensor("in_" + n, a.shape, _mybir.dt.from_np(a.dtype), kind="ExternalInput").ap() for n, a in arrays.items()}
    shape = arrays["x"].shape
    out = nc.dram_tensor("out_0", shape, F32, kind="ExternalOutput").ap()
    build(nc, handles, out)
    r = _run(nc, [{"in_" + n: a for n, a in arrays.items()}], core_ids=[0])
    return r.results[0]["out_0"].reshape(inputs["x"].shape)
```

```python
from contextlib import ExitStack

import numpy as np

import concourse.bass as bass
from concourse import mybir

F32 = mybir.dt.float32
BF16 = mybir.dt.bfloat16
U32 = mybir.dt.uint32
I32 = mybir.dt.int32
ALU = mybir.AluOpType
ACT = mybir.ActivationFunctionType
AX = mybir.AxisListType.X

P = 128
S = 32
NB = P // S
NJ = 4
J = range(NJ)
D = 256
H = D // P
KEYS = 257
KT = (KEYS - 1) // P
HD = 128
HEADS = 16
DH = D // HEADS
G = 4
HG = HEADS // G
GD = HG * DH
FF = 1024
FK = FF // P
EXP = 8
TOPK = 2
EPS = 1e-5
MAGIC = 1.5 * 2.0 ** 23
MASKED = -1e30
LNS = 6

CONSTS = ["ident", "causal", "band", "head_of_col", "head_of_dim", "fold", "before", "ones", "rev8", "trash", "row", "eids"]
WIDTH = {"ident": P, "causal": P, "band": P, "head_of_col": D, "head_of_dim": HG, "fold": S, "before": P,
         "ones": P, "rev8": EXP, "trash": TOPK, "row": 1, "eids": EXP}
FULL = ["x0_Wv", "a1_Wq", "a1_Wk", "a1_Wv"]
SETUP = ["x0_Wq_T", "x0_Wk_T", "x1_woT"]
ROWS = ["x0_bv", "a0_bo", "x1_bo", "a1_bv"]
COLS = ["x0_bq", "x1_bq", "x1_bv", "a1_bq", "a1_bk"]


class Signal:

    def __init__(self, handle, per):
        self.handle, self.per = handle, per

    def at(self, r, k):
        return r * self.per + k


def build(nc, t_in, out):
    tiles = t_in["x"].shape[0]
    rounds = tiles // NJ
    tokens = tiles * P
    cap = max(1, int(1.25 * tokens / EXP * TOPK))
    blocks = tokens * TOPK // P + EXP
    assert tiles % NJ == 0 and rounds >= 2 and blocks % 2 == 0 and blocks <= P

    xres = nc.dram_tensor("xres", [tiles, P, D], F32).ap()
    xnorm = nc.dram_tensor("xnorm", [tiles, P, D], F32).ap()
    xrows = nc.dram_tensor("xrows", [blocks + TOPK, P, D], F32).ap()
    yrows = nc.dram_tensor("yrows", [blocks + TOPK, P, D], F32).ap()

    top = ExitStack()
    with top:
        def sem(name, stack=top):
            return stack.enter_context(nc.semaphore(name))

        def sig(name, per):
            return Signal(sem(name), per)

        def sb_in(stack):
            return lambda name, shape, dt=F32: stack.enter_context(nc.sbuf_tensor(name, shape, dt))

        keep = sb_in(top)
        const = {n: keep("c_" + n, [P, WIDTH[n]]) for n in CONSTS}
        ident = const["ident"]
        logits = keep("logits", [P, tiles, EXP])
        ps = top.enter_context(nc.psum_tensor("ps", [P, 8, 512], F32))
        zero = keep("zero", [P, 1, D])
        consts_loaded = sem("consts_loaded")

        main = ExitStack()
        with main:
            stack_phase(nc, main, t_in, const, logits, ps, consts_loaded, zero, xrows, yrows, xres, xnorm, rounds, sem, sig, sb_in(main))
        moe = ExitStack()
        with moe:
            expert_phase(nc, t_in, const, logits, ps, xres, xnorm, xrows, yrows, out, tiles // 2, cap, blocks, zero,
                         sem, sig, sb_in(moe))


def stack_phase(nc, ctx, t_in, const, logits, ps, consts_loaded, zero, xrows, yrows, xres, xnorm, rounds, sem, sig, sb):
    ident = const["ident"]
    full = {n: sb("w_" + n, [P, H, D]) for n in FULL}
    rows = {n: sb("r_" + n, [P, D]) for n in ROWS}
    cols = {n: sb("b_" + n, [P, H]) for n in COLS}
    a0_qkv = {n: sb("w_" + n, [P, H, HD]) for n in ("a0_Wq_T", "a0_Wk_T", "a0_Wv_T")}
    a0_woT = sb("a0_woT", [P, D])
    a0_col = {n: sb("b_" + n, [P, 1]) for n in ("a0_bq", "a0_bk", "a0_bv")}
    router = sb("router", [P, H, EXP])
    fw = [sb("f1", [P, H, FF], BF16), sb("f2", [P, FK, D], BF16)]
    fw_abs = sb("fw_abs", [P, 2])
    fw_scale = sb("fw_scale", [P, 2])
    fw_inv = sb("fw_inv", [P, 2])
    identb = sb("identb", [P, P], BF16)
    x0_A = sb("x0_A", [P, H, D])
    x0_c = sb("x0_c", [P, H])
    x1_B = sb("x1_B", [P, H, P])
    x1_c = sb("x1_c", [P, H])
    x1_cm = sb("x1_cm", [P, HG])
    x1_W = sb("x1_W", [P, H, D])
    minus_half = sb("minus_half", [P, 1])

    def per_tile(name, shape, dt=F32):
        return [sb(f"{name}{j}", shape, dt) for j in J]

    xin = per_tile("xin", [P, D])
    cn = per_tile("cn", [P, NB, KT, D])
    cT = per_tile("cT", [P, H, NB, KEYS])
    lastq = per_tile("lastq", [P, D])
    lastk = per_tile("lastk", [P, NB, D])
    x = per_tile("x", [P, D])
    xb = per_tile("xb", [P, D])
    st6 = per_tile("st6", [P, 6])
    mv = per_tile("mv", [P, 2])
    ve = per_tile("ve", [P, 1])
    rstd = per_tile("rstd", [P, 1])
    xn = per_tile("xn", [P, D])
    xnT = per_tile("xnT", [P, H, P])
    qT = per_tile("qT", [P, H, P])
    val = per_tile("val", [P, D])
    nmax = per_tile("nmax", [P, 1])
    rsum = per_tile("rsum", [P, 1])
    rinv = per_tile("rinv", [P, 1])
    prob = per_tile("prob", [P, KEYS])
    probT = per_tile("probT", [P, KT, P])
    att = per_tile("att", [P, D])
    attT = per_tile("attT", [P, H, P])
    kT = [t[:].rearrange("p (h t) -> p h t", h=H) for t in att]
    am = per_tile("am", [P, 1])
    qs = per_tile("qs", [P, 1])
    dq = per_tile("dq", [P, 2])
    xq = per_tile("xq", [P, D], BF16)
    xqT = per_tile("xqT", [P, H, P], BF16)
    hold = sb("hold", [P, NJ])
    nmax1 = [sb(f"nmax1_{q}", [P, G]) for q in (0, 1)]
    rsum1 = [sb(f"rsum1_{q}", [P, G]) for q in (0, 1)]
    rinv1 = [sb(f"rinv1_{q}", [P, G]) for q in (0, 1)]
    lastv = [sb(f"lastv{q}", [P, G, GD]) for q in (0, 1)]
    select = [sb(f"select{q}", [P, G, GD]) for q in (0, 1)]
    om = [sb(f"om{q}", [P, G, GD]) for q in (0, 1)]
    wide = sb("wide", [P, NJ * FF])
    region_p = sb("region_p", [P, 2 * G * KEYS])
    region_t = sb("region_t", [P, 2 * G * KT * P])
    fw_raw = [wide[:, 0:H * FF], wide[:, H * FF:2 * H * FF]]
    hid = [wide[:, j * FF:(j + 1) * FF] for j in J]
    qblk = [wide[:, j * FF:(j + 1) * FF].rearrange("p (h b n q) -> p h b n q", h=H, b=NB, n=HG) for j in J]
    setup_w = {n: region_p[:, i * H * D:(i + 1) * H * D].rearrange("p (h d) -> p h d", h=H) for i, n in enumerate(SETUP)}
    hq = [region_p[:, j * FF // 2:(j + 1) * FF // 2].bitcast(BF16) for j in J]
    p1 = [region_p[:, q * G * KEYS:(q + 1) * G * KEYS].rearrange("p (g k) -> p g k", g=G) for q in (0, 1)]
    *bd_views, bv_rep = [region_t[:, i * H * P:(i + 1) * H * P].rearrange("p (h d) -> p h d", h=H) for i in range(4)]
    bd = dict(zip(("x1_wq", "x1_wk", "x1_wv"), bd_views))
    hqT = [region_t[:, j * FF // 2:(j + 1) * FF // 2].bitcast(BF16).rearrange("p (k t) -> p k t", k=FK) for j in J]
    p1T = [region_t[:, q * G * KT * P:(q + 1) * G * KT * P].rearrange("p (g k t) -> p g k t", g=G, k=KT) for q in (0, 1)]

    wload = sem("weights_loaded")
    NW = len(FULL) + len(SETUP) + len(ROWS) + len(COLS) + 3 + 1 + 3 + 3 + 1 + 2
    su_mm, su_cp = sem("setup_product"), sem("setup_copied")
    SU_CP, SU_Q = 9, 11
    su_q = sem("weights_quantised_step")
    half_set = sem("minus_half_set")
    zero_ok, zeroed = sem("zero_rows"), sem("rows_zeroed")
    x_in = [sem(f"x_in{j}") for j in J]
    c_in = [sem(f"context_in{j}") for j in J]
    x_saved, n_saved = [sem(f"x_saved{j}") for j in J], [sem(f"norm_saved{j}") for j in J]
    LN = NJ * LNS
    ln_st, ln_mv, ln_ve, ln_rs = sig("ln_stats", LN), sig("ln_moments", LN), sig("ln_var_eps", LN), sig("ln_rstd", LN)
    xn_ok, xnT_ps, xnT_ok = sig("xn_ready", LN), sig("xnT_in_psum", LN - NJ), sig("xnT_ready", LN - NJ)
    x_new = sig("residual_updated", NJ * (LNS - 1))
    xb_ok = sig("residual_plus_bias", NJ * 4)
    SM = NJ * 3
    q_ps, q_ok = sig("queries_in_psum", NJ * 4), sig("queries_ready", NJ * 3)
    k_ok, v_ok = sig("keys_ready", NJ * 2), sig("values_ready", NJ * 2)
    sc_ps, sc_m, nm_ok = sig("scores_in_psum", SM), sig("scores_masked", NJ * 2), sig("row_max_ready", SM)
    pr_ok, ri_ok, pn_ok = sig("probs_ready", SM), sig("row_sum_inverted", SM), sig("probs_scaled", NJ)
    pT_ps, pT_ok = sig("probsT_in_psum", SM), sig("probsT_ready", SM)
    pv_ps = sig("attended_in_psum", SM)
    att_ok, attT_ps, attT_ok = sig("attended_ready", NJ), sig("attendedT_in_psum", NJ), sig("attendedT_ready", NJ * 2)
    y_ps = sig("block_out_in_psum", NJ * 3)
    am_raw, am_ok, qs_ok, dq_ok = sig("absmax_raw", NJ * 2), sig("absmax_ready", NJ * 2), sig("quant_scale_ready", NJ * 2), sig("dequant_ready", NJ * 2)
    qr_ok, qz_ok, qT_ps, qT_ok = sig("scaled_rounded", NJ * 2), sig("quantised", NJ * 2), sig("quantisedT_in_psum", NJ * 2), sig("quantisedT_ready", NJ * 2)
    up_ps, hid_ok, dn_ps = sig("up_in_psum", NJ), sig("hidden_ready", NJ), sig("down_in_psum", NJ)
    qb_dve, qb_act = sig("query_blocks_lo", NJ), sig("query_blocks_hi", NJ)
    U = NJ * NB
    s1_ps, m1_ok, e1_ok = sig("x1_scores_in_psum", U * G), sig("x1_row_max", U * G), sig("x1_probs", U * G)
    t1_ps, t1_act, t1_dve = sig("x1_probsT_in_psum", U * G), sig("x1_probsT_lo", U), sig("x1_probsT_hi", U)
    v1_ps, r1_ok, lv_ok, sel_ok = sig("x1_attended_in_psum", U), sig("x1_row_sum_inverted", U), sig("x1_last_key_values", U), sig("x1_selection", U)
    o1_ok, om_ok = sig("x1_last_key_added", U), sig("x1_heads_selected", U)
    f1_ps, f1_ok = sig("x1_folded_in_psum", U), sig("x1_folded_ready", U)
    lg_ps, lg_ok = sig("logits_in_psum", NJ), sig("logits_saved", NJ)

    def W(eng, s, r, k):
        eng.wait_ge(s.handle, s.at(r, k))

    def ap(t):
        return t if isinstance(t, bass.AP) else t[:]

    def bank(j, b):
        return ps[:, 2 * j + b, :]

    def halves(ap):
        return ap[:, 0:H * P].rearrange("p (h t) -> p h t", h=H)

    with nc.Block() as block:
        @block.sync
        def _(sp):
            for n in CONSTS:
                sp.dma_start(const[n][:], t_in["c_" + n]).then_inc(consts_loaded, 16)
            for n, buf in list(setup_w.items()) + list(full.items()):
                sp.dma_start(ap(buf), t_in[n].rearrange("(h p) d -> p h d", p=P)).then_inc(wload, 16)
            for n in ROWS:
                sp.dma_start(rows[n][:], t_in[n].partition_broadcast(P)).then_inc(wload, 16)
            for n in COLS:
                sp.dma_start(cols[n][:], t_in[n]).then_inc(wload, 16)
            for n, buf in a0_qkv.items():
                sp.dma_start(buf[:], t_in[n].rearrange("(h p) d -> p h d", p=P)).then_inc(wload, 16)
            sp.dma_start(a0_woT[:], t_in["a0_woT"]).then_inc(wload, 16)
            for n, buf in a0_col.items():
                sp.dma_start(buf[:], t_in[n]).then_inc(wload, 16)
            for n, buf in bd.items():
                sp.dma_start(buf, t_in[n]).then_inc(wload, 16)
            sp.dma_start(router[:], t_in["router"].rearrange("(h p) e -> p h e", p=P)).then_inc(wload, 16)
            sp.dma_start(fw_raw[0].rearrange("p (h f) -> p h f", h=H), t_in["f1"].rearrange("(h p) f -> p h f", p=P)).then_inc(wload, 16)
            sp.dma_start(fw_raw[1].rearrange("p (k d) -> p k d", k=FK), t_in["f2"].rearrange("(k p) d -> p k d", p=P)).then_inc(wload, 16)

            def load_x(r, j):
                sp.dma_start(xin[j][:], t_in["x"][r * NJ + j]).then_inc(x_in[j], 16)

            def load_context(r, j):
                sp.dma_start(cT[j][:], t_in["cT"][r * NJ + j]).then_inc(c_in[j], 16)
                sp.dma_start(cn[j][:], t_in["cn"][r * NJ + j]).then_inc(c_in[j], 16)
                sp.dma_start(lastq[j][:], t_in["lastq"][r * NJ + j]).then_inc(c_in[j], 16)
                sp.dma_start(lastk[j][:], t_in["lastk"][r * NJ + j].partition_broadcast(P)).then_inc(c_in[j], 16)

            def store(r):
                for j in J:
                    W(sp, x_new, r, NJ * (LNS - 2) + j + 1)
                    sp.dma_start(xres[r * NJ + j], x[j][:]).then_inc(x_saved[j], 16)
                for j in J:
                    W(sp, xn_ok, r, NJ * (LNS - 1) + j + 1)
                    sp.dma_start(xnorm[r * NJ + j], xn[j][:]).then_inc(n_saved[j], 16)

            for j in J:
                load_x(0, j)
            for j in J:
                load_context(0, j)
            sp.wait_ge(zero_ok, 1)
            n_rows = xrows.shape[0]
            sp.dma_start(xrows.rearrange("b p d -> p b d"), zero[:].broadcast_to([P, n_rows, D])).then_inc(zeroed, 16)
            sp.dma_start(yrows[n_rows - TOPK:n_rows].rearrange("b p d -> p b d"), zero[:].broadcast_to([P, TOPK, D])).then_inc(zeroed, 16)
            with sp.Fori(0, rounds - 1) as r:
                for j in J:
                    W(sp, x_new, r, j + 1)
                    load_x(r + 1, j)
                for j in J:
                    W(sp, om_ok, r, (j + 1) * NB)
                    load_context(r + 1, j)
                store(r)
            store(rounds - 1)
            sp.wait_ge(zeroed, 32)
            for j in J:
                sp.wait_ge(x_saved[j], 16 * rounds + 16)
                sp.wait_ge(n_saved[j], 16 * rounds + 16)

        @block.tensor
        def _(pe):
            pe.wait_ge(consts_loaded, 16 * len(CONSTS))
            pe.wait_ge(wload, 16 * NW)
            mm = nc.tensor.matmul
            for h in range(H):
                for k in range(H):
                    mm(ps[:, h, 0:D], setup_w["x0_Wq_T"][:, k, h * P:(h + 1) * P], setup_w["x0_Wk_T"][:, k, :], start=k == 0, stop=k == H - 1)
            for h in range(H):
                mm(ps[:, 2, h * P:(h + 1) * P], bd["x1_wq"][:, h, :], bd["x1_wk"][:, h, :], start=True, stop=True)
            for h in range(H):
                mm(ps[:, 3 + h, 0:D], bd["x1_wv"][:, h, :], setup_w["x1_woT"][:, h, :], start=True, stop=True)
            for h in range(H):
                for k in range(H):
                    mm(ps[:, 5, h:h + 1], setup_w["x0_Wk_T"][:, k, h * P:(h + 1) * P], cols["x0_bq"][:, k:k + 1], start=k == 0, stop=k == H - 1)
            for h in range(H):
                mm(ps[:, 5, 8 + h:9 + h], bd["x1_wk"][:, h, :], cols["x1_bq"][:, h:h + 1], start=True, stop=True)
            pe.wait_ge(su_cp, 1)
            for k in range(H):
                t = mm(ps[:, 6, 0:D], bv_rep[:, k, :], setup_w["x1_woT"][:, k, :], start=k == 0, stop=k == H - 1)
            t.then_inc(su_mm, 1)
            pe.wait_ge(su_q, 3)
            mm(ps[:, 7, 0:2], const["ones"][:], fw_abs[:], start=True, stop=True).then_inc(su_mm, 1)
            pe.wait_ge(su_q, SU_Q)
            pe.wait_ge(su_cp, SU_CP)

            def norm_T(r, u, b):
                for j in J:
                    W(pe, xn_ok, r, NJ * (u if u < 2 else u + 1) + j + 1)
                    for h in range(H):
                        t = nc.tensor.transpose(halves(bank(j, b))[:, h, :], xn[j][:, h * P:(h + 1) * P], ident[:])
                    t.then_inc(xnT_ps.handle, 1)

            def probs_T(r, n, b, parts, ready, at):
                for j in J:
                    W(pe, ready, r, at + j + 1)
                    if n > 0:
                        W(pe, v_ok, r, NJ * (n - 1) + j + 1)
                    for k in range(parts):
                        t = nc.tensor.transpose(halves(bank(j, b))[:, k, :], prob[j][:, k * P:(k + 1) * P], ident[:])
                    t.then_inc(pT_ps.handle, 1)

            def unit_scores(r, v):
                j, b = v // NB, v % NB
                for g in range(G):
                    lo = GD * (g % 2)
                    mm(ps[:, g, 0:KEYS], qblk[j][lo:lo + GD, g // 2, b, :, :].rearrange("p h q -> p (h q)"),
                       cT[j][lo:lo + GD, g // 2, b, :], start=True, stop=True).then_inc(s1_ps.handle, 1)

            def unit_probs_T(r, u):
                for g in range(G):
                    W(pe, e1_ok, r, G * u + g + 1)
                    for k in range(KT):
                        t = nc.tensor.transpose(ps[:, 4 + g // 2, ((g % 2) * KT + k) * P:((g % 2) * KT + k + 1) * P], p1[u % 2][:, g, k * P:(k + 1) * P], ident[:])
                    t.then_inc(t1_ps.handle, 1)

            def unit_values(r, u):
                j, b = u // NB, u % NB
                if u >= 1:
                    W(pe, o1_ok, r, u)
                for g in range(G):
                    if g % 2 == 0:
                        W(pe, t1_act if g == 0 else t1_dve, r, u + 1)
                    for k in range(KT):
                        t = mm(ps[:, 6, g * P:(g + 1) * P], p1T[u % 2][:, g, k, :], cn[j][:, b, k, g // 2 * P:(g // 2 + 1) * P], start=k == 0, stop=k == KT - 1)
                t.then_inc(v1_ps.handle, 1)

            def unit_fold(r, u):
                W(pe, om_ok, r, u + 1)
                if u >= 1:
                    W(pe, f1_ok, r, u)
                for h in range(H):
                    t = mm(ps[:, 7, h * S:(h + 1) * S], om[u % 2][:, 2 * h:2 * h + 2, :].rearrange("p g d -> p (g d)"), const["fold"][:], start=True, stop=True)
                t.then_inc(f1_ps.handle, 1)

            with pe.Fori(0, rounds) as r:
                norm_T(r, 0, 0)
                for j in J:
                    W(pe, xnT_ok, r, j + 1)
                    for h in range(H):
                        for k in range(H):
                            t = mm(halves(bank(j, 1))[:, h, :], x0_A[:, k, h * P:(h + 1) * P], xnT[j][:, k, :], start=k == 0, stop=k == H - 1)
                    t.then_inc(q_ps.handle, 1)
                for j in J:
                    W(pe, q_ok, r, j + 1)
                    pe.wait_ge(c_in[j], r * 64 + 64)
                    for b in range(NB):
                        for k in range(H):
                            t = mm(bank(j, 0)[b * S:(b + 1) * S, 0:KEYS], qT[j][:, k, b * S:(b + 1) * S], cT[j][:, k, b, :], start=k == 0, stop=k == H - 1)
                    t.then_inc(sc_ps.handle, 1)
                probs_T(r, 0, 1, KT, pr_ok, 0)
                for j in J:
                    W(pe, pT_ok, r, j + 1)
                    for b in range(NB):
                        for k in range(KT):
                            t = mm(bank(j, 0)[b * S:(b + 1) * S, 0:D], probT[j][:, k, b * S:(b + 1) * S], cn[j][:, b, k, :], start=k == 0, stop=k == KT - 1)
                    t.then_inc(pv_ps.handle, 1)
                for j in J:
                    W(pe, att_ok, r, j + 1)
                    for h in range(H):
                        t = nc.tensor.transpose(halves(bank(j, 1))[:, h, :], att[j][:, h * P:(h + 1) * P], ident[:])
                    t.then_inc(attT_ps.handle, 1)
                for j in J:
                    W(pe, attT_ok, r, j + 1)
                    for k in range(H):
                        t = mm(bank(j, 0)[:, 0:D], attT[j][:, k, :], full["x0_Wv"][:, k, :], start=k == 0, stop=k == H - 1)
                    t.then_inc(y_ps.handle, 1)
                norm_T(r, 1, 1)
                for j in J:
                    W(pe, xnT_ok, r, NJ + j + 1)
                    for n, wname in enumerate(("a0_Wq_T", "a0_Wk_T")):
                        for k in range(H):
                            t = mm(halves(bank(j, 0))[:, n, :], a0_qkv[wname][:, k, :], xnT[j][:, k, :], start=k == 0, stop=k == H - 1)
                    for k in range(H):
                        t = mm(bank(j, 1)[:, 0:HD], xnT[j][:, k, :], a0_qkv["a0_Wv_T"][:, k, :], start=k == 0, stop=k == H - 1)
                    t.then_inc(q_ps.handle, 1)
                for j in J:
                    W(pe, q_ok, r, NJ + j + 1)
                    W(pe, k_ok, r, j + 1)
                    mm(bank(j, 0)[:, 0:P], qT[j][:, 0, :], kT[j][:, 0, :], start=True, stop=True).then_inc(sc_ps.handle, 1)
                probs_T(r, 1, 1, 1, pn_ok, 0)
                for j in J:
                    W(pe, pT_ok, r, NJ + j + 1)
                    mm(bank(j, 0)[:, 0:P], val[j][:, 0:HD], probT[j][:, 0, :], start=True, stop=True).then_inc(pv_ps.handle, 1)
                for j in J:
                    W(pe, attT_ok, r, NJ + j + 1)
                    mm(bank(j, 1)[:, 0:D], attT[j][:, 0, :], a0_woT[:], start=True, stop=True).then_inc(y_ps.handle, 1)
                for j in J:
                    W(pe, qz_ok, r, j + 1)
                    dst = bank(j, 0).bitcast(BF16)
                    for h in range(H):
                        t = nc.tensor.transpose(dst[:, h * P:(h + 1) * P], xq[j][:, h * P:(h + 1) * P], identb[:])
                    t.then_inc(qT_ps.handle, 1)
                for j in J:
                    W(pe, qT_ok, r, j + 1)
                    for n in range(FF // 512):
                        for k in range(H):
                            t = mm(bank(j, n), xqT[j][:, k, :], fw[0][:, k, n * 512:(n + 1) * 512], start=k == 0, stop=k == H - 1)
                    t.then_inc(up_ps.handle, 1)
                for j in J:
                    W(pe, qz_ok, r, NJ + j + 1)
                    dst = bank(j, 0).bitcast(BF16)
                    for k in range(FK):
                        t = nc.tensor.transpose(dst[:, k * P:(k + 1) * P], hq[j][:, k * P:(k + 1) * P], identb[:])
                    t.then_inc(qT_ps.handle, 1)
                for j in J:
                    W(pe, qT_ok, r, NJ + j + 1)
                    for k in range(FK):
                        t = mm(bank(j, 1)[:, 0:D], hqT[j][:, k, :], fw[1][:, k, :], start=k == 0, stop=k == FK - 1)
                    t.then_inc(dn_ps.handle, 1)
                norm_T(r, 2, 0)
                for j in J:
                    W(pe, xnT_ok, r, 2 * NJ + j + 1)
                    mm(bank(j, 1)[:, 0:P], x1_B[:, 0, :], xnT[j][:, 0, :], start=True, stop=True)
                    mm(bank(j, 0)[:, 0:P], x1_B[:, 1, :], xnT[j][:, 1, :], start=True, stop=True).then_inc(q_ps.handle, 1)
                W(pe, qb_dve, r, NJ)
                W(pe, qb_act, r, NJ)
                for v in range(U + 2):
                    if 1 <= v <= U:
                        unit_probs_T(r, v - 1)
                    if v < U:
                        unit_scores(r, v)
                    if 1 <= v <= U:
                        unit_values(r, v - 1)
                    if v >= 2:
                        unit_fold(r, v - 2)
                for j in J:
                    W(pe, f1_ok, r, U)
                    for k in range(H):
                        t = mm(bank(j, 1)[:, 0:D], attT[j][:, k, :], x1_W[:, k, :], start=k == 0, stop=k == H - 1)
                    t.then_inc(y_ps.handle, 1)
                norm_T(r, 3, 0)
                for j in J:
                    W(pe, xnT_ok, r, 3 * NJ + j + 1)
                    for n, wname in enumerate(("a1_Wq", "a1_Wk")):
                        for h in range(H):
                            for k in range(H):
                                t = mm(bank(j, 1)[:, (n * H + h) * P:(n * H + h + 1) * P], full[wname][:, k, h * P:(h + 1) * P], xnT[j][:, k, :], start=k == 0, stop=k == H - 1)
                    for k in range(H):
                        t = mm(bank(j, 0)[:, 0:D], xnT[j][:, k, :], full["a1_Wv"][:, k, :], start=k == 0, stop=k == H - 1)
                    t.then_inc(q_ps.handle, 1)
                for j in J:
                    W(pe, q_ok, r, 2 * NJ + j + 1)
                    W(pe, k_ok, r, NJ + j + 1)
                    for k in range(H):
                        t = mm(bank(j, 1)[:, 0:P], qT[j][:, k, :], kT[j][:, k, :], start=k == 0, stop=k == H - 1)
                    t.then_inc(sc_ps.handle, 1)
                probs_T(r, 2, 0, 1, pr_ok, 2 * NJ)
                for j in J:
                    W(pe, pT_ok, r, 2 * NJ + j + 1)
                    mm(bank(j, 1)[:, 0:D], probT[j][:, 0, :], val[j][:], start=True, stop=True).then_inc(pv_ps.handle, 1)
                norm_T(r, 4, 0)
                for j in J:
                    W(pe, xnT_ok, r, 4 * NJ + j + 1)
                    for k in range(H):
                        t = mm(bank(j, 1)[:, 0:EXP], xnT[j][:, k, :], router[:, k, :], start=k == 0, stop=k == H - 1)
                    t.then_inc(lg_ps.handle, 1)

        @block.scalar
        def _(act):
            A = nc.scalar.activation
            act.wait_ge(consts_loaded, 16 * len(CONSTS))
            act.wait_ge(wload, 16 * NW)
            act.wait_ge(su_cp, SU_CP)

            def norm_T(r, u, b):
                for j in J:
                    W(act, xnT_ps, r, NJ * u + j + 1)
                    A(xnT[j][:], halves(bank(j, b)), ACT.Copy).then_inc(xnT_ok.handle, 1)

            def softmax(r, n, width):
                for j in J:
                    W(act, nm_ok, r, NJ * n + j + 1)
                    src = bank(j, 0)[:, 0:width] if n == 0 else att[j][:, 0:width]
                    A(prob[j][:, 0:width], src, ACT.Exp, bias=nmax[j][:], accum_out=rsum[j][:]).then_inc(pr_ok.handle, 1)

            def probs_T(r, n, b, parts):
                for j in J:
                    W(act, pT_ps, r, NJ * n + j + 1)
                    A(probT[j][:, 0:parts, :], halves(bank(j, b))[:, 0:parts, :], ACT.Copy).then_inc(pT_ok.handle, 1)

            with act.Fori(0, rounds) as r:
                norm_T(r, 0, 0)
                for j in J:
                    W(act, q_ps, r, j + 1)
                    for h in range(H):
                        t = A(qT[j][:, h, :], halves(bank(j, 1))[:, h, :], ACT.Identity, bias=x0_c[:, h:h + 1])
                    t.then_inc(q_ok.handle, 1)
                softmax(r, 0, KEYS)
                probs_T(r, 0, 1, KT)
                for j in J:
                    W(act, attT_ps, r, j + 1)
                    A(attT[j][:], halves(bank(j, 1)), ACT.Copy).then_inc(attT_ok.handle, 1)
                norm_T(r, 1, 1)
                for j in J:
                    W(act, q_ps, r, NJ + j + 1)
                    A(qT[j][:, 0, :], halves(bank(j, 0))[:, 0, :], ACT.Identity, bias=a0_col["a0_bq"][:]).then_inc(q_ok.handle, 1)
                    A(kT[j][:, 0, :], halves(bank(j, 0))[:, 1, :], ACT.Identity, bias=a0_col["a0_bk"][:]).then_inc(k_ok.handle, 1)
                softmax(r, 1, P)
                probs_T(r, 1, 1, 1)
                for j in J:
                    W(act, pv_ps, r, NJ + j + 1)
                    A(attT[j][:, 0, :], bank(j, 0)[:, 0:P], ACT.Identity, bias=a0_col["a0_bv"][:]).then_inc(attT_ok.handle, 1)
                for j in J:
                    W(act, qT_ps, r, j + 1)
                    A(xqT[j][:].rearrange("p h t -> p (h t)"), bank(j, 0).bitcast(BF16)[:, 0:H * P], ACT.Copy).then_inc(qT_ok.handle, 1)
                for j in J:
                    W(act, up_ps, r, j + 1)
                    W(act, dq_ok, r, j + 1)
                    A(hid[j], ps[:, 2 * j:2 * j + 2, :].rearrange("p b f -> p (b f)"), ACT.Gelu, scale=dq[j][:, 0:1]).then_inc(hid_ok.handle, 1)
                for j in J:
                    W(act, qT_ps, r, NJ + j + 1)
                    A(hqT[j].rearrange("p k t -> p (k t)"), bank(j, 0).bitcast(BF16), ACT.Copy).then_inc(qT_ok.handle, 1)
                norm_T(r, 2, 0)
                for j in J:
                    W(act, q_ps, r, 2 * NJ + j + 1)
                    for n in range(HG):
                        t = A(qblk[j][:, 1, :, n, :], bank(j, 0)[:, 0:P].rearrange("p (b q) -> p b q", b=NB), ACT.Identity,
                              scale=const["head_of_dim"][:, n:n + 1], bias=x1_cm[:, n:n + 1])
                    t.then_inc(qb_act.handle, 1)
                for v in range(U + 1):
                    if v >= 1:
                        W(act, t1_ps, r, G * (v - 1) + 2)
                        A(p1T[(v - 1) % 2][:, 0:2].rearrange("p g k t -> p (g k t)"), ps[:, 4, :], ACT.Copy).then_inc(t1_act.handle, 1)
                    if v < U:
                        for g in range(G):
                            W(act, m1_ok, r, G * v + g + 1)
                            A(p1[v % 2][:, g, :], ps[:, g, 0:KEYS], ACT.Exp, bias=nmax1[v % 2][:, g:g + 1], accum_out=rsum1[v % 2][:, g:g + 1]).then_inc(e1_ok.handle, 1)
                norm_T(r, 3, 0)
                for j in J:
                    W(act, q_ps, r, 3 * NJ + j + 1)
                    for h in range(H):
                        t = A(qT[j][:, h, :], halves(bank(j, 1))[:, h, :], ACT.Identity, bias=cols["a1_bq"][:, h:h + 1])
                    t.then_inc(q_ok.handle, 1)
                    for h in range(H):
                        t = A(kT[j][:, h, :], bank(j, 1)[:, (H + h) * P:(H + h + 1) * P], ACT.Identity, bias=cols["a1_bk"][:, h:h + 1])
                    t.then_inc(k_ok.handle, 1)
                softmax(r, 2, P)
                probs_T(r, 2, 0, 1)
                norm_T(r, 4, 0)

        @block.gpsimd
        def _(pool):
            g_ = nc.gpsimd
            g_.memset(zero[:], 0.0).then_inc(zero_ok, 1)
            g_.memset(minus_half[:], -0.5).then_inc(half_set, 1)
            pool.wait_ge(half_set, 1)
            pool.wait_ge(wload, 16 * NW)
            pool.wait_ge(su_cp, SU_CP)

            def rstds(r, u):
                for j in J:
                    W(pool, ln_ve, r, NJ * u + j + 1)
                    g_.tensor_tensor(rstd[j][:], ve[j][:], minus_half[:], ALU.pow).then_inc(ln_rs.handle, 1)

            def plus_bias(r, n, name):
                for j in J:
                    W(pool, x_new, r, NJ * n + j + 1)
                    g_.tensor_tensor(xb[j][:], x[j][:], rows[name][:], ALU.add).then_inc(xb_ok.handle, 1)

            with pool.Fori(0, rounds) as r:
                for j in J:
                    pool.wait_ge(x_in[j], r * 16 + 16)
                    g_.tensor_tensor(xb[j][:], xin[j][:], rows["x0_bv"][:], ALU.add).then_inc(xb_ok.handle, 1)
                rstds(r, 0)
                plus_bias(r, 0, "a0_bo")
                rstds(r, 1)
                rstds(r, 2)
                plus_bias(r, 2, "x1_bo")
                rstds(r, 3)
                for u in range(U):
                    j, b = u // NB, u % NB
                    W(pool, e1_ok, r, G * u + G)
                    g_.tensor_tensor(lastv[u % 2][:], lastk[j][:, b, :].rearrange("p (g d) -> p g d", g=G),
                                     p1[u % 2][:, :, KEYS - 1:KEYS].broadcast_to([P, G, GD]), ALU.mult).then_inc(lv_ok.handle, 1)
                    W(pool, r1_ok, r, u + 1)
                    g_.tensor_tensor(select[u % 2][:], const["head_of_col"][:].rearrange("p (g d) -> p g d", g=G),
                                     rinv1[u % 2][:].unsqueeze(2).broadcast_to([P, G, GD]), ALU.mult).then_inc(sel_ok.handle, 1)
                plus_bias(r, 3, "a1_bv")
                rstds(r, 4)
                rstds(r, 5)

        @block.vector
        def _(dve):
            v_ = nc.vector
            dve.wait_ge(consts_loaded, 16 * len(CONSTS))
            dve.wait_ge(wload, 16 * NW)
            for h in range(H):
                t = v_.tensor_copy(bv_rep[:, h, :], cols["x1_bv"][:, h:h + 1].to_broadcast([P, P]))
            t.then_inc(su_cp, 1)
            v_.tensor_copy(identb[:], ident[:]).then_inc(su_q, 1)
            for n in (0, 1):
                v_.tensor_reduce(fw_abs[:, n:n + 1], fw_raw[n], AX, ALU.add, apply_absolute_value=True).then_inc(su_q, 1)
            dve.wait_ge(su_mm, 2)
            v_.tensor_scalar(fw_scale[:], ps[:, 7, 0:2], 1.0 / (D * FF), EPS, ALU.mult, ALU.max).then_inc(su_q, 1)
            dve.wait_ge(su_q, 4)
            v_.reciprocal(fw_inv[:], fw_scale[:]).then_inc(su_q, 1)
            dve.wait_ge(su_q, 5)
            for n in (0, 1):
                v_.tensor_scalar(fw_raw[n], fw_raw[n], fw_inv[:, n:n + 1], MAGIC, ALU.mult, ALU.add).then_inc(su_q, 1)
            dve.wait_ge(su_q, 7)
            for n in (0, 1):
                v_.tensor_scalar(fw_raw[n], fw_raw[n], MAGIC, 1.0, ALU.subtract, ALU.min).then_inc(su_q, 1)
            dve.wait_ge(su_q, 9)
            v_.tensor_scalar(fw[0][:].rearrange("p h f -> p (h f)"), fw_raw[0], -1.0, None, ALU.max).then_inc(su_q, 1)
            v_.tensor_scalar(fw[1][:].rearrange("p k d -> p (k d)"), fw_raw[1], -1.0, None, ALU.max).then_inc(su_q, 1)
            v_.tensor_copy(x0_A[:], ps[:, 0:2, 0:D]).then_inc(su_cp, 1)
            v_.tensor_copy(x1_B[:], halves(ps[:, 2, :])).then_inc(su_cp, 1)
            v_.tensor_copy(x1_W[:], ps[:, 3:5, 0:D]).then_inc(su_cp, 1)
            v_.tensor_copy(x0_c[:], ps[:, 5, 0:H]).then_inc(su_cp, 1)
            v_.tensor_copy(x1_c[:], ps[:, 5, 8:8 + H]).then_inc(su_cp, 1)
            v_.tensor_tensor(rows["x1_bo"][:], ps[:, 6, 0:D], rows["x1_bo"][:], ALU.add)
            v_.tensor_scalar(full["x0_Wv"][:], full["x0_Wv"][:], float(D) ** -0.5, None, ALU.mult)
            v_.tensor_scalar(rows["x0_bv"][:], rows["x0_bv"][:], float(D) ** -0.5, None, ALU.mult).then_inc(su_cp, 2)
            dve.wait_ge(su_cp, 8)
            v_.tensor_scalar(x1_cm[:], const["head_of_dim"][:], x1_c[:, 1:2], None, ALU.mult).then_inc(su_cp, 1)
            dve.wait_ge(su_cp, SU_CP)
            dve.wait_ge(su_q, SU_Q)
            for j in J:
                dve.sem_inc(x_saved[j], 16)
                dve.sem_inc(n_saved[j], 16)

            def norm(r, u):
                src = xin if u == 0 else x
                for j in J:
                    if u == 0:
                        dve.wait_ge(x_in[j], r * 16 + 16)
                        dve.wait_ge(n_saved[j], r * 16 + 16)
                    else:
                        W(dve, x_new, r, NJ * (u - 1) + j + 1)
                    v_.bn_stats(st6[j][:], src[j][:]).then_inc(ln_st.handle, 1)
                for j in J:
                    W(dve, ln_st, r, NJ * u + j + 1)
                    v_.memset(hold[:, j:j + 1], 0.0)
                    v_.bn_aggr(mv[j][:], st6[j][:]).then_inc(ln_mv.handle, 1)
                for j in J:
                    W(dve, ln_mv, r, NJ * u + j + 1)
                    v_.tensor_scalar(ve[j][:], mv[j][:, 1:2], EPS, None, ALU.add).then_inc(ln_ve.handle, 1)
                for j in J:
                    W(dve, ln_rs, r, NJ * u + j + 1)
                    v_.tensor_scalar(xn[j][:], src[j][:], mv[j][:, 0:1], rstd[j][:], ALU.subtract, ALU.mult).then_inc(xn_ok.handle, 1)

            def row_max(r, n, b, width, scale, mask):
                for j in J:
                    W(dve, sc_ps, r, NJ * n + j + 1)
                    if mask is None:
                        v_.tensor_reduce(nmax[j][:], bank(j, b)[:, 0:width], AX, ALU.max, negate=True).then_inc(nm_ok.handle, 1)
                    else:
                        v_.scalar_tensor_tensor(att[j][:, 0:width], bank(j, b)[:, 0:width], scale, mask[:], ALU.mult, ALU.add).then_inc(sc_m.handle, 1)
                if mask is not None:
                    for j in J:
                        W(dve, sc_m, r, NJ * (n - 1) + j + 1)
                        v_.tensor_reduce(nmax[j][:], att[j][:, 0:width], AX, ALU.max, negate=True).then_inc(nm_ok.handle, 1)

            def inverse_sum(r, n):
                for j in J:
                    W(dve, pr_ok, r, NJ * n + j + 1)
                    v_.reciprocal(rinv[j][:], rsum[j][:]).then_inc(ri_ok.handle, 1)

            def quantise(r, n, src, rounded, q):
                for j in J:
                    if n == 0:
                        W(dve, xn_ok, r, 2 * NJ + j + 1)
                    else:
                        W(dve, hid_ok, r, j + 1)
                    v_.tensor_reduce(am[j][:], ap(src[j]), AX, ALU.max, apply_absolute_value=True).then_inc(am_raw.handle, 1)
                for j in J:
                    W(dve, am_raw, r, NJ * n + j + 1)
                    v_.tensor_scalar(am[j][:], am[j][:], EPS, 1.0 / 127.0, ALU.max, ALU.mult).then_inc(am_ok.handle, 1)
                for j in J:
                    W(dve, am_ok, r, NJ * n + j + 1)
                    v_.reciprocal(qs[j][:], am[j][:]).then_inc(qs_ok.handle, 1)
                    v_.tensor_scalar(dq[j][:, n:n + 1], am[j][:], fw_scale[:, n:n + 1], None, ALU.mult).then_inc(dq_ok.handle, 1)
                for j in J:
                    W(dve, qs_ok, r, NJ * n + j + 1)
                    v_.tensor_scalar(ap(rounded[j]), ap(src[j]), qs[j][:], MAGIC, ALU.mult, ALU.add).then_inc(qr_ok.handle, 1)
                for j in J:
                    W(dve, qr_ok, r, NJ * n + j + 1)
                    v_.tensor_scalar(ap(q[j]), ap(rounded[j]), MAGIC, 127.0, ALU.subtract, ALU.min).then_inc(qz_ok.handle, 1)

            with dve.Fori(0, rounds) as r:
                norm(r, 0)
                row_max(r, 0, 0, KEYS, 1.0, None)
                inverse_sum(r, 0)
                for j in J:
                    W(dve, pv_ps, r, j + 1)
                    v_.scalar_tensor_tensor(att[j][:], lastq[j][:], prob[j][:, KEYS - 1:KEYS], bank(j, 0)[:, 0:D], ALU.mult, ALU.add).then_inc(att_ok.handle, 1)
                for j in J:
                    W(dve, y_ps, r, j + 1)
                    W(dve, ri_ok, r, j + 1)
                    W(dve, xb_ok, r, j + 1)
                    dve.wait_ge(x_saved[j], r * 16 + 16)
                    v_.scalar_tensor_tensor(x[j][:], bank(j, 0)[:, 0:D], rinv[j][:], xb[j][:], ALU.mult, ALU.add).then_inc(x_new.handle, 1)
                norm(r, 1)
                for j in J:
                    W(dve, q_ps, r, NJ + j + 1)
                    v_.tensor_copy(val[j][:, 0:HD], bank(j, 1)[:, 0:HD]).then_inc(v_ok.handle, 1)
                row_max(r, 1, 0, P, float(HD) ** -0.5, const["causal"])
                inverse_sum(r, 1)
                for j in J:
                    W(dve, ri_ok, r, NJ + j + 1)
                    v_.tensor_scalar(prob[j][:, 0:P], prob[j][:, 0:P], rinv[j][:], None, ALU.mult).then_inc(pn_ok.handle, 1)
                for j in J:
                    W(dve, y_ps, r, NJ + j + 1)
                    W(dve, xb_ok, r, NJ + j + 1)
                    v_.tensor_tensor(x[j][:], bank(j, 1)[:, 0:D], xb[j][:], ALU.add).then_inc(x_new.handle, 1)
                norm(r, 2)
                quantise(r, 0, xn, att, xq)
                quantise(r, 1, hid, hid, hq)
                for j in J:
                    W(dve, dn_ps, r, j + 1)
                    W(dve, dq_ok, r, NJ + j + 1)
                    v_.scalar_tensor_tensor(x[j][:], bank(j, 1)[:, 0:D], dq[j][:, 1:2], x[j][:], ALU.mult, ALU.add).then_inc(x_new.handle, 1)
                norm(r, 3)
                for j in J:
                    W(dve, q_ps, r, 2 * NJ + j + 1)
                    for n in range(HG):
                        t = v_.tensor_scalar(qblk[j][:, 0, :, n, :], bank(j, 1)[:, 0:P].rearrange("p (b q) -> p b q", b=NB),
                                             x1_c[:, 0:1], const["head_of_dim"][:, n:n + 1], ALU.add, ALU.mult)
                    t.then_inc(qb_dve.handle, 1)
                for v in range(U + 3):
                    if v >= 3:
                        u = v - 3
                        j, b = u // NB, u % NB
                        W(dve, f1_ps, r, u + 1)
                        v_.tensor_copy(attT[j][:, :, b * S:(b + 1) * S], ps[:, 7, 0:H * S].rearrange("p (h q) -> p h q", h=H)).then_inc(f1_ok.handle, 1)
                    if 1 <= v <= U:
                        u = v - 1
                        W(dve, e1_ok, r, G * u + G)
                        v_.reciprocal(rinv1[u % 2][:], rsum1[u % 2][:]).then_inc(r1_ok.handle, 1)
                        W(dve, t1_ps, r, G * u + G)
                        v_.tensor_copy(p1T[u % 2][:, 2:4].rearrange("p g k t -> p (g k t)"), ps[:, 5, :]).then_inc(t1_dve.handle, 1)
                    if 2 <= v <= U + 1:
                        u = v - 2
                        W(dve, v1_ps, r, u + 1)
                        W(dve, lv_ok, r, u + 1)
                        by_half = ps[:, 6, :].rearrange("p (h c) -> p h c", h=H)
                        for n, lo in ((0, 0), (1, P + GD)):
                            t = v_.tensor_tensor(om[u % 2][:, n::2, :], by_half[:, :, lo:lo + GD], lastv[u % 2][:, n::2, :], ALU.add)
                        t.then_inc(o1_ok.handle, 1)
                        W(dve, o1_ok, r, u + 1)
                        W(dve, sel_ok, r, u + 1)
                        v_.tensor_tensor(om[u % 2][:], om[u % 2][:], select[u % 2][:], ALU.mult).then_inc(om_ok.handle, 1)
                    if v < U:
                        for g in range(G):
                            W(dve, s1_ps, r, G * v + g + 1)
                            v_.tensor_reduce(nmax1[v % 2][:, g:g + 1], ps[:, g, 0:KEYS], AX, ALU.max, negate=True).then_inc(m1_ok.handle, 1)
                for j in J:
                    W(dve, y_ps, r, 2 * NJ + j + 1)
                    W(dve, xb_ok, r, 2 * NJ + j + 1)
                    v_.tensor_tensor(x[j][:], bank(j, 1)[:, 0:D], xb[j][:], ALU.add).then_inc(x_new.handle, 1)
                norm(r, 4)
                for j in J:
                    W(dve, q_ps, r, 3 * NJ + j + 1)
                    v_.tensor_copy(val[j][:], bank(j, 0)[:, 0:D]).then_inc(v_ok.handle, 1)
                row_max(r, 2, 1, P, float(D) ** -0.5, const["band"])
                inverse_sum(r, 2)
                for j in J:
                    W(dve, pv_ps, r, 2 * NJ + j + 1)
                    W(dve, ri_ok, r, 2 * NJ + j + 1)
                    W(dve, xb_ok, r, 3 * NJ + j + 1)
                    v_.scalar_tensor_tensor(x[j][:], bank(j, 1)[:, 0:D], rinv[j][:], xb[j][:], ALU.mult, ALU.add).then_inc(x_new.handle, 1)
                norm(r, 5)
                for j in J:
                    W(dve, lg_ps, r, j + 1)
                    v_.tensor_copy(logits[:, r * NJ + j, :], bank(j, 1)[:, 0:EXP]).then_inc(lg_ok.handle, 1)


def expert_phase(nc, t_in, const, logits, ps, xres, xnorm, xrows, yrows, out, pairs, cap, blocks, zero, sem, sig, sb):
    ident = const["ident"]
    T = pairs * 2
    w1 = sb("w1", [P, EXP, H, FF])
    w2 = sb("w2", [P, EXP, FK, D])
    hold = sb("rt_hold", [P, 2])
    prob = sb("rt_prob", [P, T, EXP])
    prob2 = sb("rt_prob2", [P, T, EXP])
    key = sb("rt_key", [P, T, EXP])
    hot = sb("rt_hot", [P, T, TOPK, EXP])
    best = sb("rt_best", [P, TOPK, T])
    tmp = sb("rt_tmp", [P, T])
    scan = [sb(f"rt_scan{n}", [P, T, TOPK * EXP]) for n in (0, 1)]
    pos = sb("rt_pos", [P, T, TOPK, EXP])
    kept = sb("rt_kept", [P, T, TOPK])
    gate = sb("gate", [P, T, TOPK])
    slotf = sb("rt_slotf", [P, T, TOPK])
    slot = sb("slot", [P, T, TOPK], U32)
    count = sb("rt_count", [P, EXP])
    first = sb("rt_first", [P, EXP])
    nb_i = sb("rt_blocks_i", [P, EXP], I32)
    nb = sb("rt_blocks", [P, EXP])
    upto = sb("rt_upto", [P, EXP + 1])
    ge = sb("rt_ge", [P, EXP])
    lt = sb("rt_lt", [P, EXP])
    tab = sb("rt_tab", [P, 1])
    tab_i = sb("block_expert", [1, P], I32)
    xs = [sb(f"xs{b}", [P, D]) for b in (0, 1)]
    ix = [sb(f"ix{b}", [P, TOPK], U32) for b in (0, 1)]
    xe = [sb(f"xe{b}", [P, D]) for b in (0, 1)]
    xeT = [sb(f"xeT{b}", [P, H, P]) for b in (0, 1)]
    he = [sb(f"he{b}", [P, FF]) for b in (0, 1)]
    heT = [sb(f"heT{b}", [P, FK, P]) for b in (0, 1)]
    ye = [sb(f"ye{b}", [P, D]) for b in (0, 1)]
    xo = [sb(f"xo{b}", [P, D]) for b in (0, 1)]
    yg = [[sb(f"yg{b}{k}", [P, D]) for k in range(TOPK)] for b in (0, 1)]

    w_in = sem("expert_weights_in")
    rt = sem("routing_step")
    rt_exp = sem("routing_exp")
    rt_pe = sem("routing_sums_in_psum")
    tab_ok = sem("block_table_ready")
    xs_in = [sem(f"norm_rows_in{b}") for b in (0, 1)]
    ix_ok = sig("slots_staged", 2)
    sent = [sem(f"rows_sent{b}") for b in (0, 1)]
    carried = sem("waits_carried")
    xe_in = [sem(f"block_in{b}") for b in (0, 1)]
    ye_out = [sem(f"block_out{b}") for b in (0, 1)]
    xeT_ps, xeT_ok, up_ps, he_ok = sig("block_xT_in_psum", 1), sig("block_xT_ready", 1), sig("block_up_in_psum", 2), sig("block_hidden", 2)
    heT_ps, heT_lo, heT_hi, y_ps, ye_ok = sig("block_hiddenT_in_psum", 2), sig("block_hiddenT_lo", 1), sig("block_hiddenT_hi", 1), sig("block_y_in_psum", 1), sig("block_y", 1)
    xo_in = [sem(f"residual_in{b}") for b in (0, 1)]
    yg_in = [sem(f"expert_rows_in{b}") for b in (0, 1)]
    ix2_ok, g_ok, xo_ok = sig("slots_staged_again", 2), sig("gated_first", 2), sig("output_ready", 2)
    out_saved = [sem(f"output_saved{b}") for b in (0, 1)]

    def W(eng, s, r, k):
        eng.wait_ge(s.handle, s.at(r, k))

    def skewed(eng, block_work):
        for u in (0, 1):
            block_work(u, u, first=u == 0)
        with eng.Fori(1, blocks // 2 - 1) as i:
            for b in (0, 1):
                block_work(i * 2 + b, b)
        for u in (blocks - 2, blocks - 1):
            block_work(u, u % 2, last=u == blocks - 1)

    R_LOGIT, R_HOT, R_KEPT, R_TAB = {}, {}, {}, {}

    def routing(dve):
        v_ = nc.vector
        n = [0]

        def step(ins):
            n[0] += 1
            ins.then_inc(rt, 1)
            dve.wait_ge(rt, n[0])
            return n[0]

        def bc(ap, axis, size):
            shape = list(ap.shape)
            shape.insert(axis, size)
            return ap.unsqueeze(axis).broadcast_to(shape)

        step(v_.tensor_reduce(tmp[:], logits[:], AX, ALU.max))
        R_LOGIT[0] = step(v_.tensor_tensor(prob[:], logits[:], bc(tmp[:], 2, EXP), ALU.subtract))
        dve.wait_ge(rt_exp, 1)
        step(v_.tensor_reduce(tmp[:], prob[:], AX, ALU.add))
        step(v_.reciprocal(tmp[:], tmp[:]))
        step(v_.tensor_tensor(prob[:], prob[:], bc(tmp[:], 2, EXP), ALU.mult))
        src = prob
        for k in range(TOPK):
            step(v_.tensor_reduce(best[:, k, :], src[:], AX, ALU.max))
            step(v_.tensor_tensor(key[:], src[:], bc(best[:, k, :], 2, EXP), ALU.is_equal))
            step(v_.tensor_tensor(key[:], key[:], bc(const["rev8"][:], 1, T), ALU.mult))
            step(v_.tensor_reduce(tmp[:], key[:], AX, ALU.max))
            R_HOT[0] = step(v_.tensor_tensor(hot[:, :, k, :], key[:], bc(tmp[:], 2, EXP), ALU.is_equal))
            if k == 0:
                step(v_.scalar_tensor_tensor(prob2[:], hot[:, :, 0, :], -2.0, prob[:], ALU.mult, ALU.add))
                src = prob2
        step(v_.tensor_tensor(tmp[:], best[:, 0, :], best[:, 1, :], ALU.add))
        step(v_.reciprocal(tmp[:], tmp[:]))
        for k in range(TOPK):
            step(v_.tensor_tensor(gate[:, :, k], best[:, k, :], tmp[:], ALU.mult))

        def running(width, inside, totals):
            a, b = scan
            step(v_.tensor_copy(a[:, :, 0:width], totals))
            d = 1
            while d < T:
                step(v_.tensor_copy(b[:, 0:d, 0:width], a[:, 0:d, 0:width]))
                step(v_.tensor_tensor(b[:, d:T, 0:width], a[:, d:T, 0:width], a[:, 0:T - d, 0:width], ALU.add))
                a, b = b, a
                d *= 2
            step(v_.tensor_copy(b[:, :, 0:width], a[:, :, 0:width]))
            step(v_.tensor_tensor(b[:, :, 0:width], b[:, :, 0:width], totals, ALU.subtract))
            step(v_.tensor_tensor(b[:, :, 0:width], b[:, :, 0:width], inside, ALU.add))
            return a, b

        TE = TOPK * EXP
        dve.wait_ge(rt_pe, 1)
        _, where = running(TE, ps[:, 0, 0:T * TE].rearrange("p (t e) -> p t e", e=TE), ps[:, 1, 0:T * TE].rearrange("p (t e) -> p t e", e=TE))
        hot_f = hot[:].rearrange("p t k e -> p t (k e)")
        R_KEPT[0] = step(v_.scalar_tensor_tensor(hot_f, where[:, :, 0:TE], float(cap), hot_f, ALU.is_lt, ALU.mult))
        step(v_.tensor_reduce(kept[:], hot[:], AX, ALU.add))
        step(v_.tensor_tensor(gate[:], gate[:], kept[:], ALU.mult))
        R_KEPT[0] = step(v_.tensor_tensor(key[:], hot[:, :, 0, :], hot[:, :, 1, :], ALU.add))
        dve.wait_ge(rt_pe, 2)
        total, where = running(EXP, ps[:, 2, 0:T * EXP].rearrange("p (t e) -> p t e", e=EXP), ps[:, 3, 0:T * EXP].rearrange("p (t e) -> p t e", e=EXP))
        step(v_.tensor_copy(count[:], total[:, T - 1, 0:EXP]))
        step(v_.tensor_scalar(count[:], count[:], float(P - 1), None, ALU.add))
        step(v_.tensor_copy(nb_i[:], count[:]))
        step(v_.tensor_scalar(nb_i[:], nb_i[:], P.bit_length() - 1, None, ALU.arith_shift_right))
        step(v_.tensor_copy(nb[:], nb_i[:]))
        step(v_.memset(upto[:], 0.0))
        for e in range(EXP):
            step(v_.tensor_tensor(upto[:, e + 1:e + 2], upto[:, e:e + 1], nb[:, e:e + 1], ALU.add))
        step(v_.tensor_scalar(first[:], upto[:, 0:EXP], float(P), None, ALU.mult))
        step(v_.tensor_tensor(where[:, :, 0:EXP], where[:, :, 0:EXP], bc(first[:], 1, T), ALU.add))
        for k in range(TOPK):
            step(v_.tensor_tensor(pos[:, :, k, :], hot[:, :, k, :], where[:, :, 0:EXP], ALU.mult))
        step(v_.tensor_reduce(slotf[:], pos[:], AX, ALU.add))
        step(v_.tensor_scalar(kept[:], kept[:], -1.0, 1.0, ALU.mult, ALU.add))
        step(v_.tensor_tensor(kept[:], kept[:], bc(const["trash"][:], 1, T), ALU.mult))
        step(v_.tensor_tensor(slotf[:], slotf[:], kept[:], ALU.add))
        step(v_.tensor_copy(slot[:], slotf[:]))
        for b in (0, 1):
            v_.tensor_copy(ix[b][:], slot[:, b, :]).then_inc(ix_ok.handle, 1)
        step(v_.tensor_scalar(ge[:], upto[:, 0:EXP], const["row"][:], None, ALU.is_le))
        step(v_.tensor_scalar(lt[:], upto[:, 1:EXP + 1], const["row"][:], None, ALU.is_gt))
        step(v_.tensor_tensor(ge[:], ge[:], lt[:], ALU.mult))
        step(v_.tensor_tensor(lt[:], ge[:], const["eids"][:], ALU.mult))
        R_TAB[0] = step(v_.tensor_reduce(tab[:], lt[:], AX, ALU.add))
        dve.wait_ge(rt_pe, 3)
        v_.tensor_copy(tab_i[:], ps[0:1, 4, 0:P]).then_inc(tab_ok, 1)

    with nc.Block() as block:
        @block.vector
        def _(dve):
            v_ = nc.vector
            routing(dve)
            with dve.Fori(1, pairs) as i:
                for b in (0, 1):
                    dve.wait_ge(sent[b], i * 32)
                    v_.tensor_copy(ix[b][:], slot[:, i * 2 + b, :]).then_inc(ix_ok.handle, 1)
            def block_copies(u, b, first=False, last=False):
                if not last:
                    W(dve, xeT_ps, u + 1, 1)
                    v_.tensor_copy(xeT[1 - b][:].rearrange("p h t -> p (h t)"), ps[:, 5 - b, 0:D]).then_inc(xeT_ok.handle, 1)
                if not first:
                    down_copy(u - 1, 1 - b)
                W(dve, heT_ps, u, 2)
                v_.tensor_copy(heT[b][:, FK // 2:FK, :].rearrange("p k t -> p (k t)"), ps[:, 2 * b + 1, :]).then_inc(heT_hi.handle, 1)

            def down_copy(u, b):
                W(dve, y_ps, u, 1)
                dve.wait_ge(ye_out[b], (u - b) * 8 + 16)
                v_.tensor_copy(ye[b][:], ps[:, 6 + b, 0:D]).then_inc(ye_ok.handle, 1)

            W(dve, xeT_ps, 0, 1)
            v_.tensor_copy(xeT[0][:].rearrange("p h t -> p (h t)"), ps[:, 4, 0:D]).then_inc(xeT_ok.handle, 1)
            skewed(dve, block_copies)
            down_copy(blocks - 1, 1)

            def stage_slots(i, b):
                v_.tensor_copy(ix[b][:], slot[:, i * 2 + b, :]).then_inc(ix2_ok.handle, 1)

            def combine(i):
                for b in (0, 1):
                    dve.wait_ge(yg_in[b], i * 32 + 32)
                    dve.wait_ge(xo_in[b], i * 16 + 16)
                    v_.scalar_tensor_tensor(xo[b][:], yg[b][0][:], gate[:, i * 2 + b, 0:1], xo[b][:], ALU.mult, ALU.add).then_inc(g_ok.handle, 1)
                for b in (0, 1):
                    W(dve, g_ok, i, b + 1)
                    v_.scalar_tensor_tensor(xo[b][:], yg[b][1][:], gate[:, i * 2 + b, 1:2], xo[b][:], ALU.mult, ALU.add).then_inc(xo_ok.handle, 1)

            for b in (0, 1):
                stage_slots(0, b)
            with dve.Fori(0, pairs - 1) as i:
                combine(i)
                for b in (0, 1):
                    stage_slots(i + 1, b)
            combine(pairs - 1)

        @block.tensor
        def _(pe):
            mm = nc.tensor.matmul
            TE = TOPK * EXP
            for src, s, width, at in ((hot[:].rearrange("p t k e -> p (t k e)"), R_HOT, T * TE, 0), (key[:].rearrange("p t e -> p (t e)"), R_KEPT, T * EXP, 2)):
                pe.wait_ge(rt, s[0] if s is R_KEPT else R_HOT[0])
                mm(ps[:, at, 0:width], const["before"][:], src, start=True, stop=True)
                mm(ps[:, at + 1, 0:width], const["ones"][:], src, start=True, stop=True).then_inc(rt_pe, 1)
            pe.wait_ge(rt, R_TAB[0])
            mm(ps[0:1, 4, 0:P], tab[:], ident[:], start=True, stop=True).then_inc(rt_pe, 1)
            pe.wait_ge(tab_ok, 1)
            pe.wait_ge(w_in, 2 * EXP * 16)

            def rows_T(u, b):
                pe.wait_ge(xe_in[b], (u - b) * 8 + 16)
                for h in range(H):
                    t = nc.tensor.transpose(ps[:, 4 + b, h * P:(h + 1) * P], xe[b][:, h * P:(h + 1) * P], ident[:])
                t.then_inc(xeT_ps.handle, 1)

            def down(u, b, e):
                W(pe, heT_lo, u, 1)
                W(pe, heT_hi, u, 1)
                for k in range(FK):
                    t = mm(ps[:, 6 + b, 0:D], heT[b][:, k, :], w2[:, e, k, :], start=k == 0, stop=k == FK - 1)
                t.then_inc(y_ps.handle, 1)

            def expert(u):
                return pe.value_load(tab_i[0:1, bass.ds(u, 1)], min_val=0, max_val=EXP - 1)

            def block_products(u, b, first=False, last=False):
                e = expert(u)
                W(pe, xeT_ok, u, 1)
                for n in range(2):
                    for k in range(H):
                        t = mm(ps[:, 2 * b + n, :], xeT[b][:, k, :], w1[:, e, k, n * 512:(n + 1) * 512], start=k == 0, stop=k == H - 1)
                    t.then_inc(up_ps.handle, 1)
                if not last:
                    rows_T(u + 1, 1 - b)
                if not first:
                    down(u - 1, 1 - b, expert(u - 1))
                for n in range(2):
                    W(pe, he_ok, u, n + 1)
                    for k in range(FK // 2):
                        f = n * FK // 2 + k
                        t = nc.tensor.transpose(ps[:, 2 * b + n, k * P:(k + 1) * P], he[b][:, f * P:(f + 1) * P], ident[:])
                    t.then_inc(heT_ps.handle, 1)

            rows_T(0, 0)
            skewed(pe, block_products)
            down(blocks - 1, 1, expert(blocks - 1))

        @block.scalar
        def _(act):
            A = nc.scalar.activation
            act.wait_ge(rt, R_LOGIT[0])
            A(prob[:], prob[:], ACT.Exp).then_inc(rt_exp, 1)

            def block_gelu(u, b, first=False, last=False):
                for n in range(2):
                    W(act, up_ps, u, n + 1)
                    A(he[b][:, n * 512:(n + 1) * 512], ps[:, 2 * b + n, :], ACT.Gelu).then_inc(he_ok.handle, 1)
                W(act, heT_ps, u, 1)
                A(heT[b][:, 0:FK // 2, :].rearrange("p k t -> p (k t)"), ps[:, 2 * b, :], ACT.Copy).then_inc(heT_lo.handle, 1)

            skewed(act, block_gelu)

        @block.gpsimd
        def _(pool):
            g = nc.gpsimd
            pool.sem_inc(carried, 1)
            x_flat, y_flat = xrows.rearrange("b p d -> (b p) d"), yrows.rearrange("b p d -> (b p) d")
            with pool.Fori(0, pairs) as i:
                for b in (0, 1):
                    pool.wait_ge(xs_in[b], i * 16 + 16)
                    W(pool, ix_ok, i, b + 1)
                    pool.wait_ge(carried, i * 2 + b + 1)
                    g.tensor_tensor(hold[:, 0:1], zero[:, 0, 0:1], zero[:, 0, 0:1], ALU.add).then_inc(carried, 1)
                    for k in range(TOPK):
                        g.indirect_dma_start(x_flat, bass.IndirectOffsetOnAxis(ap=ix[b][:, k:k + 1], axis=0), xs[b][:], None).then_inc(sent[b], 16)
            with pool.Fori(0, pairs) as i:
                for b in (0, 1):
                    for q in (0, 1):
                        pool.wait_ge(ye_out[q], 16 * (blocks // 2) + 16)
                    W(pool, ix2_ok, i, b + 1)
                    pool.wait_ge(carried, pairs * 2 + i * 2 + b + 1)
                    g.tensor_tensor(hold[:, 0:1], zero[:, 0, 0:1], zero[:, 0, 0:1], ALU.add).then_inc(carried, 1)
                    for k in range(TOPK):
                        g.indirect_dma_start(yg[b][k][:], None, y_flat, bass.IndirectOffsetOnAxis(ap=ix[b][:, k:k + 1], axis=0)).then_inc(yg_in[b], 16)

        @block.sync
        def _(sp):
            for b in (0, 1):
                sp.sem_inc(ye_out[b], 16)
                sp.sem_inc(out_saved[b], 16)
            for e in range(EXP):
                sp.dma_start(w1[:, e], t_in["m_w1"][e]).then_inc(w_in, 16)
                sp.dma_start(w2[:, e], t_in["m_w2"][e]).then_inc(w_in, 16)
            for b in (0, 1):
                sp.dma_start(xs[b][:], xnorm[b]).then_inc(xs_in[b], 16)
            with sp.Fori(1, pairs) as i:
                for b in (0, 1):
                    sp.wait_ge(sent[b], i * 32)
                    sp.dma_start(xs[b][:], xnorm[i * 2 + b]).then_inc(xs_in[b], 16)
            for b in (0, 1):
                sp.wait_ge(sent[b], pairs * 32)

            def load_block(u, b):
                sp.dma_start(xe[b][:], xrows[u]).then_inc(xe_in[b], 16)

            def store_block(u, b):
                W(sp, ye_ok, u, 1)
                sp.dma_start(yrows[u], ye[b][:]).then_inc(ye_out[b], 16)

            def block_transfers(u, b, first=False, last=False):
                if not first:
                    store_block(u - 1, 1 - b)
                if not last:
                    W(sp, xeT_ps, u + 1, 1)
                    load_block(u + 3, 1 - b)

            load_block(0, 0)
            load_block(1, 1)
            W(sp, xeT_ps, 0, 1)
            load_block(2, 0)
            block_transfers(0, 0, first=True)
            with sp.Fori(0, (blocks - 4) // 2) as i:
                for b in (0, 1):
                    block_transfers(i * 2 + b + 1, 1 - b)
            for u in range(blocks - 3, blocks):
                block_transfers(u, u % 2, last=True)
            store_block(blocks - 1, 1)
            with sp.Fori(0, pairs) as i:
                for b in (0, 1):
                    sp.wait_ge(out_saved[b], i * 16 + 16)
                    sp.dma_start(xo[b][:], xres[i * 2 + b]).then_inc(xo_in[b], 16)
                for b in (0, 1):
                    W(sp, xo_ok, i, b + 1)
                    sp.dma_start(out[i * 2 + b], xo[b][:]).then_inc(out_saved[b], 16)
            for b in (0, 1):
                sp.wait_ge(out_saved[b], pairs * 16 + 16)


def shape_constants(np, blocks):
    f = np.float32
    p = np.arange(P)
    same = p[:, None] // S == p[None, :] // S
    c = {}
    c["ident"] = np.eye(P, dtype=f)
    c["causal"] = np.where(same & (p[None, :] <= p[:, None]), 0.0, MASKED).astype(f)
    c["band"] = np.where(same & (abs(p[None, :] - p[:, None]) <= 2), 0.0, MASKED).astype(f)
    col = np.arange(D)
    c["head_of_col"] = (p[:, None] // S == (col[None, :] % GD) // DH).astype(f)
    c["head_of_dim"] = (((p % GD) // DH)[:, None] == np.arange(HG)[None, :]).astype(f) * f(DH ** -0.5)
    c["fold"] = (p[:, None] % S == np.arange(S)[None, :]).astype(f)
    c["before"] = (p[:, None] < p[None, :]).astype(f)
    c["ones"] = np.ones((P, P), f)
    c["rev8"] = np.broadcast_to((EXP - np.arange(EXP)).astype(f), (P, EXP))
    c["trash"] = (blocks * P + np.arange(TOPK)[None, :] * P + p[:, None]).astype(f)
    c["row"] = p[:, None].astype(f)
    c["eids"] = np.broadcast_to(np.arange(EXP).astype(f), (P, EXP))
    return {"c_" + n: np.ascontiguousarray(a) for n, a in c.items()}


def lay_out(np, v):
    a = {n: np.asarray(x) for n, x in v.items()}
    B = a["x"].shape[0]
    tiles = B // NB
    tokens = B * S
    d = shape_constants(np, tokens * TOPK // P + EXP)
    d["x"] = a["x"].reshape(tiles, P, D)
    ctx = a["ctx_1024"].reshape(tiles, NB, KEYS, D)
    d["cn"] = ctx[:, :, :KEYS - 1].reshape(tiles, NB, KT, P, D).transpose(0, 3, 1, 2, 4)
    d["cT"] = ctx.reshape(tiles, NB, KEYS, H, P).transpose(0, 4, 3, 1, 2)
    d["lastk"] = ctx[:, :, KEYS - 1]
    d["lastq"] = np.repeat(d["lastk"], S, axis=1)
    d["x0_Wq_T"], d["x0_Wk_T"], d["x0_Wv"] = a["L0_xattn_Wq"].T, a["L0_xattn_Wk"].T, a["L0_xattn_Wv"]
    d["x1_woT"] = a["L1_xattn_wo"].T
    for n in ("Wq", "Wk", "Wv"):
        d["a1_" + n] = a["L1_attn_" + n]
        d[f"a0_{n}_T"] = a["L0_attn_" + n].T
    d["x0_bv"], d["a0_bo"], d["x1_bo"], d["a1_bv"] = a["L0_xattn_bv"], a["L0_attn_bo"], a["L1_xattn_bo"], a["L1_attn_bv"]

    def column(x):
        return x.reshape(H, P).T

    d["x0_bq"], d["a1_bq"], d["a1_bk"] = column(a["L0_xattn_bq"]), column(a["L1_attn_bq"]), column(a["L1_attn_bk"])
    d["x1_bq"], d["x1_bv"] = column(a["L1_xattn_bq"].reshape(-1)), column(a["L1_xattn_bv"].reshape(-1))
    d["a0_woT"] = a["L0_attn_Wo"].T
    for n in ("bq", "bk", "bv"):
        d["a0_" + n] = a["L0_attn_" + n].reshape(P, 1)
    for n in ("wq", "wk", "wv"):
        w = np.zeros((P, H, P), np.float32)
        for h in range(HEADS):
            lo = h * DH % P
            w[lo:lo + DH, h * DH // P, lo:lo + DH] = a["L1_xattn_" + n][h]
        d["x1_" + n] = w
    d["router"] = a["L1_ffn_router_w"].T
    d["f1"], d["f2"] = a["L0_ffn_w1"].T, a["L0_ffn_w2"].T
    d["m_w1"] = a["L1_ffn_w1"].reshape(EXP, H, P, FF).transpose(0, 2, 1, 3)
    d["m_w2"] = a["L1_ffn_w2"].reshape(EXP, FK, P, D).transpose(0, 2, 1, 3)
    return {n: np.ascontiguousarray(x) for n, x in d.items()}


def kernel(**inputs):
    import numpy as _np
    import concourse.bacc as _bacc
    from concourse import mybir as _mybir
    from concourse.bass_utils import run_bass_kernel_spmd as _run

    arrays = lay_out(_np, inputs)
    nc = _bacc.Bacc("TRN2", target_bir_lowering=False, num_devices=1)
    handles = {n: nc.dram_tensor("in_" + n, a.shape, _mybir.dt.from_np(a.dtype), kind="ExternalInput").ap() for n, a in arrays.items()}
    shape = arrays["x"].shape
    out = nc.dram_tensor("out_0", shape, F32, kind="ExternalOutput").ap()
    build(nc, handles, out)
    r = _run(nc, [{"in_" + n: a for n, a in arrays.items()}], core_ids=[0])
    return r.results[0]["out_0"].reshape(inputs["x"].shape)
```

```python
from contextlib import ExitStack

import numpy as np

import concourse.bass as bass
from concourse import mybir

F32 = mybir.dt.float32
BF16 = mybir.dt.bfloat16
U32 = mybir.dt.uint32
I32 = mybir.dt.int32
ALU = mybir.AluOpType
ACT = mybir.ActivationFunctionType
AX = mybir.AxisListType.X

P = 128
S = 32
NB = P // S
D = 256
H = D // P
KEYS = 257
KT = (KEYS - 1) // P
HD = 128
HEADS = 16
DH = D // HEADS
G = 4
HG = HEADS // G
GD = HG * DH
FF = 1024
FK = FF // P
EXP = 8
TOPK = 2
EPS = 1e-5
MAGIC = 1.5 * 2.0 ** 23
MASKED = -1e30

WIDTH = {"ident": P, "causal": P, "band": P, "head_of_col": D, "head_of_dim": HG, "fold": S, "before": P,
         "ones": P, "rev8": EXP, "row": 1, "row_1": 1, "eids": EXP, "cols": P}
FULL = ["x0_Wv", "a1_Wq", "a1_Wk", "a1_Wv"]
SETUP = ["x0_Wq_T", "x0_Wk_T", "x1_woT"]
ROWS = ["x0_bv", "a0_bo", "x1_bo", "a1_bv"]
COLS = ["x0_bq", "x1_bq", "x1_bv", "a1_bq", "a1_bk"]


class Signal:

    def __init__(self, handle, per):
        self.handle, self.per = handle, per

    def at(self, r, k):
        return r * self.per + k


def most_blocks(tokens):
    return (tokens * TOPK + EXP * (P - 1)) // P


def build(nc, t_in, out):
    tiles = t_in["x"].shape[0]
    tokens = tiles * P
    cap = max(1, int(1.25 * tokens / EXP * TOPK))
    blocks = most_blocks(tokens)
    assert tiles % (2 * RING) == 0 and 8 <= blocks <= P

    xres = nc.dram_tensor("xres", [tiles, P, D], F32).ap()
    xnorm = nc.dram_tensor("xnorm", [tiles, P, D], F32).ap()
    yrows = nc.dram_tensor("yrows", [TOPK * tokens + blocks * P, D], F32).ap()

    top = ExitStack()
    with top:
        def sem(name, stack=top):
            return stack.enter_context(nc.semaphore(name))

        def sig(name, per):
            return Signal(sem(name), per)

        def sb_in(stack):
            return lambda name, shape, dt=F32: stack.enter_context(nc.sbuf_tensor(name, shape, dt))

        keep = sb_in(top)
        constants = keep("constants", [P, sum(WIDTH.values())])
        const, at = {}, 0
        for n, w in WIDTH.items():
            const[n] = constants[:, at:at + w]
            at += w
        ident = const["ident"]
        logits = keep("logits", [P, tiles, EXP])
        ps = top.enter_context(nc.psum_tensor("ps", [P, 8, 512], F32))
        zero = keep("zero", [P, 1, D])
        consts_loaded = sem("consts_loaded")

        main = ExitStack()
        with main:
            stack_phase(nc, t_in, const, logits, ps, constants, consts_loaded, zero, yrows, xres, xnorm, tiles, sem, sig, sb_in(main))
        moe = ExitStack()
        with moe:
            expert_phase(nc, t_in, const, logits, ps, xres, xnorm, yrows, out, tiles, cap, blocks,
                         sem, sig, sb_in(moe))


class Steps:

    def __init__(self, handle, names):
        self.handle, self.names = handle, names

    def at(self, tile, name):
        return tile * len(self.names) + self.names.index(name) + 1


class Number:

    def __init__(self, register, scale, offset):
        self.register, self.scale, self.offset = register, scale, offset

    def __add__(self, n):
        return Number(self.register, self.scale, self.offset + n)

    def __sub__(self, n):
        return self + -n

    def __mul__(self, n):
        return Number(self.register, self.scale * n, self.offset * n)


def known(n):
    return n.register * n.scale + n.offset if isinstance(n, Number) else n


PARTS = {"cross0": 3, "self0": 2, "ffn": 1, "self1": -1}
HALVES = 2 * NB
RING = 4


def stack_phase(nc, t_in, const, logits, ps, constants, consts_loaded, zero, yrows, xres, xnorm, tiles, sem, sig, sb):
    ident = const["ident"]
    full = {n: sb("w_" + n, [P, H, D]) for n in FULL}
    rows = {n: sb("r_" + n, [P, D]) for n in ROWS}
    cols = {n: sb("b_" + n, [P, H]) for n in COLS}
    a1_bqk = sb("a1_bqk", [P, 2 * H])
    a0_qkv = {n: sb("w_" + n, [P, H, HD]) for n in ("a0_Wq_T", "a0_Wk_T", "a0_Wv_T")}
    a0_woT = sb("a0_woT", [P, D])
    a0_col = {n: sb("b_" + n, [P, 1]) for n in ("a0_bq", "a0_bk", "a0_bv")}
    router = sb("router", [P, H, EXP])
    fw = [sb("f1", [P, H, FF], BF16), sb("f2", [P, FK, D], BF16)]
    fw_abs = sb("fw_abs", [P, 2])
    fw_scale = sb("fw_scale", [P, 2])
    fw_inv = sb("fw_inv", [P, 2])
    identb = sb("identb", [P, P], BF16)
    x0_A = sb("x0_A", [P, H, D])
    x0_c = sb("x0_c", [P, H])
    x1_B = sb("x1_B", [P, H, P])
    x1_c = sb("x1_c", [P, H])
    x1_W = sb("x1_W", [P, H, D])
    minus_half = sb("minus_half", [P, 1])

    xin = [sb(f"xin{m}", [P, D]) for m in range(RING)]
    lastq = [sb(f"lastq{m}", [P, D]) for m in range(RING)]
    CN, CT, LK = NB * KT * D, H * NB * KEYS, NB * D
    context = [sb(f"context{m}", [P, CN + CT + LK]) for m in range(RING)]
    cn = [c[:, 0:CN].rearrange("p (b k d) -> p b k d", b=NB, k=KT) for c in context]
    cT = [c[:, CN:CN + CT].rearrange("p (b h k) -> p b h k", b=NB, h=H) for c in context]
    lastk = [c[:, CN + CT:].rearrange("p (b d) -> p b d", b=NB) for c in context]
    fw_raw = [context[2][:, n * H * FF:(n + 1) * H * FF] for n in (0, 1)]
    setup_w = {n: context[3][:, i * H * D:(i + 1) * H * D].rearrange("p (h d) -> p h d", h=H) for i, n in enumerate(SETUP)}
    *bd_views, bv_rep = [context[3][:, 3 * H * D + i * H * P:3 * H * D + (i + 1) * H * P].rearrange("p (h d) -> p h d", h=H) for i in range(4)]
    bd = dict(zip(("x1_wq", "x1_wk", "x1_wv"), bd_views))

    def small(part, name, width=1):
        return sb(f"{part}_{name}", [P, width])

    LN_OF = ("cross0", "self0", "ffn_in", "query1", "self1", "router")
    st6 = {n: small(n, "stats", 6) for n in LN_OF}
    mv = {n: small(n, "moments", 2) for n in LN_OF}
    ve = {n: small(n, "var_eps") for n in LN_OF}
    rstd = {n: small(n, "rstd") for n in LN_OF}
    hold = {n: small(n, "hold") for n in LN_OF}
    xn = {n: small(n, "norm", D) for n in LN_OF[:-1]}
    xnT = {n: sb(f"{n}_normT", [P, H, P]) for n in LN_OF if n != "ffn_in"}
    ATT = ("cross0", "self0", "self1")
    qT = {n: sb(f"{n}_qT", [P, H, P]) for n in ("cross0", "self0", "query1")}
    kT = sb("self0_kT", [P, H, P])
    qkT = sb("self1_qkT", [P, 2 * H, P])
    val = {n: small(n, "val", D) for n in ATT[1:]}
    masked = {n: small(n, "masked", P) for n in ATT[1:]}
    nmax = {n: small(n, "nmax") for n in ATT}
    rsum = {n: small(n, "rsum") for n in ATT}
    rinv = {n: small(n, "rinv") for n in ATT}
    prob = {n: small(n, "prob", KEYS if n == "cross0" else P) for n in ATT}
    probT = {n: sb(f"{n}_probT", [P, KT if n == "cross0" else 1, P]) for n in ATT}
    att = small("cross0", "att", D)
    attT = {n: sb(f"{n}_attT", [P, H, P]) for n in ATT[:2]}
    am, qs, dq = small("ffn", "absmax", 2), small("ffn", "qscale", 2), small("ffn", "dequant", 2)
    xr = small("ffn", "rounded", D)
    xq, xqT = sb("ffn_xq", [P, D], BF16), sb("ffn_xqT", [P, H, P], BF16)
    hid = small("ffn", "hidden", FF)
    hq, hqT = sb("ffn_hq", [P, FF], BF16), sb("ffn_hqT", [P, FK, P], BF16)
    x1, x2, xb3, x5, xn5 = [[sb(f"{n}_{q}", [P, D]) for q in (0, 1)] for n in ("x1", "x2", "x3_bias", "x5", "x5_norm")]
    x3, x4 = sb("x3", [P, D]), sb("x4", [P, D])
    xb = {n: small(n, "x_bias", D) for n in ATT}
    qblk = [sb(f"query_blocks{q}", [P, H, NB, HG, S]) for q in (0, 1)]
    outT = [sb(f"x1_outT{q}", [P, H, P]) for q in (0, 1)]
    nmax1, rsum1, rinv1 = [[sb(f"{n}{q}", [P, 2]) for q in (0, 1)] for n in ("x1_nmax", "x1_rsum", "x1_rinv")]
    p1 = [sb(f"x1_prob{q}", [P, 2, KEYS]) for q in (0, 1)]
    p1T = [sb(f"x1_probT{q}", [P, 2, KT, P]) for q in (0, 1)]
    lastv = [sb(f"x1_lastv{q}", [P, 2, GD]) for q in (0, 1)]
    select = [sb(f"x1_select{q}", [P, 2, GD]) for q in (0, 1)]
    om = [sb(f"x1_own{h}", [P, 2, GD]) for h in (0, 1)]

    wload = sem("weights_loaded")
    fw_in, setup_in = sem("feed_forward_weights_loaded"), sem("setup_weights_loaded")
    NS = len(SETUP) + len(COLS) + 3
    NW = len(FULL) + len(ROWS) + 3 + 1 + 3 + 1
    su_mm, su_cp = sem("setup_product"), sem("setup_copied")
    SU_CP, SU_Q = 8, 11
    su_q = sem("weights_quantised_step")
    half_set = sem("minus_half_set")
    zero_ok, zeroed = sem("zero_rows"), sem("rows_zeroed")
    x_in = [sem(f"x_in{m}") for m in range(RING)]
    c_in = [sem(f"context_in{m}") for m in range(RING)]
    x_saved, n_saved = [sem(f"x_saved{q}") for q in (0, 1)], [sem(f"norm_saved{q}") for q in (0, 1)]
    LN = ["stats", "moments", "var"]
    QUANT = ["absmax", "clip", "qscale", "dequant", "rounded", "quant"]
    pe_s = {n: Steps(sem("tensor_" + n), v) for n, v in {
        "cross0": ["normT", "q", "scores", "probsT", "values", "attT", "out"],
        "self0": ["normT", "qkv", "scores", "probsT", "values", "out"],
        "ffn_in": ["inT"],
        "ffn": ["up", "hiddenT", "down"],
        "query1": ["normT", "q"],
        "self1": ["out", "normT", "qk", "v_scores", "probsT", "values"],
        "router": ["normT", "logits"]}.items()}
    act_s = {n: Steps(sem("scalar_" + n), v) for n, v in {
        "cross0": ["normT", "q", "probs", "probsT", "attT"],
        "self0": ["normT", "qkv", "probs", "probsT", "attT"],
        "ffn_in": ["inT"],
        "ffn": ["gelu", "hiddenT"],
        "query1": ["normT", "q"],
        "self1": ["normT", "v", "probs", "probsT"],
        "router": ["normT"]}.items()}
    dve_s = {n: Steps(sem("vector_" + n), v) for n, v in {
        "cross0": LN + ["norm", "max", "inv", "att", "x"],
        "self0": LN + ["norm", "masked", "max", "inv", "scaled", "x"],
        "ffn_in": LN + ["norm"] + QUANT,
        "ffn": QUANT + ["x"],
        "query1": LN + ["norm"],
        "self1": ["x"] + LN + ["norm", "qk", "masked", "max", "inv", "x5"],
        "router": LN + ["norm", "logits"]}.items()}
    pool_s = {n: Steps(sem("pool_" + n), v) for n, v in {
        "cross0": ["rstd", "x_bias"], "self0": ["rstd", "x_bias"], "ffn_in": ["rstd"], "query1": ["rstd", "x_bias", "blocks"],
        "self1": ["rstd", "x_bias"], "router": ["rstd"]}.items()}
    s1_ps, m1_ok, e1_ok = sig("x1_scores_in_psum", 2), sig("x1_row_max", 2), sig("x1_probs", 2)
    t1_ps, v1_ps = sig("x1_probsT_in_psum", 1), sig("x1_values_in_psum", 1)
    t1_first, t1_rest = sig("x1_first_probsT_ready", 1), sig("x1_probsT_ready", HALVES - 1)
    r1_ok, lv_ok, sel_ok = sig("x1_row_sum_inverted", 1), sig("x1_last_key_values", 1), sig("x1_selection", 1)
    o1_ok, om_ok = sig("x1_last_key_added", 1), sig("x1_own_columns", 1)
    f1_ps, f1_ok = sig("x1_folded_in_psum", 1), sig("x1_folded_ready", 1)
    B_T, B_V = 2, 3
    bank = {n: ps[:, 4 + i, :] for i, n in enumerate(PARTS)}
    bank["ffn_in"], bank["query1"], bank["router"] = bank["self0"], bank["ffn"], bank["self1"]

    def W(eng, s, r, k):
        eng.wait_ge(s.handle, known(s.at(r, k)))

    def wait_probs_T(eng, t, k):
        if k == 0:
            W(eng, t1_first, t, 1)
        else:
            W(eng, t1_rest, t, k)

    def halves(ap):
        return ap[:, 0:H * P].rearrange("p (h t) -> p h t", h=H)

    class Slot:

        def __init__(self, s, fixed, whole):
            self.s, self.fixed, self.whole = s, fixed, whole

        def tile(self, ahead):
            if not self.whole and not 0 <= self.s + ahead < tiles:
                return None
            return self.s + ahead, (self.fixed + ahead) % RING

        def half(self, k):
            got = self.tile(0 if k >= 0 else -1)
            if got is None:
                return None
            return got[0], got[1], k % HALVES, got[0] * HALVES + k % HALVES

        def steps(self, table, pos):
            for part, ahead in PARTS.items():
                if pos in table[part] and self.tile(ahead) is not None:
                    table[part][pos](*self.tile(ahead))

    def slots(eng, work):
        for s in range(-3, 1):
            work(Slot(s, s, False))
        with eng.Fori(0, (tiles - RING) // RING) as i:
            for c in range(RING):
                work(Slot(Number(i, RING, 1 + c), 1 + c, True))
        for s in range(tiles - RING + 1, tiles + 1):
            work(Slot(s, s, False))

    with nc.Block() as block:
        @block.sync
        def _(sp):
            sp.dma_start(constants[:], t_in["c_constants"]).then_inc(consts_loaded, 16)
            sp.dma_start(fw_raw[0].rearrange("p (h f) -> p h f", h=H), t_in["f1"].rearrange("(h p) f -> p h f", p=P)).then_inc(fw_in, 16)
            sp.dma_start(fw_raw[1].rearrange("p (k d) -> p k d", k=FK), t_in["f2"].rearrange("(k p) d -> p k d", p=P)).then_inc(fw_in, 16)
            for n, buf in setup_w.items():
                sp.dma_start(buf, t_in[n].rearrange("(h p) d -> p h d", p=P)).then_inc(setup_in, 16)
            for n, buf in bd.items():
                sp.dma_start(buf, t_in[n]).then_inc(setup_in, 16)
            for n in COLS:
                sp.dma_start(cols[n][:], t_in[n]).then_inc(setup_in, 16)
            for n, buf in full.items():
                sp.dma_start(buf[:], t_in[n].rearrange("(h p) d -> p h d", p=P)).then_inc(wload, 16)
            for n in ROWS:
                sp.dma_start(rows[n][:], t_in[n].partition_broadcast(P)).then_inc(wload, 16)
            for n, buf in a0_qkv.items():
                sp.dma_start(buf[:], t_in[n].rearrange("(h p) d -> p h d", p=P)).then_inc(wload, 16)
            sp.dma_start(a0_woT[:], t_in["a0_woT"]).then_inc(wload, 16)
            for n, buf in a0_col.items():
                sp.dma_start(buf[:], t_in[n]).then_inc(wload, 16)
            sp.dma_start(router[:], t_in["router"].rearrange("(h p) e -> p h e", p=P)).then_inc(wload, 16)

            def load_x(t, m):
                sp.dma_start(xin[m][:], t_in["x"][known(t)]).then_inc(x_in[m], 16)
                sp.dma_start(lastq[m][:], t_in["lastq"][known(t)]).then_inc(x_in[m], 16)

            def load_batch(t, m, b):
                sp.dma_start(cT[m][:, b], t_in["cT"][known(t), :, b]).then_inc(c_in[m], 16)
                sp.dma_start(cn[m][:, b], t_in["cn"][known(t), :, b]).then_inc(c_in[m], 16)
                sp.dma_start(lastk[m][:, b, :], t_in["lastk"][known(t), b].partition_broadcast(P)).then_inc(c_in[m], 16)

            def slot(sl):
                here, after, done = sl.tile(0), sl.tile(RING), sl.tile(-1)
                if done and sl.tile(RING - 1):
                    W(sp, om_ok, done[0] * HALVES, HALVES)
                    load_batch(*sl.tile(RING - 1), NB - 1)
                if here and after:
                    W(sp, dve_s["cross0"], here[0], "x")
                    load_x(*after)
                for b in range(NB):
                    if b == NB - 2 and done:
                        W(sp, dve_s["self1"], done[0], "x5")
                        sp.dma_start(xres[known(done[0])], x5[done[1] % 2][:]).then_inc(x_saved[done[1] % 2], 16)
                        W(sp, dve_s["router"], done[0], "norm")
                        sp.dma_start(xnorm[known(done[0])], xn5[done[1] % 2][:]).then_inc(n_saved[done[1] % 2], 16)
                    if b < NB - 1 and here and after:
                        W(sp, om_ok, here[0] * HALVES, 2 * b + 2)
                        load_batch(*after, b)

            for t in range(RING):
                if t == 2:
                    sp.wait_ge(su_cp, SU_CP)
                    sp.wait_ge(su_q, SU_Q)
                load_x(t, t)
                for b in range(NB):
                    load_batch(t, t, b)
            sp.wait_ge(zero_ok, 1)
            n_rows = TOPK * tiles
            sp.dma_start(yrows[0:n_rows * P, :].rearrange("(n p) d -> p n d", p=P), zero[:].broadcast_to([P, n_rows, D])).then_inc(zeroed, 16)
            slot(Slot(0, 0, False))
            loops = tiles // RING - 2
            if loops > 0:
                with sp.Fori(0, loops) as i:
                    for c in range(RING):
                        slot(Slot(Number(i, RING, 1 + c), 1 + c, True))
            for s in range(loops * RING + 1, tiles + 1):
                slot(Slot(s, s, False))
            sp.wait_ge(zeroed, 16)
            for q in (0, 1):
                sp.wait_ge(x_saved[q], 8 * tiles + 16)
                sp.wait_ge(n_saved[q], 8 * tiles + 16)

        @block.tensor
        def _(pe):
            mm = nc.tensor.matmul
            tr = nc.tensor.transpose
            pe.wait_ge(consts_loaded, 16)
            pe.wait_ge(su_q, 3)
            mm(ps[:, 7, 0:2], const["ones"][:], fw_abs[:], start=True, stop=True).then_inc(su_mm, 1)
            pe.wait_ge(setup_in, 16 * NS)
            for h in range(H):
                for k in range(H):
                    mm(ps[:, h, 0:D], setup_w["x0_Wq_T"][:, k, h * P:(h + 1) * P], setup_w["x0_Wk_T"][:, k, :], start=k == 0, stop=k == H - 1)
            for h in range(H):
                mm(ps[:, 2, h * P:(h + 1) * P], bd["x1_wq"][:, h, :], bd["x1_wk"][:, h, :], start=True, stop=True)
            for h in range(H):
                mm(ps[:, 3 + h, 0:D], bd["x1_wv"][:, h, :], setup_w["x1_woT"][:, h, :], start=True, stop=True)
            for h in range(H):
                for k in range(H):
                    mm(ps[:, 5, h:h + 1], setup_w["x0_Wk_T"][:, k, h * P:(h + 1) * P], cols["x0_bq"][:, k:k + 1], start=k == 0, stop=k == H - 1)
            for h in range(H):
                mm(ps[:, 5, 8 + h:9 + h], bd["x1_wk"][:, h, :], cols["x1_bq"][:, h:h + 1], start=True, stop=True)
            pe.wait_ge(su_cp, 1)
            for k in range(H):
                t = mm(ps[:, 6, 0:D], bv_rep[:, k, :], setup_w["x1_woT"][:, k, :], start=k == 0, stop=k == H - 1)
            t.then_inc(su_mm, 1)
            pe.wait_ge(su_q, SU_Q)
            pe.wait_ge(su_cp, SU_CP)
            pe.wait_ge(wload, 16 * NW)

            def product(out, pairs):
                for n, (a, b) in enumerate(pairs):
                    t = mm(out, a, b, start=n == 0, stop=n == len(pairs) - 1)
                return t

            def norm_T(part, at=0, src=None):
                def step(t, m):
                    W(pe, dve_s[part], t, "norm")
                    rows_ = (src or (lambda q: xn[part]))(m % 2)
                    for h in range(H):
                        i = tr(bank[part][:, at + h * P:at + (h + 1) * P], rows_[:, h * P:(h + 1) * P], ident[:])
                    i.then_inc(pe_s[part].handle, 1)
                return step

            def c0_q(t, m):
                W(pe, act_s["cross0"], t, "normT")
                for h in range(H):
                    i = product(bank["cross0"][:, D + h * P:D + (h + 1) * P], [(x0_A[:, k, h * P:(h + 1) * P], xnT["cross0"][:, k, :]) for k in range(H)])
                i.then_inc(pe_s["cross0"].handle, 1)

            def c0_scores(part):
                def step(t, m):
                    if part == 0:
                        W(pe, act_s["cross0"], t, "q")
                        pe.wait_ge(c_in[m], known((t - m) * (NB * 3 * 16 // RING) + NB * 3 * 16))
                    for b in range(part * NB // 2, (part + 1) * NB // 2):
                        i = product(bank["cross0"][b * S:(b + 1) * S, 0:KEYS], [(qT["cross0"][:, k, b * S:(b + 1) * S], cT[m][:, b, k, :]) for k in range(H)])
                    if part == 1:
                        i.then_inc(pe_s["cross0"].handle, 1)
                return step

            def c0_probsT(t, m):
                W(pe, act_s["cross0"], t, "probs")
                for k in range(KT):
                    i = tr(bank["cross0"][:, D + k * P:D + (k + 1) * P], prob["cross0"][:, k * P:(k + 1) * P], ident[:])
                i.then_inc(pe_s["cross0"].handle, 1)

            def c0_values(part):
                def step(t, m):
                    if part == 0:
                        W(pe, act_s["cross0"], t, "probsT")
                    for b in range(part * NB // 2, (part + 1) * NB // 2):
                        i = product(bank["cross0"][b * S:(b + 1) * S, 0:D], [(probT["cross0"][:, k, b * S:(b + 1) * S], cn[m][:, b, k, :]) for k in range(KT)])
                    if part == 1:
                        i.then_inc(pe_s["cross0"].handle, 1)
                return step

            def c0_attT(t, m):
                W(pe, dve_s["cross0"], t, "att")
                for h in range(H):
                    i = tr(bank["cross0"][:, D + h * P:D + (h + 1) * P], att[:, h * P:(h + 1) * P], ident[:])
                i.then_inc(pe_s["cross0"].handle, 1)

            def c0_out(t, m):
                W(pe, act_s["cross0"], t, "attT")
                product(bank["cross0"][:, 0:D], [(attT["cross0"][:, k, :], full["x0_Wv"][:, k, :]) for k in range(H)]).then_inc(pe_s["cross0"].handle, 1)

            def s0_qkv(t, m):
                W(pe, act_s["self0"], t, "normT")
                b = bank["self0"]
                for n, w in enumerate(("a0_Wq_T", "a0_Wk_T")):
                    product(b[:, n * P:(n + 1) * P], [(a0_qkv[w][:, k, :], xnT["self0"][:, k, :]) for k in range(H)])
                product(b[:, 2 * P:3 * P], [(xnT["self0"][:, k, :], a0_qkv["a0_Wv_T"][:, k, :]) for k in range(H)]).then_inc(pe_s["self0"].handle, 1)

            def s0_scores(t, m):
                W(pe, act_s["self0"], t, "qkv")
                mm(bank["self0"][:, 3 * P:4 * P], qT["self0"][:, 0, :], kT[:, 0, :], start=True, stop=True).then_inc(pe_s["self0"].handle, 1)

            def s0_probsT(t, m):
                W(pe, dve_s["self0"], t, "scaled")
                tr(bank["self0"][:, 0:P], prob["self0"][:], ident[:]).then_inc(pe_s["self0"].handle, 1)

            def s0_values(t, m):
                W(pe, act_s["self0"], t, "probsT")
                mm(bank["self0"][:, P:2 * P], val["self0"][:, 0:HD], probT["self0"][:, 0, :], start=True, stop=True).then_inc(pe_s["self0"].handle, 1)

            def s0_out(t, m):
                W(pe, act_s["self0"], t, "attT")
                mm(bank["self0"][:, D:2 * D], attT["self0"][:, 0, :], a0_woT[:], start=True, stop=True).then_inc(pe_s["self0"].handle, 1)

            def ff_inT(t, m):
                W(pe, dve_s["ffn_in"], t, "quant")
                dst = bank["ffn_in"].bitcast(BF16)
                for h in range(H):
                    i = tr(dst[:, h * P:(h + 1) * P], xq[:, h * P:(h + 1) * P], identb[:])
                i.then_inc(pe_s["ffn_in"].handle, 1)

            def ff_up(t, m):
                W(pe, act_s["ffn_in"], t, "inT")
                for n, b in enumerate((bank["ffn"], bank["self1"])):
                    i = product(b, [(xqT[:, k, :], fw[0][:, k, n * 512:(n + 1) * 512]) for k in range(H)])
                i.then_inc(pe_s["ffn"].handle, 1)

            def ff_bank_back(t, m):
                W(pe, act_s["ffn"], t, "gelu")

            def ff_hiddenT(t, m):
                W(pe, dve_s["ffn"], t, "quant")
                dst = bank["ffn"].bitcast(BF16)
                for k in range(FK):
                    i = tr(dst[:, k * P:(k + 1) * P], hq[:, k * P:(k + 1) * P], identb[:])
                i.then_inc(pe_s["ffn"].handle, 1)

            def ff_down(t, m):
                W(pe, act_s["ffn"], t, "hiddenT")
                product(bank["ffn"][:, 0:D], [(hqT[:, k, :], fw[1][:, k, :]) for k in range(FK)]).then_inc(pe_s["ffn"].handle, 1)

            def q1_q(t, m):
                W(pe, act_s["query1"], t, "normT")
                for h in range(H):
                    i = mm(bank["query1"][:, h * P:(h + 1) * P], x1_B[:, h, :], xnT["query1"][:, h, :], start=True, stop=True)
                i.then_inc(pe_s["query1"].handle, 1)

            def s1_out(t, m):
                W(pe, f1_ok, t * NB, NB)
                product(bank["self1"][:, 0:D], [(outT[m % 2][:, k, :], x1_W[:, k, :]) for k in range(H)]).then_inc(pe_s["self1"].handle, 1)

            def s1_qk(t, m):
                W(pe, act_s["self1"], t, "normT")
                for n, w in enumerate(("a1_Wq", "a1_Wk")):
                    for h in range(H):
                        i = product(bank["self1"][:, (n * H + h) * P:(n * H + h + 1) * P], [(full[w][:, k, h * P:(h + 1) * P], xnT["self1"][:, k, :]) for k in range(H)])
                i.then_inc(pe_s["self1"].handle, 1)

            def s1_v_scores(t, m):
                W(pe, dve_s["self1"], t, "qk")
                product(bank["self1"][:, 0:D], [(xnT["self1"][:, k, :], full["a1_Wv"][:, k, :]) for k in range(H)])
                product(bank["self1"][:, D:D + P], [(qkT[:, k, :], qkT[:, H + k, :]) for k in range(H)]).then_inc(pe_s["self1"].handle, 1)

            def s1_probsT(t, m):
                W(pe, act_s["self1"], t, "probs")
                tr(bank["self1"][:, D + P:D + 2 * P], prob["self1"][:], ident[:]).then_inc(pe_s["self1"].handle, 1)

            def s1_values(t, m):
                W(pe, act_s["self1"], t, "probsT")
                mm(bank["self1"][:, 0:D], probT["self1"][:, 0, :], val["self1"][:], start=True, stop=True).then_inc(pe_s["self1"].handle, 1)

            def ro_logits(t, m):
                W(pe, act_s["router"], t, "normT")
                product(bank["router"][:, 0:EXP], [(xnT["router"][:, k, :], router[:, k, :]) for k in range(H)]).then_inc(pe_s["router"].handle, 1)

            table = {
                "cross0": {3: norm_T("cross0"), 5: c0_q, 7: c0_scores(0), 8: c0_scores(1), 11: c0_probsT, 12: c0_values(0), 13: c0_values(1), 14: c0_attT, 15: c0_out},
                "self0": {3: norm_T("self0"), 4: s0_qkv, 5: s0_scores, 8: s0_probsT, 9: s0_values, 10: s0_out, 15: ff_inT},
                "ffn": {1: ff_up, 3: ff_bank_back, 7: ff_hiddenT, 8: ff_down, 11: norm_T("query1", D), 12: q1_q},
                "self1": {3: s1_out, 5: norm_T("self1"), 6: s1_qk, 7: s1_v_scores, 9: s1_probsT, 11: s1_values, 13: norm_T("router", D, lambda q: xn5[q]), 14: ro_logits}}

            def unit_probs_T(t, m, k, K, folded):
                if folded is not None:
                    W(pe, f1_ok, folded[0] * NB, folded[2] // 2 + 1)
                for g in (0, 1):
                    W(pe, e1_ok, K, g + 1)
                    for n in range(KT):
                        i = tr(ps[:, B_T, (g * KT + n) * P:(g * KT + n + 1) * P], p1[k % 2][:, g, n * P:(n + 1) * P], ident[:])
                i.then_inc(t1_ps.handle, 1)

            def unit_scores(t, m, k, K, g):
                if k == 0 and g == 0:
                    W(pe, pool_s["query1"], t, "blocks")
                mm(ps[:, g, 0:KEYS], qblk[m % 2][g * GD:(g + 1) * GD, k % 2, k // 2, :, :].rearrange("p h q -> p (h q)"),
                   cT[m][g * GD:(g + 1) * GD, k // 2, k % 2, :], start=True, stop=True).then_inc(s1_ps.handle, 1)

            def unit_fold(t, m, k, K, last):
                W(pe, om_ok, K, 1)
                wait_probs_T(pe, last[0], last[2])
                for h in (0, 1):
                    i = mm(ps[:, B_T, h * S:(h + 1) * S], om[h][:].rearrange("p g d -> p (g d)"), const["fold"][:], start=True, stop=True)
                i.then_inc(f1_ps.handle, 1)

            def unit_values(t, m, k, K):
                wait_probs_T(pe, t, k)
                for g in (0, 1):
                    i = product(ps[:, B_V, g * P:(g + 1) * P], [(p1T[k % 2][:, g, n, :], cn[m][:, k // 2, n, k % 2 * P:(k % 2 + 1) * P]) for n in range(KT)])
                i.then_inc(v1_ps.handle, 1)

            def slot(sl):
                for k in range(HALVES):
                    last, older, oldest = sl.half(k - 1), sl.half(k - 2), sl.half(k - 3)
                    if last:
                        unit_probs_T(*last, oldest if oldest and oldest[2] % 2 == 1 else None)
                    sl.steps(table, 2 * k)
                    if sl.half(k):
                        for g in (0, 1):
                            unit_scores(*sl.half(k), g)
                    if older and older[2] % 2 == 1:
                        unit_fold(*older, last or older)
                    sl.steps(table, 2 * k + 1)
                    if last:
                        if older:
                            W(pe, o1_ok, older[3], 1)
                        unit_values(*last)

            slots(pe, slot)

        @block.scalar
        def _(act):
            A = nc.scalar.activation
            act.wait_ge(consts_loaded, 16)
            act.wait_ge(setup_in, 16 * NS)
            act.wait_ge(wload, 16 * NW)
            act.wait_ge(su_cp, SU_CP)

            def norm_T(part, at=0):
                def step(t, m):
                    W(act, pe_s[part], t, "normT")
                    A(xnT[part][:], halves(bank[part][:, at:at + D]), ACT.Copy).then_inc(act_s[part].handle, 1)
                return step

            def softmax(part, src):
                def step(t, m):
                    W(act, dve_s[part], t, "max")
                    A(prob[part][:], src, ACT.Exp, bias=nmax[part][:], accum_out=rsum[part][:]).then_inc(act_s[part].handle, 1)
                return step

            def copy(part, wait, dst, src, bias=None):
                def step(t, m):
                    W(act, pe_s[part], t, wait)
                    if bias is None:
                        A(dst, src, ACT.Copy).then_inc(act_s[part].handle, 1)
                    else:
                        A(dst, src, ACT.Identity, bias=bias).then_inc(act_s[part].handle, 1)
                return step

            def biased_halves(part, wait, sets):
                def step(t, m):
                    W(act, pe_s[part], t, wait)
                    for dst, src, bias in sets:
                        for h in range(H):
                            i = A(dst[:, h, :], halves(src)[:, h, :], ACT.Identity, bias=bias[:, h:h + 1])
                    i.then_inc(act_s[part].handle, 1)
                return step

            def s0_qkv(t, m):
                W(act, pe_s["self0"], t, "qkv")
                b = bank["self0"]
                A(qT["self0"][:, 0, :], b[:, 0:P], ACT.Identity, bias=a0_col["a0_bq"][:])
                A(kT[:, 0, :], b[:, P:2 * P], ACT.Identity, bias=a0_col["a0_bk"][:])
                A(val["self0"][:, 0:HD], b[:, 2 * P:3 * P], ACT.Copy).then_inc(act_s["self0"].handle, 1)

            def gelu(t, m):
                W(act, pe_s["ffn"], t, "up")
                W(act, dve_s["ffn_in"], t, "dequant")
                for n, b in enumerate((bank["ffn"], bank["self1"])):
                    i = A(hid[:, n * 512:(n + 1) * 512], b, ACT.Gelu, scale=dq[:, 0:1])
                i.then_inc(act_s["ffn"].handle, 1)

            c0, s0, s1, ff = bank["cross0"], bank["self0"], bank["self1"], bank["ffn"]
            table = {
                "cross0": {4: norm_T("cross0"), 5: biased_halves("cross0", "q", [(qT["cross0"], c0[:, D:2 * D], x0_c)]), 10: softmax("cross0", c0[:, 0:KEYS]),
                           11: copy("cross0", "probsT", probT["cross0"][:], halves(c0[:, D:2 * D])), 14: copy("cross0", "attT", attT["cross0"][:], halves(c0[:, D:2 * D]))},
                "self0": {3: norm_T("self0"), 4: s0_qkv, 6: softmax("self0", masked["self0"][:]), 8: copy("self0", "probsT", probT["self0"][:, 0, :], s0[:, 0:P]),
                          9: copy("self0", "values", attT["self0"][:, 0, :], s0[:, P:2 * P], a0_col["a0_bv"][:]),
                          15: copy("ffn_in", "inT", xqT[:].rearrange("p h t -> p (h t)"), bank["ffn_in"].bitcast(BF16)[:, 0:H * P])},
                "ffn": {1: gelu, 7: copy("ffn", "hiddenT", hqT[:].rearrange("p k t -> p (k t)"), ff.bitcast(BF16)),
                        11: norm_T("query1", D), 12: biased_halves("query1", "q", [(qT["query1"], ff[:, 0:D], x1_c)])},
                "self1": {5: norm_T("self1"), 7: copy("self1", "v_scores", val["self1"][:], s1[:, 0:D]), 8: softmax("self1", masked["self1"][:]),
                          9: copy("self1", "probsT", probT["self1"][:, 0, :], s1[:, D + P:D + 2 * P]), 13: norm_T("router", D)}}

            def slot(sl):
                for k in range(HALVES):
                    if sl.half(k - 1) and k != 1:
                        t, m, kk, K = sl.half(k - 1)
                        W(act, t1_ps, K, 1)
                        A(p1T[kk % 2][:].rearrange("p g k t -> p (g k t)"), ps[:, B_T, :], ACT.Copy).then_inc(t1_rest.handle, 1)
                    sl.steps(table, 2 * k)
                    if sl.half(k):
                        t, m, kk, K = sl.half(k)
                        for g in (0, 1):
                            W(act, m1_ok, K, g + 1)
                            A(p1[kk % 2][:, g, :], ps[:, g, 0:KEYS], ACT.Exp, bias=nmax1[kk % 2][:, g:g + 1], accum_out=rsum1[kk % 2][:, g:g + 1]).then_inc(e1_ok.handle, 1)
                    sl.steps(table, 2 * k + 1)

            slots(act, slot)

        @block.gpsimd
        def _(pool):
            tt = nc.gpsimd.tensor_tensor
            nc.gpsimd.memset(zero[:], 0.0).then_inc(zero_ok, 1)
            nc.gpsimd.memset(minus_half[:], -0.5).then_inc(half_set, 1)
            pool.wait_ge(half_set, 1)
            pool.wait_ge(consts_loaded, 16)
            pool.wait_ge(setup_in, 16 * NS)
            pool.wait_ge(wload, 16 * NW)
            pool.wait_ge(su_cp, SU_CP)

            def inverse_std(part, t):
                W(pool, dve_s[part], t, "var")
                tt(rstd[part][:], ve[part][:], minus_half[:], ALU.pow).then_inc(pool_s[part].handle, 1)

            def plus_bias(part, t, dst, src, name):
                tt(dst[:], src[:], rows[name][:], ALU.add).then_inc(pool_s[part].handle, 1)

            def c0_norm(t, m):
                inverse_std("cross0", t)
                pool.wait_ge(x_in[m], known((t - m) * (32 // RING) + 32))
                plus_bias("cross0", t, xb["cross0"], xin[m], "x0_bv")

            def s0_norm(t, m):
                inverse_std("self0", t)
                W(pool, dve_s["cross0"], t, "x")
                plus_bias("self0", t, xb["self0"], x1[m % 2], "a0_bo")

            def ff_norm(t, m):
                inverse_std("ffn_in", t)

            def q1_norm(t, m):
                inverse_std("query1", t)
                W(pool, dve_s["ffn"], t, "x")
                plus_bias("query1", t, xb3[m % 2], x3, "x1_bo")

            def q1_blocks(t, m):
                W(pool, act_s["query1"], t, "q")
                for h in range(H):
                    i = tt(qblk[m % 2][:, h], qT["query1"][:, h, :].rearrange("p (b q) -> p b q", b=NB).unsqueeze(2).broadcast_to([P, NB, HG, S]),
                           const["head_of_dim"][:].unsqueeze(1).unsqueeze(3).broadcast_to([P, NB, HG, S]), ALU.mult)
                i.then_inc(pool_s["query1"].handle, 1)

            def s1_norm(t, m):
                inverse_std("self1", t)
                W(pool, dve_s["self1"], t, "x")
                plus_bias("self1", t, xb["self1"], x4, "a1_bv")

            def ro_norm(t, m):
                inverse_std("router", t)

            table = {"cross0": {1: c0_norm}, "self0": {1: s0_norm, 11: ff_norm}, "ffn": {9: q1_norm, 12: q1_blocks}, "self1": {3: s1_norm, 11: ro_norm}}

            def slot(sl):
                for k in range(HALVES):
                    if sl.half(k - 1):
                        t, m, kk, K = sl.half(k - 1)
                        W(pool, e1_ok, K, 2)
                        tt(lastv[kk % 2][:], lastk[m][:, kk // 2, kk % 2 * P:(kk % 2 + 1) * P].rearrange("p (g d) -> p g d", g=2),
                           p1[kk % 2][:, :, KEYS - 1:KEYS].broadcast_to([P, 2, GD]), ALU.mult).then_inc(lv_ok.handle, 1)
                        W(pool, r1_ok, K, 1)
                        tt(select[kk % 2][:], const["head_of_col"][:, kk % 2 * P:(kk % 2 + 1) * P].rearrange("p (g d) -> p g d", g=2),
                           rinv1[kk % 2][:].unsqueeze(2).broadcast_to([P, 2, GD]), ALU.mult).then_inc(sel_ok.handle, 1)
                    sl.steps(table, 2 * k)
                    sl.steps(table, 2 * k + 1)

            slots(pool, slot)

        @block.vector
        def _(dve):
            v_ = nc.vector
            dve.wait_ge(consts_loaded, 16)
            v_.tensor_copy(identb[:], ident[:]).then_inc(su_q, 1)
            dve.wait_ge(fw_in, 32)
            for n in (0, 1):
                v_.tensor_reduce(fw_abs[:, n:n + 1], fw_raw[n], AX, ALU.add, apply_absolute_value=True).then_inc(su_q, 1)
            dve.wait_ge(setup_in, 16 * NS)
            for h in range(H):
                t = v_.tensor_copy(bv_rep[:, h, :], cols["x1_bv"][:, h:h + 1].to_broadcast([P, P]))
            t.then_inc(su_cp, 1)
            for n, name in enumerate(("a1_bq", "a1_bk")):
                v_.tensor_copy(a1_bqk[:, n * H:(n + 1) * H], cols[name][:])
            dve.wait_ge(su_mm, 1)
            v_.tensor_scalar(fw_scale[:], ps[:, 7, 0:2], 1.0 / (D * FF), EPS, ALU.mult, ALU.max).then_inc(su_q, 1)
            dve.wait_ge(su_q, 4)
            v_.reciprocal(fw_inv[:], fw_scale[:]).then_inc(su_q, 1)
            dve.wait_ge(su_q, 5)
            for n in (0, 1):
                v_.tensor_scalar(fw_raw[n], fw_raw[n], fw_inv[:, n:n + 1], MAGIC, ALU.mult, ALU.add).then_inc(su_q, 1)
            dve.wait_ge(su_q, 7)
            for n in (0, 1):
                v_.tensor_scalar(fw_raw[n], fw_raw[n], MAGIC, 1.0, ALU.subtract, ALU.min).then_inc(su_q, 1)
            dve.wait_ge(su_q, 9)
            v_.tensor_scalar(fw[0][:].rearrange("p h f -> p (h f)"), fw_raw[0], -1.0, None, ALU.max).then_inc(su_q, 1)
            v_.tensor_scalar(fw[1][:].rearrange("p k d -> p (k d)"), fw_raw[1], -1.0, None, ALU.max).then_inc(su_q, 1)
            dve.wait_ge(su_mm, 2)
            v_.tensor_copy(x0_A[:], ps[:, 0:2, 0:D]).then_inc(su_cp, 1)
            v_.tensor_copy(x1_B[:], halves(ps[:, 2, :])).then_inc(su_cp, 1)
            v_.tensor_copy(x1_W[:], ps[:, 3:5, 0:D]).then_inc(su_cp, 1)
            v_.tensor_copy(x0_c[:], ps[:, 5, 0:H]).then_inc(su_cp, 1)
            v_.tensor_copy(x1_c[:], ps[:, 5, 8:8 + H]).then_inc(su_cp, 1)
            dve.wait_ge(wload, 16 * NW)
            v_.tensor_tensor(rows["x1_bo"][:], ps[:, 6, 0:D], rows["x1_bo"][:], ALU.add)
            v_.tensor_scalar(full["x0_Wv"][:], full["x0_Wv"][:], float(D) ** -0.5, None, ALU.mult)
            v_.tensor_scalar(rows["x0_bv"][:], rows["x0_bv"][:], float(D) ** -0.5, None, ALU.mult).then_inc(su_cp, 2)
            dve.wait_ge(su_cp, SU_CP)
            dve.wait_ge(su_q, SU_Q)
            for q in (0, 1):
                dve.sem_inc(x_saved[q], 16)
                dve.sem_inc(n_saved[q], 16)

            def moments(part, t, src):
                v_.bn_stats(st6[part][:], src).then_inc(dve_s[part].handle, 1)
                W(dve, dve_s[part], t, "stats")
                v_.memset(hold[part][:], 0.0)
                v_.bn_aggr(mv[part][:], st6[part][:]).then_inc(dve_s[part].handle, 1)
                W(dve, dve_s[part], t, "moments")
                v_.tensor_scalar(ve[part][:], mv[part][:, 1:2], EPS, None, ALU.add).then_inc(dve_s[part].handle, 1)

            def normalise(part, t, src, dst):
                W(dve, pool_s[part], t, "rstd")
                v_.tensor_scalar(dst, src, mv[part][:, 0:1], rstd[part][:], ALU.subtract, ALU.mult).then_inc(dve_s[part].handle, 1)

            def row_max(part, t, src):
                v_.tensor_reduce(nmax[part][:], src, AX, ALU.max, negate=True).then_inc(dve_s[part].handle, 1)

            def masked_max(part, src, scale, mask):
                def step(t, m):
                    if part == "self0":
                        W(dve, pe_s[part], t, "scores")
                    else:
                        W(dve, act_s[part], t, "v")
                    v_.scalar_tensor_tensor(masked[part][:], src, scale, mask[:], ALU.mult, ALU.add).then_inc(dve_s[part].handle, 1)
                    W(dve, dve_s[part], t, "masked")
                    row_max(part, t, masked[part][:])
                return step

            def inverse_sum(part):
                def step(t, m):
                    W(dve, act_s[part], t, "probs")
                    v_.reciprocal(rinv[part][:], rsum[part][:]).then_inc(dve_s[part].handle, 1)
                return step

            def c0_moments(t, m):
                dve.wait_ge(x_in[m], known((t - m) * (32 // RING) + 32))
                moments("cross0", t, xin[m][:])

            def c0_norm(t, m):
                normalise("cross0", t, xin[m][:], xn["cross0"][:])

            def c0_max(t, m):
                W(dve, pe_s["cross0"], t, "scores")
                row_max("cross0", t, bank["cross0"][:, 0:KEYS])

            def c0_att(t, m):
                W(dve, pe_s["cross0"], t, "values")
                v_.scalar_tensor_tensor(att[:], lastq[m][:], prob["cross0"][:, KEYS - 1:KEYS], bank["cross0"][:, 0:D], ALU.mult, ALU.add).then_inc(dve_s["cross0"].handle, 1)

            def c0_x(t, m):
                W(dve, pe_s["cross0"], t, "out")
                W(dve, pool_s["cross0"], t, "x_bias")
                W(dve, dve_s["cross0"], t, "inv")
                v_.scalar_tensor_tensor(x1[m % 2][:], bank["cross0"][:, 0:D], rinv["cross0"][:], xb["cross0"][:], ALU.mult, ALU.add).then_inc(dve_s["cross0"].handle, 1)

            def s0_moments(t, m):
                W(dve, dve_s["cross0"], t, "x")
                moments("self0", t, x1[m % 2][:])

            def s0_norm(t, m):
                normalise("self0", t, x1[m % 2][:], xn["self0"][:])

            def s0_inv(t, m):
                inverse_sum("self0")(t, m)
                W(dve, dve_s["self0"], t, "inv")
                v_.tensor_scalar(prob["self0"][:], prob["self0"][:], rinv["self0"][:], None, ALU.mult).then_inc(dve_s["self0"].handle, 1)

            def s0_x(t, m):
                W(dve, pe_s["self0"], t, "out")
                W(dve, pool_s["self0"], t, "x_bias")
                v_.tensor_tensor(x2[m % 2][:], bank["self0"][:, D:2 * D], xb["self0"][:], ALU.add).then_inc(dve_s["self0"].handle, 1)
                W(dve, dve_s["self0"], t, "x")
                moments("ffn_in", t, x2[m % 2][:])

            def row_scale(part, n, src):
                d, c = dve_s[part], slice(n, n + 1)

                def step(t, m):
                    if n == 0:
                        W(dve, d, t, "norm")
                    else:
                        W(dve, act_s["ffn"], t, "gelu")
                    v_.tensor_reduce(am[:, c], src[:], AX, ALU.max, apply_absolute_value=True).then_inc(d.handle, 1)
                    W(dve, d, t, "absmax")
                    v_.tensor_scalar(am[:, c], am[:, c], EPS, 1.0 / 127.0, ALU.max, ALU.mult).then_inc(d.handle, 1)
                    W(dve, d, t, "clip")
                    v_.reciprocal(qs[:, c], am[:, c]).then_inc(d.handle, 1)
                    v_.tensor_scalar(dq[:, c], am[:, c], fw_scale[:, c], None, ALU.mult).then_inc(d.handle, 1)
                return step

            def quantise(part, n, src, rounded, q):
                d = dve_s[part]

                def step(t, m):
                    W(dve, d, t, "qscale")
                    v_.tensor_scalar(rounded[:], src[:], qs[:, n:n + 1], MAGIC, ALU.mult, ALU.add).then_inc(d.handle, 1)
                    W(dve, d, t, "rounded")
                    v_.tensor_scalar(q[:], rounded[:], MAGIC, 127.0, ALU.subtract, ALU.min).then_inc(d.handle, 1)
                return step

            def ff_norm(t, m):
                normalise("ffn_in", t, x2[m % 2][:], xn["ffn_in"][:])

            def ff_in(t, m):
                row_scale("ffn_in", 0, xn["ffn_in"])(t, m)
                quantise("ffn_in", 0, xn["ffn_in"], xr, xq)(t, m)

            def ff_x(t, m):
                W(dve, pe_s["ffn"], t, "down")
                W(dve, dve_s["ffn"], t, "dequant")
                v_.scalar_tensor_tensor(x3[:], bank["ffn"][:, 0:D], dq[:, 1:2], x2[m % 2][:], ALU.mult, ALU.add).then_inc(dve_s["ffn"].handle, 1)
                W(dve, dve_s["ffn"], t, "x")
                moments("query1", t, x3[:])

            def q1_norm(t, m):
                normalise("query1", t, x3[:], xn["query1"][:])

            def s1_x(t, m):
                W(dve, pe_s["self1"], t, "out")
                W(dve, pool_s["query1"], t, "x_bias")
                v_.tensor_tensor(x4[:], bank["self1"][:, 0:D], xb3[m % 2][:], ALU.add).then_inc(dve_s["self1"].handle, 1)
                W(dve, dve_s["self1"], t, "x")
                moments("self1", t, x4[:])

            def s1_norm(t, m):
                normalise("self1", t, x4[:], xn["self1"][:])

            def s1_qk(t, m):
                W(dve, pe_s["self1"], t, "qk")
                v_.tensor_tensor(qkT[:], bank["self1"].rearrange("p (n t) -> p n t", t=P), a1_bqk[:].unsqueeze(2).broadcast_to([P, 2 * H, P]), ALU.add).then_inc(dve_s["self1"].handle, 1)

            def s1_x5(t, m):
                q = m % 2
                W(dve, pe_s["self1"], t, "values")
                W(dve, dve_s["self1"], t, "inv")
                W(dve, pool_s["self1"], t, "x_bias")
                dve.wait_ge(x_saved[q], known((t - q) * 8 + 16))
                v_.scalar_tensor_tensor(x5[q][:], bank["self1"][:, 0:D], rinv["self1"][:], xb["self1"][:], ALU.mult, ALU.add).then_inc(dve_s["self1"].handle, 1)
                W(dve, dve_s["self1"], t, "x5")
                moments("router", t, x5[q][:])

            def ro_norm(t, m):
                dve.wait_ge(n_saved[m % 2], known((t - m % 2) * 8 + 16))
                normalise("router", t, x5[m % 2][:], xn5[m % 2][:])

            def ro_logits(t, m):
                W(dve, pe_s["router"], t, "logits")
                v_.tensor_copy(logits[:, known(t), :], bank["router"][:, 0:EXP]).then_inc(dve_s["router"].handle, 1)

            table = {
                "cross0": {0: c0_moments, 2: c0_norm, 9: c0_max, 10: inverse_sum("cross0"), 13: c0_att, 15: c0_x},
                "self0": {1: s0_moments, 2: s0_norm, 6: masked_max("self0", bank["self0"][:, 3 * P:4 * P], float(HD) ** -0.5, const["causal"]), 7: s0_inv, 11: s0_x,
                          12: ff_norm, 14: ff_in},
                "ffn": {3: row_scale("ffn", 1, hid), 5: quantise("ffn", 1, hid, hid, hq), 9: ff_x, 10: q1_norm},
                "self1": {3: s1_x, 4: s1_norm, 6: s1_qk, 7: masked_max("self1", bank["self1"][:, D:D + P], float(D) ** -0.5, const["band"]), 8: inverse_sum("self1"),
                          11: s1_x5, 12: ro_norm, 14: ro_logits}}

            def unit_values(t, m, k, K):
                q = k % 2
                W(dve, v1_ps, K, 1)
                W(dve, lv_ok, K, 1)
                own = ps[:, B_V, 0:2 * (P + GD)].rearrange("p (g c) -> p g c", g=2)[:, :, 0:GD]
                v_.tensor_tensor(om[q][:], own, lastv[q][:], ALU.add).then_inc(o1_ok.handle, 1)
                W(dve, o1_ok, K, 1)
                W(dve, sel_ok, K, 1)
                v_.tensor_tensor(om[q][:], om[q][:], select[q][:], ALU.mult).then_inc(om_ok.handle, 1)

            def unit_inverse(t, m, k, K):
                W(dve, e1_ok, K, 2)
                v_.reciprocal(rinv1[k % 2][:], rsum1[k % 2][:]).then_inc(r1_ok.handle, 1)

            def unit_max(t, m, k, K):
                for g in (0, 1):
                    W(dve, s1_ps, K, g + 1)
                    v_.tensor_reduce(nmax1[k % 2][:, g:g + 1], ps[:, g, 0:KEYS], AX, ALU.max, negate=True).then_inc(m1_ok.handle, 1)

            def unit_folded(t, m, k, K):
                b = k // 2
                W(dve, f1_ps, t * NB, b + 1)
                v_.tensor_copy(outT[m % 2][:, :, b * S:(b + 1) * S], ps[:, B_T, 0:H * S].rearrange("p (h q) -> p h q", h=H)).then_inc(f1_ok.handle, 1)

            def slot(sl):
                for k in range(HALVES):
                    last, older = sl.half(k - 1), sl.half(k - 2)
                    if older:
                        unit_values(*older)
                    if k == 1 and last:
                        W(dve, t1_ps, last[3], 1)
                        v_.tensor_copy(p1T[0][:].rearrange("p g k t -> p (g k t)"), ps[:, B_T, :]).then_inc(t1_first.handle, 1)
                    if last:
                        unit_inverse(*last)
                    sl.steps(table, 2 * k)
                    if sl.half(k):
                        unit_max(*sl.half(k))
                    if older and older[2] % 2 == 1:
                        unit_folded(*older)
                    sl.steps(table, 2 * k + 1)

            slots(dve, slot)


def expert_phase(nc, t_in, const, logits, ps, xres, xnorm, yrows, out, tiles, cap, blocks, sem, sig, sb):
    ident = const["ident"]
    T = tiles
    tokens = tiles * P
    GROUP, groups = 4, tiles // 4
    w1 = sb("w1", [P, EXP, H, FF])
    w2 = sb("w2", [P, EXP, FK, D])
    hold = sb("rt_hold", [P, 1])
    prob = sb("rt_prob", [P, T, EXP])
    prob2 = sb("rt_prob2", [P, T, EXP])
    key = sb("rt_key", [P, T, EXP])
    hot = sb("rt_hot", [P, T, TOPK, EXP])
    best = sb("rt_best", [P, TOPK, T])
    tmp = sb("rt_tmp", [P, T])
    tiles_before = sb("rt_tiles_before", [P, T])
    tile_sum = sb("rt_tile_sum", [P, TOPK * EXP])
    spread = sb("rt_spread", [P, T, TOPK * EXP])
    total = sb("rt_total", [P, TOPK, EXP])
    offset = sb("rt_offset", [P, TOPK, EXP])
    pos = sb("rt_pos", [P, T, TOPK, EXP])
    kept = sb("rt_kept", [P, T, TOPK])
    gate = sb("gate", [P, T, TOPK])
    slotf = sb("rt_slotf", [P, T, TOPK])
    place_i = sb("rt_place_i", [P, T, TOPK], I32)
    block_of = sb("rt_block_of", [P, T, TOPK])
    row_of = sb("rt_row_of", [P, T, TOPK])
    tile_no = sb("rt_tile_no", [P, T, TOPK])
    numbers = [sb(f"rt_numbers{b}", [P, GROUP, TOPK, 2, blocks], BF16) for b in (0, 1)]
    spare = sb("rt_spare", [P, blocks])
    number, empty, second = [sb("rt_" + n, [P, blocks]) for n in ("number", "empty", "second")]
    places = sb("places", [P, blocks, 2], U32)
    count = sb("rt_count", [P, EXP])
    first = sb("rt_first", [P, EXP])
    nb_i = sb("rt_blocks_i", [P, EXP], I32)
    nb = sb("rt_blocks", [P, EXP])
    upto = sb("rt_upto", [P, EXP + 1])
    ge = sb("rt_ge", [P, EXP])
    lt = sb("rt_lt", [P, EXP])
    tab = sb("rt_tab", [P, 1])
    tab_i = sb("block_expert", [1, P], I32)
    from_ix = [sb(f"from_ix{b}", [P, 1], U32) for b in (0, 1)]
    to_ix = [sb(f"to_ix{b}", [P, 1], U32) for b in (0, 1)]
    xe = [sb(f"xe{b}", [P, D]) for b in (0, 1)]
    xeT = [sb(f"xeT{b}", [P, H, P]) for b in (0, 1)]
    he = [sb(f"he{b}", [P, FF]) for b in (0, 1)]
    heT = [sb(f"heT{b}", [P, FK, P]) for b in (0, 1)]
    ye = [sb(f"ye{b}", [P, D]) for b in (0, 1)]
    xo = sb("residual", [P, T, D])
    is_row = [x[:].bitcast(BF16)[:, 0:GROUP * TOPK * P].rearrange("p (n k c) -> p n k c", n=GROUP, k=TOPK) for x in he]
    is_block = [x[:].rearrange("p k t -> p (k t)")[:, 0:GROUP * TOPK * blocks].rearrange("p (n k c) -> p n k c", n=GROUP, k=TOPK) for x in heT]
    yg = w1[:].rearrange("p e h f -> p (e h f)")[:, 0:TOPK * T * D].rearrange("p (k t d) -> p k t d", k=TOPK, t=T)

    w_in = [sem(f"expert_weights_in{e}") for e in range(EXP)]
    experts_in = sem("experts_loaded")
    rt = sem("routing_step")
    rt_exp = sem("routing_exp")
    rt_pe = sem("routing_sums_in_psum")
    tab_ok = sem("block_table_ready")
    rc_in = sem("routing_constants_in")
    eq_ok, row_ok, hot_ok, ix_pe = sig("place_blocks_compared", 1), sig("place_rows", 1), sig("place_one_hots", 1), sig("place_one_hots_used", 1)
    from_ok = sig("gather_rows_staged", 1)
    carried = sem("waits_carried")
    xe_in = [sem(f"block_in{b}") for b in (0, 1)]
    ye_out = [sem(f"block_out{b}") for b in (0, 1)]
    xeT_ps, xeT_ok, up_ps, he_ok = sig("block_xT_in_psum", 1), sig("block_xT_ready", 1), sig("block_up_in_psum", 2), sig("block_hidden", 2)
    heT_ps, heT_lo, heT_hi, y_ps, ye_ok = sig("block_hiddenT_in_psum", 2), sig("block_hiddenT_lo", 1), sig("block_hiddenT_hi", 1), sig("block_y_in_psum", 1), sig("block_y", 1)
    xo_in = sem("residual_in")
    yg_in = [sem(f"expert_rows_in{b}") for b in (0, 1)]
    g_ok, xo_ok = sig("gated_first", GROUP), sig("output_ready", GROUP)
    out_saved = sem("output_saved")

    def W(eng, s, r, k):
        eng.wait_ge(s.handle, s.at(r, k))

    def skewed(eng, block_work):
        for u in range(4):
            block_work(u, u % 2, first=u == 0)
        with eng.Fori(2, (blocks - 4) // 2) as i:
            for b in (0, 1):
                block_work(i * 2 + b, b)
        for u in range((blocks - 4) // 2 * 2, blocks):
            block_work(u, u % 2, last=u == blocks - 1)

    R_LOGIT, R_HOT, R_SPREAD, R_TAB = {}, {}, {}, {}

    def routing(dve):
        v_ = nc.vector
        n = [0]

        def step(ins):
            n[0] += 1
            ins.then_inc(rt, 1)
            dve.wait_ge(rt, n[0])
            return n[0]

        def bc(ap, axis, size):
            shape = list(ap.shape)
            shape.insert(axis, size)
            return ap.unsqueeze(axis).broadcast_to(shape)

        step(v_.tensor_reduce(tmp[:], logits[:], AX, ALU.max))
        R_LOGIT[0] = step(v_.tensor_tensor(prob[:], logits[:], bc(tmp[:], 2, EXP), ALU.subtract))
        dve.wait_ge(rt_exp, 1)
        step(v_.tensor_reduce(tmp[:], prob[:], AX, ALU.add))
        step(v_.reciprocal(tmp[:], tmp[:]))
        step(v_.tensor_tensor(prob[:], prob[:], bc(tmp[:], 2, EXP), ALU.mult))
        src = prob
        for k in range(TOPK):
            step(v_.tensor_reduce(best[:, k, :], src[:], AX, ALU.max))
            step(v_.tensor_tensor(key[:], src[:], bc(best[:, k, :], 2, EXP), ALU.is_equal))
            step(v_.tensor_tensor(key[:], key[:], bc(const["rev8"][:], 1, T), ALU.mult))
            step(v_.tensor_reduce(tmp[:], key[:], AX, ALU.max))
            R_HOT[0] = step(v_.tensor_tensor(hot[:, :, k, :], key[:], bc(tmp[:], 2, EXP), ALU.is_equal))
            if k == 0:
                step(v_.scalar_tensor_tensor(prob2[:], hot[:, :, 0, :], -2.0, prob[:], ALU.mult, ALU.add))
                src = prob2
        step(v_.tensor_tensor(tmp[:], best[:, 0, :], best[:, 1, :], ALU.add))
        step(v_.reciprocal(tmp[:], tmp[:]))
        for k in range(TOPK):
            step(v_.tensor_tensor(gate[:, :, k], best[:, k, :], tmp[:], ALU.mult))

        TE = TOPK * EXP
        dve.wait_ge(rc_in, 48)
        dve.wait_ge(rt_pe, 1)
        step(v_.tensor_copy(tile_sum[0:T, :], ps[0:T, 2, 0:TE]))
        R_SPREAD[0] = step(v_.tensor_tensor(spread[0:T], bc(tile_sum[0:T, :], 1, T), bc(tiles_before[0:T, :], 2, TE), ALU.mult))
        dve.wait_ge(rt_pe, 2)
        where = ps[:, 0, 0:T * TE].rearrange("p (t e) -> p t e", e=TE)
        hot_f = hot[:].rearrange("p t k e -> p t (k e)")
        step(v_.scalar_tensor_tensor(hot_f, where, float(cap), hot_f, ALU.is_lt, ALU.mult))
        step(v_.tensor_reduce(kept[:], hot[:], AX, ALU.add))
        step(v_.tensor_tensor(gate[:], gate[:], kept[:], ALU.mult))
        step(v_.tensor_scalar(total[:].rearrange("p k e -> p (k e)"), ps[:, 3, 0:TE], float(cap), None, ALU.min))
        step(v_.tensor_tensor(count[:], total[:, 0, :], total[:, 1, :], ALU.add))
        step(v_.tensor_scalar(count[:], count[:], float(P - 1), None, ALU.add))
        step(v_.tensor_copy(nb_i[:], count[:]))
        step(v_.tensor_scalar(nb_i[:], nb_i[:], P.bit_length() - 1, None, ALU.arith_shift_right))
        step(v_.tensor_copy(nb[:], nb_i[:]))
        step(v_.memset(upto[:], 0.0))
        for e in range(EXP):
            step(v_.tensor_tensor(upto[:, e + 1:e + 2], upto[:, e:e + 1], nb[:, e:e + 1], ALU.add))
        step(v_.tensor_scalar(first[:], upto[:, 0:EXP], float(P), None, ALU.mult))
        step(v_.tensor_copy(offset[:, 0, :], first[:]))
        step(v_.tensor_tensor(offset[:, 1, :], first[:], total[:, 0, :], ALU.add))
        pos_f = pos[:].rearrange("p t k e -> p t (k e)")
        step(v_.tensor_tensor(pos_f, where, bc(offset[:].rearrange("p k e -> p (k e)"), 1, T), ALU.add))
        step(v_.tensor_tensor(pos_f, pos_f, hot_f, ALU.mult))
        step(v_.tensor_reduce(slotf[:], pos[:], AX, ALU.add))
        step(v_.tensor_scalar(kept[:], kept[:], -float(blocks * P), float(blocks * P), ALU.mult, ALU.add))
        step(v_.tensor_tensor(slotf[:], slotf[:], kept[:], ALU.add))
        step(v_.tensor_copy(place_i[:], slotf[:]))
        step(v_.tensor_scalar(place_i[:], place_i[:], P.bit_length() - 1, None, ALU.arith_shift_right))
        step(v_.tensor_copy(block_of[:], place_i[:]))
        step(v_.scalar_tensor_tensor(row_of[:], block_of[:], -float(P), slotf[:], ALU.mult, ALU.add))
        step(v_.tensor_scalar(ge[:], upto[:, 0:EXP], const["row"][:], None, ALU.is_le))
        step(v_.tensor_scalar(lt[:], upto[:, 1:EXP + 1], const["row"][:], None, ALU.is_gt))
        step(v_.tensor_tensor(ge[:], ge[:], lt[:], ALU.mult))
        step(v_.tensor_tensor(lt[:], ge[:], const["eids"][:], ALU.mult))
        R_TAB[0] = step(v_.tensor_reduce(tab[:], lt[:], AX, ALU.add))
        dve.wait_ge(rt_pe, 3)
        v_.tensor_copy(tab_i[:], ps[0:1, 4, 0:P]).then_inc(tab_ok, 1)

        def one_hots(i, b, first=False):
            if not first:
                W(dve, ix_pe, i - 2, 1)
            own = bass.ds(i * GROUP, GROUP)

            def spread_of(x, width):
                return x[:, own, :].unsqueeze(3).broadcast_to([P, GROUP, TOPK, width])

            every = const["cols"][:].unsqueeze(1).unsqueeze(1).broadcast_to([P, GROUP, TOPK, P])
            v_.tensor_tensor(is_block[b], every[:, :, :, 0:blocks], spread_of(block_of, blocks), ALU.is_equal).then_inc(eq_ok.handle, 1)
            v_.tensor_tensor(is_row[b], every, spread_of(row_of, P), ALU.is_equal)
            W(dve, eq_ok, i, 1)
            v_.tensor_tensor(numbers[b][:, :, :, 0, :], is_block[b], spread_of(tile_no, blocks), ALU.mult).then_inc(hot_ok.handle, 1)

        for i in (0, 1):
            one_hots(i, i, first=True)
        if groups > 2:
            with dve.Fori(1, groups // 2) as i:
                for b in (0, 1):
                    one_hots(i * 2 + b, b)
        W(dve, ix_pe, groups - 1, 1)
        step(v_.tensor_copy(second[:], ps[:, 5, 0:blocks]))
        step(v_.scalar_tensor_tensor(number[:], second[:], float(P), ps[:, 5, blocks:2 * blocks], ALU.mult, ALU.add))
        step(v_.tensor_scalar(empty[:], number[:], 0.0, None, ALU.is_equal))
        step(v_.tensor_scalar(second[:], number[:], float(tokens), None, ALU.is_gt))
        step(v_.tensor_tensor(empty[:], empty[:], spare[:], ALU.mult))
        step(v_.tensor_tensor(empty[:], empty[:], number[:], ALU.add))
        step(v_.tensor_scalar(places[:, :, 1], empty[:], -1.0, None, ALU.add))
        step(v_.scalar_tensor_tensor(second[:], second[:], -float(tokens), number[:], ALU.mult, ALU.add))
        step(v_.tensor_scalar(places[:, :, 0], second[:], -1.0, 0.0, ALU.add, ALU.max))

    with nc.Block() as block:
        @block.vector
        def _(dve):
            v_ = nc.vector
            routing(dve)

            def stage_from(u, b):
                v_.tensor_copy(from_ix[b][:], places[:, u, 0:1]).then_inc(from_ok.handle, 1)

            def block_copies(u, b, first=False, last=False):
                if not last:
                    W(dve, xeT_ps, u + 1, 1)
                    v_.tensor_copy(xeT[1 - b][:].rearrange("p h t -> p (h t)"), ps[:, 5 - b, 0:D]).then_inc(xeT_ok.handle, 1)
                    if not (isinstance(u, int) and u + 3 >= blocks):
                        stage_from(u + 3, 1 - b)
                if not first:
                    down_copy(u - 1, 1 - b)
                W(dve, heT_ps, u, 2)
                v_.tensor_copy(heT[b][:, FK // 2:FK, :].rearrange("p k t -> p (k t)"), ps[:, 2 * b + 1, :]).then_inc(heT_hi.handle, 1)

            def down_copy(u, b):
                W(dve, y_ps, u, 1)
                if not (isinstance(u, int) and u < 2):
                    dve.wait_ge(ye_out[b], (u - b) * 8)
                v_.tensor_copy(to_ix[b][:], places[:, u, 1:2])
                v_.tensor_copy(ye[b][:], ps[:, 6 + b, 0:D]).then_inc(ye_ok.handle, 1)

            for u in (0, 1):
                stage_from(u, u)
            W(dve, xeT_ps, 0, 1)
            v_.tensor_copy(xeT[0][:].rearrange("p h t -> p (h t)"), ps[:, 4, 0:D]).then_inc(xeT_ok.handle, 1)
            stage_from(2, 0)
            skewed(dve, block_copies)
            down_copy(blocks - 1, (blocks - 1) % 2)

            def gated_sum(i, b):
                dve.wait_ge(yg_in[b], (i - b) * 16 + 32)
                for n in range(GROUP):
                    t = i * GROUP + n
                    v_.scalar_tensor_tensor(xo[:, t, :], yg[:, 0, t, :], gate[:, t, 0:1], xo[:, t, :], ALU.mult, ALU.add).then_inc(g_ok.handle, 1)
                for n in range(GROUP):
                    t = i * GROUP + n
                    W(dve, g_ok, i, n + 1)
                    v_.scalar_tensor_tensor(xo[:, t, :], yg[:, 1, t, :], gate[:, t, 1:2], xo[:, t, :], ALU.mult, ALU.add).then_inc(xo_ok.handle, 1)

            dve.wait_ge(xo_in, 16 * groups)
            with dve.Fori(0, groups // 2) as i:
                for b in (0, 1):
                    gated_sum(i * 2 + b, b)

        @block.tensor
        def _(pe):
            mm = nc.tensor.matmul
            TE = TOPK * EXP
            pe.wait_ge(rt, R_HOT[0])
            hot_f = hot[:].rearrange("p t k e -> p t (k e)")
            for c in range(TE):
                t = mm(ps[0:T, 2, c:c + 1], hot_f[:, :, c], const["ones"][:, 0:1], start=True, stop=True)
            t.then_inc(rt_pe, 1)
            mm(ps[:, 0, 0:T * TE], const["before"][:], hot[:].rearrange("p t k e -> p (t k e)"), start=True, stop=False)
            pe.wait_ge(rt, R_SPREAD[0])
            mm(ps[:, 3, 0:TE], const["ones"][0:T, :], tile_sum[0:T, :], start=True, stop=True)
            mm(ps[:, 0, 0:T * TE], const["ones"][0:T, :], spread[0:T].rearrange("p t e -> p (t e)"), start=False, stop=True).then_inc(rt_pe, 1)
            pe.wait_ge(rt, R_TAB[0])
            mm(ps[0:1, 4, 0:P], tab[:], ident[:], start=True, stop=True).then_inc(rt_pe, 1)

            def places_of(i, b, first=False, last=False):
                W(pe, hot_ok, i, 1)
                W(pe, row_ok, i, 1)
                for n in range(GROUP):
                    for k in range(TOPK):
                        t = mm(ps[:, 5, 0:2 * blocks], is_row[b][:, n, k, :], numbers[b][:, n, k, :, :].rearrange("p j c -> p (j c)"), start=first and n == k == 0, stop=last and n * TOPK + k == GROUP * TOPK - 1)
                t.then_inc(ix_pe.handle, 1)

            for i in (0, 1):
                places_of(i, i, first=i == 0, last=i == groups - 1)
            if groups > 4:
                with pe.Fori(1, groups // 2 - 1) as i:
                    for b in (0, 1):
                        places_of(i * 2 + b, b)
            if groups > 2:
                for i in (groups - 2, groups - 1):
                    places_of(i, i % 2, last=i == groups - 1)
            pe.wait_ge(tab_ok, 1)

            def rows_T(u, b):
                pe.wait_ge(xe_in[b], (u - b) * 8 + 16)
                for h in range(H):
                    t = nc.tensor.transpose(ps[:, 4 + b, h * P:(h + 1) * P], xe[b][:, h * P:(h + 1) * P], ident[:])
                t.then_inc(xeT_ps.handle, 1)

            def down(u, b, e):
                W(pe, heT_lo, u, 1)
                W(pe, heT_hi, u, 1)
                for k in range(FK):
                    t = mm(ps[:, 6 + b, 0:D], heT[b][:, k, :], w2[:, e, k, :], start=k == 0, stop=k == FK - 1)
                t.then_inc(y_ps.handle, 1)

            def expert(u):
                return pe.value_load(tab_i[0:1, bass.ds(u, 1)], min_val=0, max_val=EXP - 1)

            def block_products(u, b, first=False, last=False):
                e = expert(u)
                W(pe, xeT_ok, u, 1)
                pe.wait_ge(experts_in, e + 1)
                for n in range(2):
                    for k in range(H):
                        t = mm(ps[:, 2 * b + n, :], xeT[b][:, k, :], w1[:, e, k, n * 512:(n + 1) * 512], start=k == 0, stop=k == H - 1)
                    t.then_inc(up_ps.handle, 1)
                if not last:
                    rows_T(u + 1, 1 - b)
                if not first:
                    down(u - 1, 1 - b, expert(u - 1))
                for n in range(2):
                    W(pe, he_ok, u, n + 1)
                    for k in range(FK // 2):
                        f = n * FK // 2 + k
                        t = nc.tensor.transpose(ps[:, 2 * b + n, k * P:(k + 1) * P], he[b][:, f * P:(f + 1) * P], ident[:])
                    t.then_inc(heT_ps.handle, 1)

            rows_T(0, 0)
            skewed(pe, block_products)
            down(blocks - 1, (blocks - 1) % 2, expert(blocks - 1))

        @block.scalar
        def _(act):
            A = nc.scalar.activation
            act.wait_ge(rt, R_LOGIT[0])
            A(prob[:], prob[:], ACT.Exp).then_inc(rt_exp, 1)

            def row_numbers(i, b):
                W(act, eq_ok, i, 1)
                if not (isinstance(i, int) and i < 2):
                    W(act, ix_pe, i - 2, 1)
                A(numbers[b][:, :, :, 1, :], is_block[b], ACT.Copy, scale=const["row_1"]).then_inc(row_ok.handle, 1)

            for i in (0, 1):
                row_numbers(i, i)
            if groups > 2:
                with act.Fori(1, groups // 2) as i:
                    for b in (0, 1):
                        row_numbers(i * 2 + b, b)

            def block_gelu(u, b, first=False, last=False):
                for n in range(2):
                    W(act, up_ps, u, n + 1)
                    A(he[b][:, n * 512:(n + 1) * 512], ps[:, 2 * b + n, :], ACT.Gelu).then_inc(he_ok.handle, 1)
                W(act, heT_ps, u, 1)
                A(heT[b][:, 0:FK // 2, :].rearrange("p k t -> p (k t)"), ps[:, 2 * b, :], ACT.Copy).then_inc(heT_lo.handle, 1)

            skewed(act, block_gelu)

        @block.gpsimd
        def _(pool):
            g = nc.gpsimd
            pool.sem_inc(carried, 1)
            tokens_in = xnorm.rearrange("t p d -> (t p) d")

            def carrier(n):
                pool.wait_ge(carried, n + 1)
                g.tensor_tensor(hold[:], const["row"][:], const["row"][:], ALU.add).then_inc(carried, 1)

            def gather(u, b):
                g.indirect_dma_start(xe[b][:], None, tokens_in, bass.IndirectOffsetOnAxis(ap=from_ix[b][:], axis=0)).then_inc(xe_in[b], 16)

            def scatter(u, b):
                g.indirect_dma_start(yrows, bass.IndirectOffsetOnAxis(ap=to_ix[b][:], axis=0), ye[b][:], None).then_inc(ye_out[b], 16)

            for u in (0, 1):
                W(pool, from_ok, u, 1)
                carrier(u)
                gather(u, u)

            def block_transfers(u, b, first=False, last=False):
                if not (isinstance(u, int) and u + 3 >= blocks):
                    W(pool, from_ok, u + 3, 1)
                    carrier(3 if first else 2 * u + 2)
                    gather(u + 3, 1 - b)
                if not first:
                    W(pool, ye_ok, u - 1, 1)
                    carrier(blocks - 1 + u if isinstance(u, int) and u + 3 >= blocks else 2 * u + 3)
                    scatter(u - 1, 1 - b)

            W(pool, from_ok, 2, 1)
            carrier(2)
            gather(2, 0)
            skewed(pool, block_transfers)
            W(pool, ye_ok, blocks - 1, 1)
            carrier(2 * blocks - 1)
            scatter(blocks - 1, (blocks - 1) % 2)

        @block.sync
        def _(sp):
            sp.dma_start(tile_no[:], t_in["c_tile_no"]).then_inc(rc_in, 16)
            sp.dma_start(spare[:], t_in["c_spare"]).then_inc(rc_in, 16)
            sp.dma_start(tiles_before[:], t_in["c_tiles_before"]).then_inc(rc_in, 16)
            for e in range(EXP):
                sp.dma_start(w1[:, e], t_in["m_w1"][e]).then_inc(w_in[e], 16)
                sp.dma_start(w2[:, e], t_in["m_w2"][e]).then_inc(w_in[e], 16)
            by_choice = yrows[0:TOPK * tokens, :].rearrange("(k g n p) d -> k g p n d", k=TOPK, p=P, n=GROUP)
            xres_g = xres.rearrange("(g n) p d -> g p n d", n=GROUP)
            out_g = out.rearrange("(g n) p d -> g p n d", n=GROUP)

            def load_rows(i, b):
                for k in range(TOPK):
                    sp.dma_start(yg[:, k, bass.ds(i * GROUP, GROUP), :], by_choice[k, i]).then_inc(yg_in[b], 16)

            def store_out(i):
                W(sp, xo_ok, i, GROUP)
                sp.dma_start(out_g[i], xo[:, bass.ds(i * GROUP, GROUP), :]).then_inc(out_saved, 16)

            for e in range(EXP):
                sp.wait_ge(w_in[e], 32)
                sp.sem_inc(experts_in, 1)
            for i in range(groups):
                sp.dma_start(xo[:, i * GROUP:(i + 1) * GROUP, :], xres_g[i]).then_inc(xo_in, 16)
                sp.wait_ge(xo_in, 16 * (i + 1))
            for b in (0, 1):
                sp.wait_ge(ye_out[b], (blocks + 1 - b) // 2 * 16)
            for b in (0, 1):
                load_rows(b, b)

            if groups > 2:
                with sp.Fori(0, groups // 2 - 1) as i:
                    for b in (0, 1):
                        sp.wait_ge(yg_in[b], i * 32 + 32)
                        load_rows(i * 2 + b + 2, b)
                        store_out(i * 2 + b)
            for i in (groups - 2, groups - 1):
                store_out(i)
            sp.wait_ge(out_saved, 16 * groups)


def shape_constants(np, tiles, blocks):
    f = np.float32
    p = np.arange(P)
    same = p[:, None] // S == p[None, :] // S
    c = {}
    c["ident"] = np.eye(P, dtype=f)
    c["causal"] = np.where(same & (p[None, :] <= p[:, None]), 0.0, MASKED).astype(f)
    c["band"] = np.where(same & (abs(p[None, :] - p[:, None]) <= 2), 0.0, MASKED).astype(f)
    col = np.arange(D)
    c["head_of_col"] = (p[:, None] // S == (col[None, :] % GD) // DH).astype(f)
    c["head_of_dim"] = (((p % GD) // DH)[:, None] == np.arange(HG)[None, :]).astype(f) * f(DH ** -0.5)
    c["fold"] = (p[:, None] % S == np.arange(S)[None, :]).astype(f)
    c["before"] = (p[:, None] < p[None, :]).astype(f)
    c["ones"] = np.ones((P, P), f)
    c["rev8"] = np.broadcast_to((EXP - np.arange(EXP)).astype(f), (P, EXP))
    c["cols"] = np.broadcast_to(np.arange(P).astype(f), (P, P))
    c["row"] = p[:, None].astype(f)
    c["row_1"] = 1 + c["row"]
    c["eids"] = np.broadcast_to(np.arange(EXP).astype(f), (P, EXP))
    c = {"constants": np.concatenate([np.broadcast_to(c[n], (P, w)) for n, w in WIDTH.items()], axis=1)}
    tokens = tiles * P
    c["tile_no"] = np.broadcast_to(np.arange(TOPK)[None, None, :] * tiles + np.arange(tiles)[None, :, None], (P, tiles, TOPK)).astype(f)
    c["spare"] = (TOPK * tokens + 1 + np.arange(blocks)[None, :] * P + p[:, None]).astype(f)
    c["tiles_before"] = (p[:, None] < np.arange(tiles)[None, :]).astype(f)
    return {"c_" + n: np.ascontiguousarray(a) for n, a in c.items()}


def lay_out(np, v):
    a = {n: np.asarray(x) for n, x in v.items()}
    B = a["x"].shape[0]
    tiles = B // NB
    tokens = B * S
    d = shape_constants(np, tiles, most_blocks(tokens))
    d["x"] = a["x"].reshape(tiles, P, D)
    ctx = a["ctx_1024"].reshape(tiles, NB, KEYS, D)
    d["cn"] = ctx[:, :, :KEYS - 1].reshape(tiles, NB, KT, P, D).transpose(0, 3, 1, 2, 4)
    d["cT"] = ctx.reshape(tiles, NB, KEYS, H, P).transpose(0, 4, 1, 3, 2)
    d["lastk"] = ctx[:, :, KEYS - 1]
    d["lastq"] = np.repeat(d["lastk"], S, axis=1)
    d["x0_Wq_T"], d["x0_Wk_T"], d["x0_Wv"] = a["L0_xattn_Wq"].T, a["L0_xattn_Wk"].T, a["L0_xattn_Wv"]
    d["x1_woT"] = a["L1_xattn_wo"].T
    for n in ("Wq", "Wk", "Wv"):
        d["a1_" + n] = a["L1_attn_" + n]
        d[f"a0_{n}_T"] = a["L0_attn_" + n].T
    d["x0_bv"], d["a0_bo"], d["x1_bo"], d["a1_bv"] = a["L0_xattn_bv"], a["L0_attn_bo"], a["L1_xattn_bo"], a["L1_attn_bv"]

    def column(x):
        return x.reshape(H, P).T

    d["x0_bq"], d["a1_bq"], d["a1_bk"] = column(a["L0_xattn_bq"]), column(a["L1_attn_bq"]), column(a["L1_attn_bk"])
    d["x1_bq"], d["x1_bv"] = column(a["L1_xattn_bq"].reshape(-1)), column(a["L1_xattn_bv"].reshape(-1))
    d["a0_woT"] = a["L0_attn_Wo"].T
    for n in ("bq", "bk", "bv"):
        d["a0_" + n] = a["L0_attn_" + n].reshape(P, 1)
    for n in ("wq", "wk", "wv"):
        w = np.zeros((P, H, P), np.float32)
        for h in range(HEADS):
            lo = h * DH % P
            w[lo:lo + DH, h * DH // P, lo:lo + DH] = a["L1_xattn_" + n][h]
        d["x1_" + n] = w
    d["router"] = a["L1_ffn_router_w"].T
    d["f1"], d["f2"] = a["L0_ffn_w1"].T, a["L0_ffn_w2"].T
    d["m_w1"] = a["L1_ffn_w1"].reshape(EXP, H, P, FF).transpose(0, 2, 1, 3)
    d["m_w2"] = a["L1_ffn_w2"].reshape(EXP, FK, P, D).transpose(0, 2, 1, 3)
    return {n: np.ascontiguousarray(x) for n, x in d.items()}


def kernel(**inputs):
    import numpy as _np
    import concourse.bacc as _bacc
    from concourse import mybir as _mybir
    from concourse.bass_utils import run_bass_kernel_spmd as _run

    arrays = lay_out(_np, inputs)
    nc = _bacc.Bacc("TRN2", target_bir_lowering=False, num_devices=1)
    handles = {n: nc.dram_tensor("in_" + n, a.shape, _mybir.dt.from_np(a.dtype), kind="ExternalInput").ap() for n, a in arrays.items()}
    shape = arrays["x"].shape
    out = nc.dram_tensor("out_0", shape, F32, kind="ExternalOutput").ap()
    build(nc, handles, out)
    r = _run(nc, [{"in_" + n: a for n, a in arrays.items()}], core_ids=[0])
    return r.results[0]["out_0"].reshape(inputs["x"].shape)
```
